# Optimizing a Trainium2 kernel written in Bass

```python
import numpy as np
import jax
import jax.numpy as jnp

def _softmax(x, axis=-1):
    return jax.nn.softmax(x, axis=axis)

def _gelu(x):
    return jax.nn.gelu(x, approximate=True)

def _silu(x):
    return jax.nn.silu(x)

def _sigmoid(x):
    return jax.nn.sigmoid(x)

def _layernorm(x, axis=-1, eps=1e-05):
    m = jnp.mean(x, axis=axis, keepdims=True)
    v = jnp.var(x, axis=axis, keepdims=True)
    return (x - m) / jnp.sqrt(v + eps)

def _scatter_add(tgt, idx, src, axis=0):
    return tgt.at[idx].add(src)

def _segment_sum(src, seg, n):
    return jax.ops.segment_sum(src, seg, n)
kernel_name = 'mk_decoder_preln_d2_seqx_r4_ca5b38'

def setup_inputs(seed: int=0):
    np.random.seed(seed)
    _w = jnp.asarray

    def _rec_inputs():
        import jax
        import jax.numpy as jnp
        _rk = jax.random.key(seed)
        x = 7.22e-05 + 1 * jax.random.normal(jax.random.fold_in(_rk, 1), (8, 112, 512), jnp.float32)
        _lenS = 112 - jax.random.randint(jax.random.fold_in(_rk, 7), (8,), 0, max(1, 112 // 4) + 1, jnp.int32)
        _lenS2 = 375 - jax.random.randint(jax.random.fold_in(_rk, 8), (8,), 0, max(1, 375 // 4) + 1, jnp.int32)
        _ctx_2048P = jax.random.normal(jax.random.fold_in(_rk, 12), (8, 16, 512), jnp.float32)
        _ctx_2048c = jax.random.dirichlet(jax.random.fold_in(_rk, 512), 0.3 * jnp.ones((16,), jnp.float32), (8, 375))
        _ctx_2048t = jnp.einsum('bsk,bkd->bsd', _ctx_2048c, _ctx_2048P)
        _ctx_2048t = _ctx_2048t * jax.lax.rsqrt(jnp.mean(jnp.square(_ctx_2048t)) + 1e-12) * 0.953939
        ctx_2048 = 0.00424091 + 1.0017 * (_ctx_2048t + 0.3 * jax.random.normal(jax.random.fold_in(_rk, 612), (8, 375, 512), jnp.float32))
        _validS = jnp.arange(112)[None, :] < _lenS[:, None]
        _validS2 = jnp.arange(375)[None, :] < _lenS2[:, None]
        _causal = jnp.tril(jnp.ones((112, 112), dtype=bool))
        mask_Bx1xSxS_fk0 = jnp.where(jnp.broadcast_to(_validS[:, None, None, :], (8, 1, 112, 112)), -1000000000.0, 0.0).astype(jnp.float32)
        mask_BxS2_bk0 = jnp.logical_not(jnp.broadcast_to(_validS2[:, :], (8, 375)))
        return (x, ctx_2048, mask_Bx1xSxS_fk0, mask_BxS2_bk0)
    x, ctx_2048, mask_Bx1xSxS_fk0, mask_BxS2_bk0 = _rec_inputs()

    def _L0_attn_setup():
        import jax, jax.numpy as jnp
        import numpy as np
        B, S, M = (1, 512, 512)
        H, HKV, D = (32, 8, 64)
        SW = 128
        WAVELENGTH = 150000.0
        SCALE = D ** (-0.25)
        NEG = -1000000000.0

        def _cos_sin(seq_len, dtype):
            half = D // 2
            inv_freq = 1.0 / WAVELENGTH ** (jnp.arange(half, dtype=jnp.float32) * 2.0 / D)
            t = jnp.arange(seq_len, dtype=jnp.float32)
            freqs = t[:, None] * inv_freq[None, :]
            return (jnp.cos(freqs)[None, :, None, :].astype(dtype), jnp.sin(freqs)[None, :, None, :].astype(dtype))

        def _interleaved_rope(x, cos, sin):
            x_even = x[..., ::2]
            x_odd = x[..., 1::2]
            first = x_even * cos - x_odd * sin
            second = x_odd * cos + x_even * sin
            return jnp.stack([first, second], axis=-1).reshape(x.shape)
        key = jax.random.key(seed)
        ks = jax.random.split(key, 8)
        return {'hidden_states': jax.random.normal(ks[0], (B, S, M), jnp.float32), 'Wq': jax.random.normal(ks[1], (M, H, D), jnp.float32) * 0.02, 'bq': jnp.zeros((H, D), jnp.float32), 'Wk': jax.random.normal(ks[2], (M, HKV, D), jnp.float32) * 0.02, 'bk': jnp.zeros((HKV, D), jnp.float32), 'Wv': jax.random.normal(ks[3], (M, HKV, D), jnp.float32) * 0.02, 'bv': jnp.zeros((HKV, D), jnp.float32), 'Wo': jax.random.normal(ks[4], (H, D, M), jnp.float32) * 0.02, 'bo': jnp.zeros((M,), jnp.float32), 'sinks': jax.random.normal(ks[5], (H,), jnp.float32)}
    _L0_attn_all = _L0_attn_setup()
    _L0_attn_in = {k: v for k, v in _L0_attn_all.items() if k in ('Wq', 'bq', 'Wk', 'bk', 'Wv', 'bv', 'Wo', 'bo', 'sinks')}
    del _L0_attn_all

    def _L0_xattn_setup():
        import jax, jax.numpy as jnp
        import numpy as np
        import math
        B, S, HID, H = (2, 512, 512, 32)
        D = HID // H
        AL = 10

        def _rope_tables(seq_len, dim, dtype):
            inv_freq = 1.0 / 10000.0 ** (np.arange(0, dim, 2, dtype=np.float32) / dim)
            t = np.arange(seq_len, dtype=np.float32)
            freqs = np.outer(t, inv_freq)
            emb = np.concatenate([freqs, freqs], -1)
            return (jnp.asarray(np.cos(emb), dtype), jnp.asarray(np.sin(emb), dtype))

        def _rotate_half(x):
            x1, x2 = jnp.split(x, 2, axis=-1)
            return jnp.concatenate([-x2, x1], axis=-1)
        key = jax.random.key(seed)
        ks = jax.random.split(key, 8)
        hidden_states = jax.random.normal(ks[0], (B, S, HID), dtype=jnp.float32)
        adapter = jax.random.normal(ks[1], (B, AL, HID), dtype=jnp.float32)
        causal = jnp.tril(jnp.ones((S, S), dtype=bool))
        attention_mask = jnp.broadcast_to(jnp.where(causal, 0.0, -1000000000.0).astype(jnp.float32)[None, None], (B, 1, S, S))
        scale = 0.02
        Wq = jax.random.normal(ks[2], (HID, HID), dtype=jnp.float32) * scale
        Wk = jax.random.normal(ks[3], (HID, HID), dtype=jnp.float32) * scale
        Wv = jax.random.normal(ks[4], (HID, HID), dtype=jnp.float32) * scale
        Wo = jax.random.normal(ks[5], (HID, HID), dtype=jnp.float32) * scale
        gate = jax.random.normal(ks[6], (1, H, 1, 1), dtype=jnp.float32) * 0.1
        return {'hidden_states': hidden_states, 'attention_mask': attention_mask, 'adapter': adapter, 'Wq': Wq, 'Wk': Wk, 'Wv': Wv, 'Wo': Wo, 'gate': gate}
    _L0_xattn_all = _L0_xattn_setup()
    _L0_xattn_in = {k: v for k, v in _L0_xattn_all.items() if k in ('Wq', 'Wk', 'Wv', 'Wo', 'gate')}
    del _L0_xattn_all

    def _L0_ffn_setup():
        import jax, jax.numpy as jnp
        import numpy as np
        TOP_K = 2
        key = jax.random.key(seed)
        ks = jax.random.split(key, 4)
        G, S, F, E, H = (4, 512, 512, 8, 512)
        return {'x': jax.random.normal(ks[0], (G, S, F), dtype=jnp.float32), 'router_logits': jax.random.normal(ks[1], (F, E), dtype=jnp.float32) * 0.02, 'gating_einsum': jax.random.normal(ks[2], (E, 2, H, F), dtype=jnp.float32) * 0.02, 'linear': jax.random.normal(ks[3], (E, H, F), dtype=jnp.float32) * 0.02, 'per_expert_scale': jnp.ones((E,), dtype=jnp.float32), 'router_scale': jnp.ones((F,), dtype=jnp.float32)}
    _L0_ffn_all = _L0_ffn_setup()
    _L0_ffn_in = {k: v for k, v in _L0_ffn_all.items() if k in ('router_logits', 'gating_einsum', 'linear', 'per_expert_scale', 'router_scale')}
    del _L0_ffn_all

    def _L1_attn_setup():
        import jax, jax.numpy as jnp
        import numpy as np
        D_MODEL = 512
        N_HEADS = 16
        N_KV_HEADS = 4
        D_HEAD = 128
        R_K = 64
        R_V = 96
        ROPE_BASE = 10000.0
        B, S = (4, 512)

        def _rope_tables(seq_len, dtype):
            inv_freq = 1.0 / ROPE_BASE ** (jnp.arange(0, D_HEAD, 2, dtype=jnp.float32) / D_HEAD)
            pos = jnp.arange(seq_len, dtype=jnp.float32)
            freqs = pos[:, None] * inv_freq[None, :]
            emb = jnp.concatenate([freqs, freqs], axis=-1)
            return (jnp.cos(emb).astype(dtype), jnp.sin(emb).astype(dtype))

        def _rotate_half(x):
            x1, x2 = jnp.split(x, 2, axis=-1)
            return jnp.concatenate([-x2, x1], axis=-1)
        key = jax.random.key(seed)
        ks = jax.random.split(key, 9)
        sc = 0.02
        return {'hidden_states': jax.random.normal(ks[0], (B, S, D_MODEL), jnp.float32), 'Wq': jax.random.normal(ks[1], (N_HEADS * D_HEAD, D_MODEL), jnp.float32) * sc, 'Wk_down': jax.random.normal(ks[2], (R_K, D_MODEL), jnp.float32) * sc, 'Wk_up': jax.random.normal(ks[3], (N_KV_HEADS * D_HEAD, R_K), jnp.float32) * sc, 'Wv_down': jax.random.normal(ks[4], (R_V, D_MODEL), jnp.float32) * sc, 'Wv_up': jax.random.normal(ks[5], (N_KV_HEADS * D_HEAD, R_V), jnp.float32) * sc, 'k_anchor': jax.random.normal(ks[6], (N_KV_HEADS * D_HEAD,), jnp.float32) * sc, 'v_anchor': jax.random.normal(ks[7], (N_KV_HEADS * D_HEAD,), jnp.float32) * sc, 'Wo': jax.random.normal(ks[8], (D_MODEL, N_HEADS * D_HEAD), jnp.float32) * sc}
    _L1_attn_all = _L1_attn_setup()
    _L1_attn_in = {k: v for k, v in _L1_attn_all.items() if k in ('Wq', 'Wk_down', 'Wk_up', 'Wv_down', 'Wv_up', 'k_anchor', 'v_anchor', 'Wo')}
    del _L1_attn_all

    def _L1_xattn_setup():
        import jax, jax.numpy as jnp
        import numpy as np
        key = jax.random.key(seed)
        k1, k2, k3 = jax.random.split(key, 3)
        B, S, D, M = (8, 512, 512, 128)
        hidden_states = jax.random.normal(k1, (B, S, D), dtype=jnp.float32)
        memory_tokens = jax.random.normal(k2, (B, M, D), dtype=jnp.float32)
        memory_mask = jax.random.randint(k3, (B, M), 0, 2).astype(jnp.bool_)
        return {'hidden_states': hidden_states, 'memory_tokens': memory_tokens, 'memory_mask': memory_mask}
    _L1_xattn_all = _L1_xattn_setup()
    _L1_xattn_in = {k: v for k, v in _L1_xattn_all.items() if k in ()}
    del _L1_xattn_all

    def _L1_ffn_setup():
        import jax, jax.numpy as jnp
        import numpy as np
        import math
        B, S, D = (2, 512, 512)
        P = 4
        PW = 2
        L = 2
        STD = 0.02
        EPS = 1e-05

        def _layer_norm(x, g, b):
            m = jnp.mean(x, axis=-1, keepdims=True)
            v = jnp.mean(jnp.square(x - m), axis=-1, keepdims=True)
            return (x - m) * jax.lax.rsqrt(v + EPS) * g + b
        key = jax.random.key(seed)
        ks = jax.random.split(key, 16)
        n = lambda k, shape: jax.random.normal(k, shape, dtype=jnp.float32) * STD
        inp = {'x': jax.random.normal(ks[0], (B, S, D), dtype=jnp.float32), 'amp_w': n(ks[1], (D, D)), 'amp_b': jnp.zeros((D,), jnp.float32), 'ph_w': n(ks[2], (D, D)), 'ph_b': jnp.zeros((D,), jnp.float32), 'ent_w': n(ks[3], (L, D, P * D)), 'ent_b': jnp.zeros((L, P * D), jnp.float32), 'ent_pw': n(ks[4], (L, P * D, D)), 'ent_pb': jnp.zeros((L, D), jnp.float32), 'path_w': n(ks[5], (L, PW, D, D)), 'path_b': jnp.zeros((L, PW, D), jnp.float32), 'phase': jax.random.normal(ks[6], (L, PW, D), dtype=jnp.float32), 'ln3_g': jnp.ones((L, D), jnp.float32), 'ln3_b': jnp.zeros((L, D), jnp.float32), 'ln4_g': jnp.ones((L, D), jnp.float32), 'ln4_b': jnp.zeros((L, D), jnp.float32)}
        return inp
    _L1_ffn_all = _L1_ffn_setup()
    _L1_ffn_in = {k: v for k, v in _L1_ffn_all.items() if k in ('amp_w', 'amp_b', 'ph_w', 'ph_b', 'ent_w', 'ent_b', 'ent_pw', 'ent_pb', 'path_w', 'path_b', 'phase', 'ln3_g', 'ln3_b', 'ln4_g', 'ln4_b')}
    del _L1_ffn_all
    return {'x': x, 'ctx_2048': ctx_2048, 'mask_Bx1xSxS_fk0': mask_Bx1xSxS_fk0, 'mask_BxS2_bk0': mask_BxS2_bk0, 'L0_attn_Wq': _L0_attn_in['Wq'], 'L0_attn_bq': _L0_attn_in['bq'], 'L0_attn_Wk': _L0_attn_in['Wk'], 'L0_attn_bk': _L0_attn_in['bk'], 'L0_attn_Wv': _L0_attn_in['Wv'], 'L0_attn_bv': _L0_attn_in['bv'], 'L0_attn_Wo': _L0_attn_in['Wo'], 'L0_attn_bo': _L0_attn_in['bo'], 'L0_attn_sinks': _L0_attn_in['sinks'], 'L0_xattn_Wq': _L0_xattn_in['Wq'], 'L0_xattn_Wk': _L0_xattn_in['Wk'], 'L0_xattn_Wv': _L0_xattn_in['Wv'], 'L0_xattn_Wo': _L0_xattn_in['Wo'], 'L0_xattn_gate': _L0_xattn_in['gate'], 'L0_ffn_router_logits': _L0_ffn_in['router_logits'], 'L0_ffn_gating_einsum': _L0_ffn_in['gating_einsum'], 'L0_ffn_linear': _L0_ffn_in['linear'], 'L0_ffn_per_expert_scale': _L0_ffn_in['per_expert_scale'], 'L0_ffn_router_scale': _L0_ffn_in['router_scale'], 'L1_attn_Wq': _L1_attn_in['Wq'], 'L1_attn_Wk_down': _L1_attn_in['Wk_down'], 'L1_attn_Wk_up': _L1_attn_in['Wk_up'], 'L1_attn_Wv_down': _L1_attn_in['Wv_down'], 'L1_attn_Wv_up': _L1_attn_in['Wv_up'], 'L1_attn_k_anchor': _L1_attn_in['k_anchor'], 'L1_attn_v_anchor': _L1_attn_in['v_anchor'], 'L1_attn_Wo': _L1_attn_in['Wo'], 'L1_ffn_amp_w': _L1_ffn_in['amp_w'], 'L1_ffn_amp_b': _L1_ffn_in['amp_b'], 'L1_ffn_ph_w': _L1_ffn_in['ph_w'], 'L1_ffn_ph_b': _L1_ffn_in['ph_b'], 'L1_ffn_ent_w': _L1_ffn_in['ent_w'], 'L1_ffn_ent_b': _L1_ffn_in['ent_b'], 'L1_ffn_ent_pw': _L1_ffn_in['ent_pw'], 'L1_ffn_ent_pb': _L1_ffn_in['ent_pb'], 'L1_ffn_path_w': _L1_ffn_in['path_w'], 'L1_ffn_path_b': _L1_ffn_in['path_b'], 'L1_ffn_phase': _L1_ffn_in['phase'], 'L1_ffn_ln3_g': _L1_ffn_in['ln3_g'], 'L1_ffn_ln3_b': _L1_ffn_in['ln3_b'], 'L1_ffn_ln4_g': _L1_ffn_in['ln4_g'], 'L1_ffn_ln4_b': _L1_ffn_in['ln4_b']}

def reference(x, ctx_2048, mask_Bx1xSxS_fk0, mask_BxS2_bk0, L0_attn_Wq, L0_attn_bq, L0_attn_Wk, L0_attn_bk, L0_attn_Wv, L0_attn_bv, L0_attn_Wo, L0_attn_bo, L0_attn_sinks, L0_xattn_Wq, L0_xattn_Wk, L0_xattn_Wv, L0_xattn_Wo, L0_xattn_gate, L0_ffn_router_logits, L0_ffn_gating_einsum, L0_ffn_linear, L0_ffn_per_expert_scale, L0_ffn_router_scale, L1_attn_Wq, L1_attn_Wk_down, L1_attn_Wk_up, L1_attn_Wv_down, L1_attn_Wv_up, L1_attn_k_anchor, L1_attn_v_anchor, L1_attn_Wo, L1_ffn_amp_w, L1_ffn_amp_b, L1_ffn_ph_w, L1_ffn_ph_b, L1_ffn_ent_w, L1_ffn_ent_b, L1_ffn_ent_pw, L1_ffn_ent_pb, L1_ffn_path_w, L1_ffn_path_b, L1_ffn_phase, L1_ffn_ln3_g, L1_ffn_ln3_b, L1_ffn_ln4_g, L1_ffn_ln4_b):
    import jax
    import jax.numpy as jnp

    def _L0_attn_ref(hidden_states, Wq, bq, Wk, bk, Wv, bv, Wo, bo, sinks):
        import jax, jax.numpy as jnp
        import numpy as np
        B, S, M = (1, 512, 512)
        H, HKV, D = (32, 8, 64)
        SW = 128
        WAVELENGTH = 150000.0
        SCALE = D ** (-0.25)
        NEG = -1000000000.0

        def _cos_sin(seq_len, dtype):
            half = D // 2
            inv_freq = 1.0 / WAVELENGTH ** (jnp.arange(half, dtype=jnp.float32) * 2.0 / D)
            t = jnp.arange(seq_len, dtype=jnp.float32)
            freqs = t[:, None] * inv_freq[None, :]
            return (jnp.cos(freqs)[None, :, None, :].astype(dtype), jnp.sin(freqs)[None, :, None, :].astype(dtype))

        def _interleaved_rope(x, cos, sin):
            x_even = x[..., ::2]
            x_odd = x[..., 1::2]
            first = x_even * cos - x_odd * sin
            second = x_odd * cos + x_even * sin
            return jnp.stack([first, second], axis=-1).reshape(x.shape)
        b, s, _ = hidden_states.shape
        groups = H // HKV
        q = jnp.einsum('bqm,muh->bquh', hidden_states, Wq) + bq
        k = jnp.einsum('bkm,mvh->bkvh', hidden_states, Wk) + bk
        v = jnp.einsum('bkm,mvh->bkvh', hidden_states, Wv) + bv
        cos, sin = _cos_sin(s, hidden_states.dtype)
        q = _interleaved_rope(q, cos, sin) * SCALE
        k = _interleaved_rope(k, cos, sin) * SCALE
        k = jnp.repeat(k, groups, axis=2)
        v = jnp.repeat(v, groups, axis=2)
        scores = jnp.einsum('bquh,bkuh->buqk', q, k)
        pos = jnp.arange(s)
        sw_mask = jnp.abs(pos[:, None] - pos[None, :]) <= SW
        scores = jnp.where(sw_mask[None, None, :, :], scores, NEG)
        sink_logits = jnp.broadcast_to(sinks[None, :, None, None], (b, H, s, 1))
        combined = jnp.concatenate([scores, sink_logits], axis=-1)
        probs = jax.nn.softmax(combined.astype(jnp.float32), axis=-1)
        attn = probs[..., :-1].astype(hidden_states.dtype)
        out = jnp.einsum('buqk,bkuh->bquh', attn, v)
        return jnp.einsum('bquh,uhm->bqm', out, Wo) + bo

    def _L0_xattn_ref(hidden_states, attention_mask, adapter, Wq, Wk, Wv, Wo, gate):
        import jax, jax.numpy as jnp
        import numpy as np
        import math
        B, S, HID, H = (2, 512, 512, 32)
        D = HID // H
        AL = 10

        def _rope_tables(seq_len, dim, dtype):
            inv_freq = 1.0 / 10000.0 ** (np.arange(0, dim, 2, dtype=np.float32) / dim)
            t = np.arange(seq_len, dtype=np.float32)
            freqs = np.outer(t, inv_freq)
            emb = np.concatenate([freqs, freqs], -1)
            return (jnp.asarray(np.cos(emb), dtype), jnp.asarray(np.sin(emb), dtype))

        def _rotate_half(x):
            x1, x2 = jnp.split(x, 2, axis=-1)
            return jnp.concatenate([-x2, x1], axis=-1)
        bsz, q_len, hid = hidden_states.shape
        n_heads = gate.shape[1]
        head_dim = hid // n_heads
        inv_sqrt_d = 1.0 / math.sqrt(head_dim)

        def split_heads(x, length):
            return x.reshape(bsz, length, n_heads, head_dim).transpose(0, 2, 1, 3)
        q = split_heads(hidden_states @ Wq, q_len)
        k = split_heads(hidden_states @ Wk, q_len)
        v = split_heads(hidden_states @ Wv, q_len)
        cos, sin = _rope_tables(q_len, head_dim, q.dtype)
        q = q * cos + _rotate_half(q) * sin
        k = k * cos + _rotate_half(k) * sin
        scores = jnp.einsum('bhqd,bhkd->bhqk', q, k) * inv_sqrt_d
        scores = scores + attention_mask
        scores = jnp.maximum(scores, jnp.finfo(scores.dtype).min)
        w = jax.nn.softmax(scores.astype(jnp.float32), axis=-1).astype(q.dtype)
        attn_output = jnp.einsum('bhqk,bhkd->bhqd', w, v)
        adapter_len = adapter.shape[1]
        a_k = split_heads(adapter @ Wk, adapter_len)
        a_v = split_heads(adapter @ Wv, adapter_len)
        a_scores = jnp.einsum('bhqd,bhkd->bhqk', q, a_k) * inv_sqrt_d
        a_scores = jnp.tanh(gate) * jax.nn.softmax(a_scores.astype(jnp.float32), axis=-1).astype(q.dtype)
        attn_output = attn_output + jnp.einsum('bhqk,bhkd->bhqd', a_scores, a_v)
        attn_output = attn_output.transpose(0, 2, 1, 3).reshape(bsz, q_len, hid)
        return attn_output @ Wo

    def _L0_ffn_ref(x, router_logits, gating_einsum, linear, per_expert_scale, router_scale):
        import jax, jax.numpy as jnp
        import numpy as np
        TOP_K = 2
        G, S, F = x.shape
        E = router_logits.shape[-1]
        H = linear.shape[1]
        k = TOP_K
        dtype = x.dtype
        var = jnp.mean(jnp.square(x.astype(jnp.float32)), axis=-1, keepdims=True)
        router_input = x * jax.lax.rsqrt(var + 1e-06).astype(dtype)
        root_size = jax.lax.rsqrt(jnp.array(F, dtype=dtype))
        router_input = router_input * root_size * router_scale.astype(dtype)
        logits = jnp.einsum('gsd,de->gse', router_input, router_logits.astype(dtype))
        logits32 = logits.astype(jnp.float32)
        probs = jax.nn.softmax(logits32, axis=-1)
        _, choices = jax.lax.approx_max_k(logits32, k=k)
        indicator = jax.nn.one_hot(choices, E, dtype=probs.dtype).sum(axis=-2)
        renorm = jnp.sum(indicator * probs, axis=-1, keepdims=True)
        renorm = jnp.where(renorm > 0.0, renorm, 1.0)
        weights = probs / renorm
        x_flat = x.reshape((-1, F))
        batch_size = G * S
        choices_flat = choices.ravel()
        xs_order = choices_flat.argsort()
        xs_reverse_argsort = xs_order.argsort()
        xs_indices = jnp.repeat(jnp.arange(batch_size), k)[xs_order]
        sorted_xs = x_flat[xs_indices, :]
        choices_oh = jax.nn.one_hot(choices, num_classes=E, dtype=jnp.int32)
        tokens_per_expert = jnp.sum(choices_oh, axis=(0, 1, 2))
        combine_weights = (choices_oh.astype(jnp.float32) * jnp.expand_dims(weights, axis=2)).sum(axis=-1).astype(weights.dtype)
        w_gate = jnp.transpose(gating_einsum, (0, 3, 1, 2)).reshape(E, F, 2 * H)
        gate_out = jax.lax.ragged_dot(sorted_xs, w_gate.astype(dtype), group_sizes=tokens_per_expert)
        gate_out = gate_out.reshape(gate_out.shape[0], 2, H)
        activation = jax.nn.gelu(gate_out[:, 0, :]) * gate_out[:, 1, :]
        expert_outputs = jax.lax.ragged_dot(activation, linear.astype(dtype), group_sizes=tokens_per_expert)
        expert_indices = jnp.repeat(jnp.arange(E), tokens_per_expert, total_repeat_length=expert_outputs.shape[0])
        expert_outputs = expert_outputs * per_expert_scale.astype(expert_outputs.dtype)[expert_indices, None]
        out = expert_outputs[xs_reverse_argsort].reshape((G, S, k, -1))
        out = jnp.einsum('blkd,blk->bld', out, combine_weights, preferred_element_type=out.dtype)
        return out

    def _L1_attn_ref(hidden_states, Wq, Wk_down, Wk_up, Wv_down, Wv_up, k_anchor, v_anchor, Wo):
        import jax, jax.numpy as jnp
        import numpy as np
        D_MODEL = 512
        N_HEADS = 16
        N_KV_HEADS = 4
        D_HEAD = 128
        R_K = 64
        R_V = 96
        ROPE_BASE = 10000.0
        B, S = (4, 512)

        def _rope_tables(seq_len, dtype):
            inv_freq = 1.0 / ROPE_BASE ** (jnp.arange(0, D_HEAD, 2, dtype=jnp.float32) / D_HEAD)
            pos = jnp.arange(seq_len, dtype=jnp.float32)
            freqs = pos[:, None] * inv_freq[None, :]
            emb = jnp.concatenate([freqs, freqs], axis=-1)
            return (jnp.cos(emb).astype(dtype), jnp.sin(emb).astype(dtype))

        def _rotate_half(x):
            x1, x2 = jnp.split(x, 2, axis=-1)
            return jnp.concatenate([-x2, x1], axis=-1)
        b, s, _ = hidden_states.shape
        groups = N_HEADS // N_KV_HEADS
        scaling = 1.0 / jnp.sqrt(jnp.asarray(D_HEAD, hidden_states.dtype))
        q = hidden_states @ Wq.T
        k = hidden_states @ Wk_down.T @ Wk_up.T + k_anchor
        v = hidden_states @ Wv_down.T @ Wv_up.T + v_anchor
        q = q.reshape(b, s, N_HEADS, D_HEAD).transpose(0, 2, 1, 3)
        k = k.reshape(b, s, N_KV_HEADS, D_HEAD).transpose(0, 2, 1, 3)
        v = v.reshape(b, s, N_KV_HEADS, D_HEAD).transpose(0, 2, 1, 3)
        cos, sin = _rope_tables(s, hidden_states.dtype)
        cos = cos[None, None]
        sin = sin[None, None]
        q = q * cos + _rotate_half(q) * sin
        k = k * cos + _rotate_half(k) * sin
        k = jnp.repeat(k, groups, axis=1)
        v = jnp.repeat(v, groups, axis=1)
        scores = jnp.einsum('bhqd,bhkd->bhqk', q, k) * scaling
        causal = jnp.tril(jnp.ones((s, s), dtype=bool))
        scores = jnp.where(causal[None, None], scores, jnp.asarray(-1000000000.0, scores.dtype))
        attn = jax.nn.softmax(scores, axis=-1)
        out = jnp.einsum('bhqk,bhkd->bhqd', attn, v)
        out = out.transpose(0, 2, 1, 3).reshape(b, s, N_HEADS * D_HEAD)
        return out @ Wo.T

    def _L1_xattn_ref(hidden_states, memory_tokens, memory_mask):
        import jax, jax.numpy as jnp
        import numpy as np
        B, S, D = hidden_states.shape
        scale = 1.0 / jnp.sqrt(jnp.asarray(D, hidden_states.dtype))
        scores = jnp.einsum('bsd,bmd->bsm', hidden_states, memory_tokens) * scale
        neg_inf = jnp.asarray(-1e+30, scores.dtype)
        scores = jnp.where(memory_mask[:, None, :], scores, neg_inf)
        attn = jax.nn.softmax(scores, axis=-1)
        readout = jnp.einsum('bsm,bmd->bsd', attn, memory_tokens)
        valid_b = jnp.any(memory_mask, axis=-1)
        out = jnp.where(valid_b[:, None, None], readout, jnp.zeros_like(readout))
        return out

    def _L1_ffn_ref(x, amp_w, amp_b, ph_w, ph_b, ent_w, ent_b, ent_pw, ent_pb, path_w, path_b, phase, ln3_g, ln3_b, ln4_g, ln4_b):
        import jax, jax.numpy as jnp
        import numpy as np
        import math
        B, S, D = (2, 512, 512)
        P = 4
        PW = 2
        L = 2
        STD = 0.02
        EPS = 1e-05

        def _layer_norm(x, g, b):
            m = jnp.mean(x, axis=-1, keepdims=True)
            v = jnp.mean(jnp.square(x - m), axis=-1, keepdims=True)
            return (x - m) * jax.lax.rsqrt(v + EPS) * g + b
        amp = jax.nn.sigmoid(x @ amp_w + amp_b)
        ph = jnp.tanh(x @ ph_w + ph_b) * math.pi
        h = (jnp.cos(ph) + jnp.sin(ph)) * amp
        for l in range(L):
            e = h @ ent_w[l] + ent_b[l]
            ent = e @ ent_pw[l] + ent_pb[l]
            h = _layer_norm(h + ent, ln3_g[l], ln3_b[l])
            t = jnp.einsum('bsd,pdf->pbsf', h, path_w[l]) + path_b[l][:, None, None, :]
            mod = jnp.cos(phase[l]) + jnp.sin(phase[l])
            interf = jnp.sum(t * mod[:, None, None, :], axis=0)
            h = _layer_norm(h + interf, ln4_g[l], ln4_b[l])
        return h
    x = x + _L0_attn_ref(_layernorm(x, axis=-1), L0_attn_Wq, L0_attn_bq, L0_attn_Wk, L0_attn_bk, L0_attn_Wv, L0_attn_bv, L0_attn_Wo, L0_attn_bo, L0_attn_sinks)
    x = x + _L0_xattn_ref(_layernorm(x, axis=-1), mask_Bx1xSxS_fk0, ctx_2048, L0_xattn_Wq, L0_xattn_Wk, L0_xattn_Wv, L0_xattn_Wo, L0_xattn_gate)
    x = x + _L0_ffn_ref(_layernorm(x, axis=-1), L0_ffn_router_logits, L0_ffn_gating_einsum, L0_ffn_linear, L0_ffn_per_expert_scale, L0_ffn_router_scale)
    x = x + _L1_attn_ref(_layernorm(x, axis=-1), L1_attn_Wq, L1_attn_Wk_down, L1_attn_Wk_up, L1_attn_Wv_down, L1_attn_Wv_up, L1_attn_k_anchor, L1_attn_v_anchor, L1_attn_Wo)
    x = x + _L1_xattn_ref(_layernorm(x, axis=-1), ctx_2048, mask_BxS2_bk0)
    x = x + _L1_ffn_ref(_layernorm(x, axis=-1), L1_ffn_amp_w, L1_ffn_amp_b, L1_ffn_ph_w, L1_ffn_ph_b, L1_ffn_ent_w, L1_ffn_ent_b, L1_ffn_ent_pw, L1_ffn_ent_pb, L1_ffn_path_w, L1_ffn_path_b, L1_ffn_phase, L1_ffn_ln3_g, L1_ffn_ln3_b, L1_ffn_ln4_g, L1_ffn_ln4_b)
    return x

_drawn_inputs = setup_inputs


def setup_inputs(seed=0):
    import zlib

    import numpy as np

    out = dict(_drawn_inputs(seed))
    spreads = {'L0_attn_bq': (0.0, 0.8),
     'L0_attn_bk': (0.0, 0.8),
     'L0_attn_bv': (0.0, 0.1),
     'L0_attn_bo': (0.0, 0.1),
     'L0_ffn_per_expert_scale': (1.0, 0.6),
     'L0_ffn_router_scale': (1.0, 0.6),
     'L1_ffn_amp_b': (0.0, 0.271),
     'L1_ffn_ph_b': (0.0, 0.1),
     'L1_ffn_ent_b': (0.0, 0.1),
     'L1_ffn_ent_pb': (0.0, 0.1),
     'L1_ffn_path_b': (0.0, 0.1),
     'L1_ffn_ln3_g': (1.0, 0.2),
     'L1_ffn_ln3_b': (0.0, 0.1),
     'L1_ffn_ln4_g': (1.0, 0.2),
     'L1_ffn_ln4_b': (0.0, 0.1)}
    factors = {'L0_attn_Wq': 6.193,
     'L0_attn_Wk': 6.335,
     'L0_attn_sinks': 29.379,
     'L0_xattn_Wq': 5.5,
     'L0_xattn_Wk': 5.468,
     'L0_xattn_gate': 4.266,
     'L1_attn_Wq': 8.0,
     'L1_attn_Wk_down': 8.0,
     'L1_attn_Wk_up': 8.0,
     'L1_attn_Wv_up': 2.74,
     'L1_attn_k_anchor': 31.356,
     'L1_attn_v_anchor': 3.339}
    for name, (base, spread) in spreads.items():
        noise = np.random.default_rng([zlib.crc32(name.encode()), seed]).standard_normal(out[name].shape)
        drawn = base * np.exp(spread * noise) if base else spread * noise
        out[name] = jnp.asarray(drawn.astype(out[name].dtype))
    for name, factor in factors.items():
        out[name] = (out[name] * factor).astype(out[name].dtype)
    return out
```

```python
from contextlib import ExitStack

import numpy as np
import concourse.bass as bass
from concourse import mybir

F32 = mybir.dt.float32
U8 = mybir.dt.uint8
ALU = mybir.AluOpType
ACT = mybir.ActivationFunctionType
AX = mybir.AxisListType

NBATCH = 8
S = 112
D = 512
SC = 375
KC = 125
UB = 2
NU = NBATCH // UB
UT = UB * S
FMIN = float(np.finfo(np.float32).min)


class Op:

    def __init__(self, queue, issue, after):
        self.queue, self.issue, self.after = queue, issue, after
        self.used = False
        self.value = 0
        self.sem = None


class Queue:

    def __init__(self, name, sem):
        self.name, self.sem, self.ops = name, sem, []

    def __call__(self, issue, *after):
        op = Op(self, issue, flat(after))
        op.sem = self.sem
        self.ops.append(op)
        return op


class Load:

    def __init__(self, queue, sem, issues, after):
        self.queue, self.sem, self.used = queue, sem, True
        self.value = 16 * len(issues)
        for n, issue in enumerate(issues):
            op = Op(queue, issue, flat(after) if n == 0 else [])
            op.sem, op.dma = sem, True
            queue.ops.append(op)


def flat(after):
    out = []
    for a in after:
        if a is None:
            continue
        if isinstance(a, (list, tuple)):
            out += flat(a)
        else:
            out.append(a)
    return out


def count(queues):
    for q in queues:
        for op in q.ops:
            for a in op.after:
                a.used = True
    for q in queues:
        n = 0
        for op in q.ops:
            if op.sem is q.sem and op.used:
                n += 1
                op.value = n


def play(engine, queue):
    seen = {}
    for op in queue.ops:
        need = {}
        for a in op.after:
            key = a.sem.name
            if key not in need or need[key][1] < a.value:
                need[key] = (a.sem, a.value)
        for key, (sem, value) in need.items():
            if seen.get(key, 0) < value:
                engine.wait_ge(sem, value)
                seen[key] = value
        ins = op.issue(engine)
        if op.sem is not queue.sem:
            ins.then_inc(op.sem, 16)
        elif op.used:
            ins.then_inc(op.sem, 1)


CST = {}


def constants():
    parts = []

    def add(name, a):
        at = sum(p.shape[1] for p in parts)
        CST[name] = (at, a.shape[1])
        parts.append(a.astype(np.float32))

    f = np.float32
    p = np.arange(128)
    add("ident", np.eye(128))
    rot = np.zeros((128, 128), f)
    for j in range(128):
        if j % 16 < 8:
            rot[j + 8, j] = -1.0
        else:
            rot[j - 8, j] = 1.0
    add("rot", rot)
    t = np.arange(S, dtype=f)
    inv = f(1.0) / np.power(f(150000.0), np.arange(32, dtype=f) * f(2.0) / f(64))
    ang = (t[:, None] * inv[None, :]).astype(f).T[p % 32]
    c0, s0 = np.cos(ang), np.sin(ang)
    add("q0cos", c0 * f(0.125))
    add("q0sin", s0 * f(0.125))
    add("k0cos", c0)
    add("k0sin", s0)
    inv = f(1.0) / f(10000.0) ** (np.arange(0, 16, 2, dtype=f) / f(16))
    ang = np.outer(t, inv).astype(f).T[p % 8]
    c1, s1 = np.cos(ang), np.sin(ang)
    add("qxcos", c1 * f(0.25))
    add("qxsin", s1 * f(0.25))
    add("kxcos", c1)
    add("kxsin", s1)
    inv = f(1.0) / np.power(f(10000.0), np.arange(0, 128, 2, dtype=f) / f(128))
    ang = (t[:, None] * inv[None, :]).astype(f).T[p % 64]
    add("l1cos", np.cos(ang))
    add("l1sin", np.sin(ang))
    add("even", ((p // 16) % 2 == 0)[:, None])
    add("odd", ((p // 16) % 2 == 1)[:, None])
    k = np.arange(S)
    causal = np.where(k[None, :] <= k[:, None], 0.0, -1e9)
    add("causal", np.concatenate([causal, np.zeros((16, S))], 0))
    add("halfpi", np.full((128, 1), np.pi / 2))
    strict = np.zeros((128, S))
    strict[:S] = (k[:, None] < k[None, :])
    add("strict", strict)
    return np.ascontiguousarray(np.concatenate(parts, 1))


CONSTS = constants()
NCST = CONSTS.shape[1]
COLS = {"bq": (0, 16), "bk": (16, 4), "rscale": (20, 4), "kanch": (24, 4), "wr": (28, 32), "entb": (60, 32)}
NCOL = 92
ROWS = {"bv": (0, 512), "bo": (512, 512), "sinks": (1024, 32), "gate": (1056, 32), "pes": (1088, 8),
        "vanch": (1096, 512)}
NROW = 1608
ROW2 = ["ampb", "phb", "entpb0", "entpb1", "pb00", "pb01", "pb10", "pb11", "ph00", "ph01", "ph10", "ph11",
        "g30", "b30", "g31", "b31", "g40", "b40", "g41", "b41"]
WSLOTS = 10
RSIZE = 18700


def program(nc, a, out, stop=9):
    with ExitStack() as ctx:
        def sb(name, shape, dt=F32):
            return ctx.enter_context(nc.sbuf_tensor(name, shape, dt))

        def sem(name):
            return ctx.enter_context(nc.semaphore(name))

        PS = ctx.enter_context(nc.psum_tensor("PS", [128, 8, 512], F32))
        x = sb("x", [128, NBATCH, D])
        xT = sb("xT", [128, 4, NBATCH * S])
        W = sb("W", [128, WSLOTS, 2048])
        R = sb("R", [128, RSIZE])
        cst = sb("cst", [128, NCST])
        col = sb("col", [128, NCOL])
        row = sb("row", [128, NROW])
        st = sb("st", [128, NBATCH, 6])
        mv = sb("mv", [128, NBATCH, 2])
        rstd = sb("rstd", [128, NBATCH])
        veps = sb("veps", [128, NBATCH])
        mhalf = sb("mhalf", [128, 16])
        xn = sb("xn", [128, 2, D])

        pe = Queue("pe", sem("s_pe"))
        dve = Queue("dve", sem("s_dve"))
        act = Queue("act", sem("s_act"))
        pool = Queue("pool", sem("s_pool"))
        sp = Queue("sp", sem("s_sp"))
        queues = [pe, dve, act, pool, sp]

        def load(name, pairs, *after, q=sp):
            return Load(q, sem("d_" + name), [
                (lambda e, d=d, s=s: e.dma_start(d, s)) for d, s in pairs], after)

        def last():
            return [q.ops[-1] for q in (pe, dve, act, pool) if q.ops]

        def C(name, lo=0, hi=128):
            at, n = CST[name]
            return cst[lo:hi, at:at + n]

        def CL(name):
            at, n = COLS[name]
            return col[:, at:at + n]

        def RW(name, hi=S):
            at, n = ROWS[name]
            return row[0:hi, at:at + n]

        def mm(o, l, r, start, stop_, *after):
            return pe(lambda e: e.matmul(o, l, r, start=start, stop=stop_), *after)

        def tr(o, i, n, *after):
            return pe(lambda e: e.transpose(o, i, C("ident", 0, n)[:, 0:n]), *after)

        free = [None] * 8

        l_c = load("cst", [(cst[:, :], a["consts"]), (col[:, :], a["cols"]), (row[:, :], a["rows"])])
        l_x = [load(f"x{u}", [(x[0:S, u * UB:(u + 1) * UB, :], a["x"][:, u * UB:(u + 1) * UB, :])])
               for u in range(NU)]
        c_mh = pool(lambda e: e.memset(mhalf[:, :], -0.5))

        xn_free = [None, None]
        xT_ready = [None] * NBATCH
        read_x = [None] * NBATCH
        ncount = [0]

        def norm(b, deps, src=None, dst=None):
            src = x[0:S, b, :] if src is None else src
            k = ncount[0] % 2
            ncount[0] += 1
            dst_, w = (xn[0:S, k, :], xn_free[k]) if dst is None else (dst, None)
            o1 = dve(lambda e: e.bn_stats(st[0:S, b, :], src), deps)
            o2 = dve(lambda e: e.bn_aggr(mv[0:S, b, :], st[0:S, b, :]), o1)
            o3 = dve(lambda e: e.tensor_scalar(veps[0:S, b:b + 1], mv[0:S, b, 1:2], 1e-5, None, ALU.add), o2)
            o4 = pool(lambda e: e.tensor_tensor(rstd[0:S, b:b + 1], veps[0:S, b:b + 1], mhalf[0:S, 0:1],
                                                ALU.pow), o3, c_mh)
            o5 = dve(lambda e: e.tensor_scalar(dst_, src, mv[0:S, b, 0:1], rstd[0:S, b:b + 1],
                                               ALU.subtract, ALU.mult), o4, w)
            return o5, k, dst_

        def norm_t(b, deps, bank, src=None):
            o5, k, v = norm(b, deps, src)
            read_x[b] = o5
            return put_t(b, v, [o5], bank, k)

        def put_t(b, v, deps, bank, k=None, eng=None):
            for c in range(4):
                t = tr(PS[:, bank, c * S:(c + 1) * S], v[:, c * 128:(c + 1) * 128], S, deps, free[bank], l_c)
            if k is not None:
                xn_free[k] = t
            e_ = act if eng is None else eng
            src_ = PS[:, bank, 0:4 * S].rearrange("p (c n) -> p c n", c=4)
            dst_ = xT[:, :, b * S:(b + 1) * S]
            if e_ is act:
                o = act(lambda e: e.activation(dst_, src_, ACT.Copy), t, xT_free[b])
            else:
                o = dve(lambda e: e.tensor_copy(dst_, src_), t, xT_free[b])
            free[bank] = o
            xT_ready[b] = o
            return o

        xT_free = [None] * NBATCH
        x_ready = [l_x[b // UB] for b in range(NBATCH)]

        def wload(name, slot, src, n, *after):
            return load(name, [(W[:, slot:slot + n, :], src)], *after)

        l_kv = wload("w0kv", 4, a["w0kv"], 2)
        l_q = [wload(f"w0q{n}", n, a["w0q"][:, n:n + 1, :], 1) for n in range(4)]
        l_o = wload("w0o", 6, a["w0o"], 4)
        Wq = W[:, 0:4, :].rearrange("p a (c k n) -> p (a c) k n", c=2, k=4)
        Wk = W[:, 4, :].rearrange("p (k n) -> p k n", k=4)
        Wv = W[:, 5, :].rearrange("p (k n) -> p k n", k=4)
        Wo = W[:, 6:10, :].rearrange("p a (t n) -> p (a t) n", n=D)

        at = [0]

        def carve(n):
            o = at[0]
            at[0] += n
            assert at[0] <= RSIZE, at[0]
            return R[:, o:o + n]

        Q = carve(2 * 16 * UT).rearrange("p (z c a n) -> p z c a n", z=2, c=8, a=2)
        K = carve(4 * UT).rearrange("p (c a n) -> p c a n", c=2, a=2)
        V = carve(UB * 520).rearrange("p (b h n) -> p b h n", b=UB, h=8)
        T4 = carve(4 * UT).rearrange("p (k n) -> p k n", k=4)
        SS = carve(2 * 1792).rearrange("p (z n) -> p z n", z=2)
        PT = carve(4 * 448).rearrange("p (z n) -> p z n", z=4)
        O = carve(1024)
        OT = carve(8 * S).rearrange("p (t n) -> p t n", t=8)
        small = sb("small", [128, 2, 5, 32])
        rec4 = sb("rec4", [128, 4])
        ones_v = pool(lambda e: e.memset(V[0:S, :, :, 64:65], 1.0))

        def bc(t, n):
            return t.unsqueeze(1).to_broadcast([128, n, S])

        t4_free = [None]
        t4_buf = [T4]
        kv_free = [None]
        q_free = [None, None]

        def rope(bank, ba, bb, cos, sin, da, db, w_out, mmop):
            T4 = t4_buf[0]
            A = PS[:, bank, 0:UT].rearrange("p (b n) -> p b n", b=UB)
            B = PS[:, bank, UT:2 * UT].rearrange("p (b n) -> p b n", b=UB)

            def half(k, src, bias, tab, *w):
                o = T4[:, k, :].rearrange("p (b n) -> p b n", b=UB)
                return dve(lambda e: e.scalar_tensor_tensor(o, src, bias, bc(tab, UB), ALU.add, ALU.mult), *w)

            half(0, A, ba, cos, mmop, t4_free[0], l_c)
            o1 = half(1, B, bb, sin)
            half(2, B, bb, cos)
            o3 = half(3, A, ba, sin)
            free[bank] = o3
            p1 = pool(lambda e: e.tensor_tensor(da, T4[:, 0, :], T4[:, 1, :], ALU.subtract), o1, w_out)
            p2 = pool(lambda e: e.tensor_tensor(db, T4[:, 2, :], T4[:, 3, :], ALU.add), o3)
            t4_free[0] = p2
            return p2

        def project0(u, banks):
            tok = slice(u * UT, (u + 1) * UT)
            xr = [xT_ready[u * UB + i] for i in range(UB)]
            kr, vr, qr = [None] * 2, [None] * UB, [None] * 8
            n = 0
            for c in range(2):
                bank = banks[n % len(banks)]
                n += 1
                for ab in range(2):
                    for k in range(4):
                        lo = (c * 2 + ab) * 128
                        o = mm(PS[:, bank, ab * UT:(ab + 1) * UT], Wk[:, k, lo:lo + 128], xT[:, k, tok],
                               k == 0, k == 3, xr, l_kv, free[bank])
                bk = CL("bk")
                kr[c] = rope(bank, bk[:, 2 * c:2 * c + 1], bk[:, 2 * c + 1:2 * c + 2], C("k0cos"), C("k0sin"),
                             K[:, c, 0, :], K[:, c, 1, :], kv_free[0], o)
                yield
            for i in range(UB):
                bank = banks[n % len(banks)]
                n += 1
                b = u * UB + i
                for k in range(4):
                    o = mm(PS[0:S, bank, :], xT[:, k, b * S:(b + 1) * S], Wv[:, k, :], k == 0, k == 3,
                           xr, free[bank])
                vr[i] = dve(lambda e, bank=bank, i=i: e.tensor_tensor(
                    V[0:S, i, :, 0:64], PS[0:S, bank, :].rearrange("p (h n) -> p h n", h=8),
                    RW("bv").rearrange("p (h n) -> p h n", h=8), ALU.add), o, kv_free[0])
                free[bank] = vr[i]
                yield
            for c in range(8):
                bank = banks[n % len(banks)]
                n += 1
                for ab in range(2):
                    for k in range(4):
                        o = mm(PS[:, bank, ab * UT:(ab + 1) * UT], Wq[:, c, k, ab * 128:ab * 128 + 128],
                               xT[:, k, tok], k == 0, k == 3, xr, l_q[c // 2], free[bank])
                bq = CL("bq")
                qr[c] = rope(bank, bq[:, 2 * c:2 * c + 1], bq[:, 2 * c + 1:2 * c + 2], C("q0cos"), C("q0sin"),
                             Q[:, u % 2, c, 0, :], Q[:, u % 2, c, 1, :], q_free[u % 2], o)
                yield
            done0[u] = (kr, vr, qr)
            for i in range(UB):
                xT_free[u * UB + i] = o
            return

        done0 = [None] * NU
        ss_free = [None, None]
        pt_free = [None] * 4
        o_free, ot_free = [None], [None]
        pt_n = [0]

        def evac(k, dst, src, *w):
            if k % 2 == 0:
                return act(lambda e: e.activation(dst, src, ACT.Copy), *w)
            return dve(lambda e: e.tensor_copy(dst, src), *w)

        def attend0(u):
            kr, vr, qr = done0[u]
            todo = [(i, g) for i in range(UB) for g in range(2)]
            state = {}

            def scores(n):
                i, g = todo[n]
                tk = slice(i * S, (i + 1) * S)
                z = n % 2
                for j in range(4):
                    for ab in range(2):
                        for r in range(4):
                            ro = slice(32 * r, 32 * r + 32)
                            o = mm(PS[0:S, r, j * S:(j + 1) * S], Q[ro, u % 2, 4 * g + j, ab, tk],
                                   K[ro, g, ab, tk], ab == 0, ab == 1, qr[4 * g + j], kr[g], free[r])
                sm = small[0:S, z]
                pss = PS[0:S, 0:4, 0:448]
                o1 = dve(lambda e: e.tensor_reduce(sm[:, 0, 0:16], pss.rearrange("p r (j n) -> p r j n", j=4),
                                                   AX.X, ALU.max), o)
                sk = RW("sinks")[:, 16 * g:16 * g + 16]
                o2 = dve(lambda e: e.tensor_tensor(sm[:, 1, 0:16], sm[:, 0, 0:16], sk, ALU.max), o1)
                o3 = dve(lambda e: e.tensor_tensor(
                    SS[0:S, z, :].rearrange("p (r j n) -> p r j n", r=4, j=4),
                    pss.rearrange("p r (j n) -> p r j n", j=4),
                    sm[:, 1, 0:16].rearrange("p (r j) -> p r j", r=4).unsqueeze(3).to_broadcast([S, 4, 4, S]),
                    ALU.subtract), o2, ss_free[z])
                for r in range(4):
                    free[r] = o3
                o4 = dve(lambda e: e.tensor_tensor(sm[:, 2, 0:16], sk, sm[:, 1, 0:16], ALU.subtract), o2)
                o5 = act(lambda e: e.activation(SS[0:S, z, :], SS[0:S, z, :], ACT.Exp), o3)
                o6 = act(lambda e: e.activation(sm[:, 3, 0:16], sm[:, 2, 0:16], ACT.Exp), o4)
                state[n] = (o5, o6)

            def values(n):
                i, g = todo[n]
                b = u * UB + i
                z = n % 2
                o5, o6 = state[n]
                sm = small[0:S, z]
                pend = []

                def pv(q, oe, slot):
                    bank = 6
                    for h in range(4):
                        kvh = 4 * g + q
                        o = mm(PS[0:S, bank, h * 65:h * 65 + 65], PT[0:S, slot, h * S:(h + 1) * S],
                               V[0:S, i, kvh, :], True, True, oe, vr[i], ones_v, free[bank])
                    pt_free[slot] = o
                    pv_ = PS[0:S, bank, 0:260].rearrange("p (h n) -> p h n", h=4)
                    d1 = dve(lambda e: e.tensor_tensor(rec4[0:S, :], pv_[:, :, 64], sm[:, 3, 4 * q:4 * q + 4],
                                                       ALU.add), o, o6)
                    d2 = dve(lambda e: e.reciprocal(rec4[0:S, :], rec4[0:S, :]), d1)
                    d3 = dve(lambda e: e.tensor_tensor(
                        O[0:S, q * 256:(q + 1) * 256].rearrange("p (h n) -> p h n", h=4), pv_[:, :, 0:64],
                        rec4[0:S, :].unsqueeze(2).to_broadcast([S, 4, 64]), ALU.mult), d2, o_free[0])
                    free[bank] = d3
                    return o, d3

                for q in range(4):
                    bank = 4 + q % 2
                    slot = pt_n[0] % 4
                    pt_n[0] += 1
                    for h in range(4):
                        at_ = (q * 4 + h) * S
                        t = tr(PS[0:S, bank, h * S:(h + 1) * S], SS[0:S, z, at_:at_ + S], S, o5, free[bank])
                    oe = evac(q, PT[0:S, slot, :], PS[0:S, bank, 0:448], t, pt_free[slot])
                    free[bank] = oe
                    pend.append((q, oe, slot))
                    if len(pend) > 1:
                        pv(*pend.pop(0))
                ss_free[z] = t
                yield
                lastpv, d3 = pv(*pend.pop(0))
                for half in range(2):
                    bank = 4 + half
                    for c in range(4):
                        cc = half * 4 + c
                        t = tr(PS[:, bank, c * S:(c + 1) * S], O[0:S, cc * 128:(cc + 1) * 128], S, d3, free[bank])
                    oe = evac(half, OT[:, half * 4:half * 4 + 4, :],
                              PS[:, bank, 0:448].rearrange("p (c n) -> p c n", c=4), t, ot_free[0])
                    free[bank] = oe
                    oes = [oe] if half == 0 else oes + [oe]
                o_free[0] = t
                yield
                for c in range(8):
                    o = mm(PS[0:S, 7, :], OT[:, c, :], Wo[:, g * 8 + c, :], c == 0, c == 7, oes, l_o, free[7])
                ot_free[0] = o
                xa = dve(lambda e: e.tensor_tensor(x[0:S, b, :], x[0:S, b, :], PS[0:S, 7, :], ALU.add),
                         o, x_ready[b])
                free[7] = xa
                x_ready[b] = xa
                return lastpv

            for n in range(5):
                if n < 4:
                    scores(n)
                    yield
                if n >= 1:
                    lp = yield from values(n - 1)
                    yield
            kv_free[0] = lp
            q_free[u % 2] = lp

        def weave(main, fill, ratio):
            k = 0.0
            for _ in main:
                k += ratio
                while k >= 1:
                    next(fill, None)
                    k -= 1
            for _ in fill:
                pass

        def prep0(u):
            for i in range(UB):
                b = u * UB + i
                norm_t(b, [x_ready[b]], 4 + i % 2)
                x_ready[b] = pool(lambda e, b=b: e.tensor_tensor(x[0:S, b, :], x[0:S, b, :], RW("bo"), ALU.add),
                                  read_x[b], l_c)

        prep0(0)
        prep0(1)
        for _ in project0(0, [7, 0, 1, 2, 3]):
            pass
        for u in range(NU):
            if u + 2 < NU:
                prep0(u + 2)
            for _ in attend0(u):
                pass
            if u + 1 < NU:
                for _ in project0(u + 1, [7]):
                    pass

        if stop >= 2:
            fence = last()
            last_q0 = [done for done in xT_free]
            l_xw = [wload(f"wx{n}", n, a["wx"][:, n:n + 1, :], 1, last_q0) for n in range(4)]
            at[0] = 0
            X0 = W[:, 4:10, :].rearrange("p a n -> p (a n)")
            KcT = X0[:, 0:3000].rearrange("p (z c n) -> p z c n", z=2, c=4)
            Vc = X0[:, 3000:6072].rearrange("p (z t n) -> p z t n", z=2, t=3)
            CT = X0[:, 6072:9072].rearrange("p (z c n) -> p z c n", z=2, c=4)
            P = X0[:, 9072:12072].rearrange("p (z r n) -> p z r n", z=2, r=4)
            QM = carve(2 * 2 * 4 * UT).rearrange("p (z e c n) -> p z e c n", z=2, e=2, c=4)
            KX = carve(2 * 4 * UT).rearrange("p (z c n) -> p z c n", z=2, c=4)
            VX = carve(2 * UB * 544).rearrange("p (z b h n) -> p z b h n", z=2, b=UB, h=32)
            MK = carve(NBATCH * S).rearrange("p (b n) -> p b n", b=NBATCH)
            SX = carve(2 * 896).rearrange("p (z n) -> p z n", z=2)
            PX = carve(8 * 448).rearrange("p (z n) -> p z n", z=8)
            OX = carve(D)
            OXT = carve(4 * S).rearrange("p (t n) -> p t n", t=4)
            RT = carve(4 * UT).rearrange("p (k n) -> p k n", k=4)
            tg = sb("tg", [128, 32])
            sx = sb("sx", [128, 2, 2, 8])
            nmx = sb("nmx", [128, 2, 4])
            sumc = sb("sumc", [128, 2, 8])
            fx = sb("fx", [128, 2, 8])
            t128 = sb("t128", [128, 128])
            Wx = [W[:, n, :].rearrange("p (k n) -> p k n", k=4) for n in range(4)]

            l_mk = load("mask", [(MK[0:S], a["mask"])], fence)
            o_tg = act(lambda e: e.activation(tg[:, :], RW("gate", 128), ACT.Tanh), fence)
            ones_x = pool(lambda e: e.memset(VX[0:S, :, :, :, 16:17], 1.0), fence)
            f_dve = dve(lambda e: e.tensor_copy(veps[0:1, 0:1], veps[0:1, 0:1]), fence)
            l_ct = [None] * NBATCH
            ct_free = [None, None]
            kc_free = [None, None]
            qx_free = [None, None]
            rt_free = [None, None]
            kc_done = [None] * NBATCH
            qx_done = [None] * NU

            def load_ct(b):
                l_ct[b] = load(f"ct{b}", [(CT[:, b % 2], a["ctxT"][b])], fence, ct_free[b % 2])

            load_ct(0)
            load_ct(1)

            def context(b):
                z = b % 2
                kd, vd = [], []
                for c in range(4):
                    for k in range(4):
                        o = mm(PS[:, 7, 0:SC], Wx[1][:, k, c * 128:(c + 1) * 128], CT[:, z, k, :], k == 0, k == 3,
                               l_ct[b], l_xw[1], free[7])
                    oe = evac(c, KcT[:, z, c, :], PS[:, 7, 0:SC], o, kc_free[z], f_dve, fence)
                    free[7] = oe
                    kd.append(oe)
                    yield
                for t in range(3):
                    for k in range(4):
                        o = mm(PS[0:KC, 7, :], CT[:, z, k, t * KC:(t + 1) * KC], Wx[2][:, k, :], k == 0, k == 3,
                               l_xw[2], free[7])
                    oe = evac(t, Vc[0:KC, z, t, :], PS[0:KC, 7, :], o)
                    free[7] = oe
                    vd.append(oe)
                    yield
                ct_free[z] = o
                if b + 2 < NBATCH:
                    load_ct(b + 2)
                kc_done[b] = kd + vd

            def projectx(u):
                z = u % 2
                tok = slice(u * UT, (u + 1) * UT)
                xr = [xT_ready[u * UB + i] for i in range(UB)]
                done = []

                def b3(t):
                    return t.rearrange("p (b n) -> p b n", b=UB)

                for c in range(4):
                    for which in range(2):
                        cos, sin = (("qxcos", "qxsin"), ("kxcos", "kxsin"))[which]
                        for k in range(4):
                            o = mm(PS[:, 7, 0:UT], Wx[which][:, k, c * 128:(c + 1) * 128], xT[:, k, tok],
                                   k == 0, k == 3, xr, l_xw[which], free[7])
                        e1 = act(lambda e: e.activation(RT[:, 0, :], PS[:, 7, 0:UT], ACT.Copy), o, rt_free[0],
                                 fence)
                        t1 = pool(lambda e, cos=cos: e.tensor_tensor(
                            b3(RT[:, 1, :]), b3(RT[:, 0, :]), bc(C(cos), UB), ALU.mult), e1)
                        o = mm(PS[:, 7, UT:2 * UT], C("rot"), RT[:, 0, :], True, True, e1)
                        t2 = dve(lambda e, sin=sin: e.tensor_tensor(
                            b3(RT[:, 2, :]), b3(PS[:, 7, UT:2 * UT]), bc(C(sin), UB), ALU.mult), o, rt_free[0])
                        free[7] = t2
                        if which:
                            t3 = pool(lambda e, c=c: e.tensor_tensor(KX[:, z, c, :], RT[:, 1, :], RT[:, 2, :],
                                                                     ALU.add), t2, t1, qx_free[z])
                            rt_free[0] = t3
                            done.append(t3)
                        else:
                            t3 = pool(lambda e: e.tensor_tensor(RT[:, 3, :], RT[:, 1, :], RT[:, 2, :],
                                                                ALU.add), t2, t1)
                            for par in range(2):
                                t4 = dve(lambda e, par=par, c=c: e.tensor_scalar(
                                    QM[:, z, par, c, :], RT[:, 3, :], C(("even", "odd")[par]), None, ALU.mult),
                                    t3, qx_free[z])
                            rt_free[0] = t4
                            done.append(t4)
                    yield
                for i in range(UB):
                    b = u * UB + i
                    for k in range(4):
                        o = mm(PS[0:S, 7, :], xT[:, k, b * S:(b + 1) * S], Wx[2][:, k, :], k == 0, k == 3,
                               xr, l_xw[2], free[7])
                    oe = act(lambda e, i=i: e.activation(
                        VX[0:S, z, i, :, 0:16], PS[0:S, 7, :].rearrange("p (h n) -> p h n", h=32), ACT.Copy),
                        o, qx_free[z], fence)
                    free[7] = oe
                    done.append(oe)
                    xT_free[b] = o
                    yield
                qx_done[u] = done

            sx_free = [None, None]
            p_free = [None, None]
            px_free = [None] * 8
            px_n = [0]
            ox_free, oxt_free = [None], [None]
            small_free = [None, None]
            tb = [0]

            def attendx(b):
                u, i = b // UB, b % UB
                z = u % 2
                tk = slice(i * S, (i + 1) * S)
                zc = b % 2
                tasks = [(c, kind) for c in range(4) for kind in range(3)]
                state = {}

                def tbank():
                    tb[0] += 1
                    return 4 + tb[0] % 2

                def scores(n):
                    c, kind = tasks[n]
                    if kind == 0:
                        zz = c % 2
                        for par in range(2):
                            for r in range(4):
                                ro = slice(32 * r, 32 * r + 32)
                                o = mm(PS[0:S, r, par * S:(par + 1) * S], QM[ro, z, par, c, tk], KX[ro, z, c, tk],
                                       True, True, qx_done[u], free[r])
                        v3 = SX[0:S, zz, :].rearrange("p (h n) -> p h n", h=8)
                        pss = PS[0:S, 0:4, 0:2 * S].rearrange("p r (e n) -> p r e n", e=2)
                        sm = sx[0:S, zz]
                        o1 = dve(lambda e: e.tensor_tensor(
                            SX[0:S, zz, :].rearrange("p (r e n) -> p r e n", r=4, e=2), pss,
                            MK[0:S, b, :].unsqueeze(1).unsqueeze(1).to_broadcast([S, 4, 2, S]), ALU.add),
                            o, l_mk, sx_free[zz], fence)
                        for r in range(4):
                            free[r] = o1
                        o2 = dve(lambda e: e.tensor_reduce(sm[:, 0, :], v3, AX.X, ALU.max), o1)
                        o3 = dve(lambda e: e.tensor_scalar(sm[:, 1, :], sm[:, 0, :], FMIN, None, ALU.max), o2)
                        o4 = dve(lambda e: e.scalar_tensor_tensor(
                            v3, v3, FMIN, sm[:, 1, :].unsqueeze(2).to_broadcast([S, 8, S]),
                            ALU.max, ALU.subtract), o3)
                        o5 = act(lambda e: e.activation(SX[0:S, zz, :], SX[0:S, zz, :], ACT.Exp), o4)
                        state[n] = o5
                    else:
                        par = kind - 1
                        zz = (c * 2 + par) % 2
                        ops = []
                        for r in range(4):
                            ro = slice(32 * r, 32 * r + 32)
                            o = mm(PS[0:S, r, 0:SC], QM[ro, z, par, c, tk], KcT[ro, zc, c, :],
                                   True, True, kc_done[b], qx_done[u], free[r])
                            ops.append(o)
                        for r in range(4):
                            o1 = dve(lambda e, r=r: e.tensor_reduce(nmx[0:S, zz, r:r + 1], PS[0:S, r, 0:SC],
                                                                    AX.X, ALU.max, negate=True), ops[r],
                                     p_free[zz])
                            o2 = act(lambda e, r=r: e.activation(
                                P[0:S, zz, r, :], PS[0:S, r, 0:SC], ACT.Exp, bias=nmx[0:S, zz, r:r + 1],
                                accum_out=sumc[0:S, c % 2, 2 * r + par:2 * r + par + 1]),
                                o1, p_free[zz], small_free[c % 2], fence)
                            free[r] = o2
                            ops[r] = o2
                        state[n] = ops

                def values(n):
                    c, kind = tasks[n]
                    if kind == 0:
                        zz = c % 2
                        o5 = state[n]
                        got = []
                        for half in range(2):
                            bank = tbank()
                            slot = px_n[0] % 8
                            px_n[0] += 1
                            for h in range(4):
                                e_ = half * 4 + h
                                t = tr(PS[0:S, bank, h * S:(h + 1) * S], SX[0:S, zz, e_ * S:(e_ + 1) * S], S,
                                       o5, free[bank])
                            oe = evac(half, PX[0:S, slot, :], PS[0:S, bank, 0:448], t, px_free[slot])
                            free[bank] = oe
                            got.append((oe, slot))
                        sx_free[zz] = t
                        yield
                        for half in range(2):
                            oe, slot = got[half]
                            for h in range(4):
                                r, par = divmod(half * 4 + h, 2)
                                ln = 2 * r + par
                                o = mm(PS[0:S, 6, ln * 17:ln * 17 + 17], PX[0:S, slot, h * S:(h + 1) * S],
                                       VX[0:S, z, i, 8 * c + ln, :], True, True, oe, ones_x, free[6])
                            px_free[slot] = o
                        yield
                        return
                    par = kind - 1
                    zz = (c * 2 + par) % 2
                    ops = state[n]
                    got = []
                    for t_ in range(3):
                        bank = tbank()
                        slot = px_n[0] % 8
                        px_n[0] += 1
                        for r in range(4):
                            t = tr(PS[0:KC, bank, r * S:(r + 1) * S], P[0:S, zz, r, t_ * KC:(t_ + 1) * KC], S,
                                   ops[r], free[bank])
                        oe = evac(tb[0] + t_, PX[0:KC, slot, :], PS[0:KC, bank, 0:448], t, px_free[slot])
                        free[bank] = oe
                        got.append((oe, slot))
                    p_free[zz] = t
                    yield
                    for r in range(4):
                        ln = 2 * r + par
                        for t_ in range(3):
                            oe, slot = got[t_]
                            o = mm(PS[0:S, 6, 256 + ln * 16:272 + ln * 16], PX[0:KC, slot, r * S:(r + 1) * S],
                                   Vc[0:KC, zc, t_, (8 * c + ln) * 16:(8 * c + ln) * 16 + 16], t_ == 0, t_ == 2,
                                   oe)
                    for _, slot in got:
                        px_free[slot] = o
                    yield
                    if par == 0:
                        return
                    k = c % 2
                    sp_ = PS[0:S, 6, 0:136].rearrange("p (h n) -> p h n", h=8)
                    cp_ = PS[0:S, 6, 256:384].rearrange("p (h n) -> p h n", h=8)
                    d1 = dve(lambda e: e.reciprocal(fx[0:S, 0, :], sp_[:, :, 16]), o, fence)
                    d2 = dve(lambda e: e.reciprocal(fx[0:S, 1, :], sumc[0:S, k, :]), ops)
                    ov = OX[0:S, c * 128:(c + 1) * 128].rearrange("p (h n) -> p h n", h=8)
                    d3 = dve(lambda e: e.tensor_tensor(
                        ov, sp_[:, :, 0:16], fx[0:S, 0, :].unsqueeze(2).to_broadcast([S, 8, 16]), ALU.mult),
                        d1, ox_free[0])
                    d4 = dve(lambda e: e.tensor_tensor(fx[0:S, 1, :], fx[0:S, 1, :], tg[0:S, 8 * c:8 * c + 8],
                                                       ALU.mult), d2, o_tg)
                    d5 = dve(lambda e: e.tensor_tensor(
                        t128[0:S, :].rearrange("p (h n) -> p h n", h=8), cp_,
                        fx[0:S, 1, :].unsqueeze(2).to_broadcast([S, 8, 16]), ALU.mult), d4)
                    small_free[k] = d2
                    free[6] = d5
                    d6 = dve(lambda e: e.tensor_tensor(OX[0:S, c * 128:(c + 1) * 128],
                                                       OX[0:S, c * 128:(c + 1) * 128], t128[0:S, :], ALU.add),
                             d5, d3)
                    state["o"] = d6

                for n in range(len(tasks) + 1):
                    if n < len(tasks):
                        scores(n)
                        yield
                    if n >= 1:
                        yield from values(n - 1)
                bank = tbank()
                for c in range(4):
                    t = tr(PS[:, bank, c * S:(c + 1) * S], OX[0:S, c * 128:(c + 1) * 128], S, state["o"], free[bank])
                ox_free[0] = t
                oe = act(lambda e: e.activation(OXT[:, :, :], PS[:, bank, 0:448].rearrange("p (c n) -> p c n", c=4),
                                                ACT.Copy), t, oxt_free[0])
                free[bank] = oe
                yield
                for c in range(4):
                    o = mm(PS[0:S, 7, :], OXT[:, c, :], Wx[3][:, c, :], c == 0, c == 3, oe, l_xw[3], free[7])
                oxt_free[0] = o
                xa = dve(lambda e: e.tensor_tensor(x[0:S, b, :], x[0:S, b, :], PS[0:S, 7, :], ALU.add), o,
                         x_ready[b])
                free[7] = xa
                x_ready[b] = xa
                kc_free[zc] = px_free[(px_n[0] - 1) % 8]
                qx_free[z] = px_free[(px_n[0] - 1) % 8]

            def chain(*gens):
                for g in gens:
                    yield from g

            def prepx(u):
                for i in range(UB):
                    b = u * UB + i
                    norm_t(b, [x_ready[b]], 4 + i % 2)
                    yield

            for _ in chain(prepx(0), projectx(0), context(0)):
                pass
            for b in range(NBATCH):
                fills = []
                if b + 1 < NBATCH:
                    fills.append(context(b + 1))
                if b % UB == 0 and b // UB + 1 < NU:
                    fills += [prepx(b // UB + 1), projectx(b // UB + 1)]
                weave(attendx(b), chain(*fills), 0.4)

        if stop >= 3:
            fence = last()
            at[0] = 0
            ACC = carve(NBATCH * D).rearrange("p (b n) -> p b n", b=NBATCH)
            GA = carve(2 * 4 * 448).rearrange("p (z c n) -> p z c n", z=2, c=4)
            GS = carve(2 * 448).rearrange("p (z n) -> p z n", z=2)
            sq = carve(D)
            rt = sb("rt", [128, 12, 64])
            wr2 = sb("wr2", [128, 4, 8])
            ss8 = sb("ss8", [128, 8])
            f_act = act(lambda e: e.activation(sq[0:1, 0:1], cst[0:1, 0:1], ACT.Copy), fence)
            f_dve = dve(lambda e: e.tensor_copy(veps[0:1, 0:1], veps[0:1, 0:1]), fence)
            l_we = [None] * 8

            def load_e(x_, *after):
                l_we[x_] = wload(f"we{x_}", 3 * (x_ % 2), a["we"][x_], 3, *after)

            load_e(0, fence)
            load_e(1, fence)
            wr_o = [dve(lambda e, k=k: e.tensor_scalar(
                wr2[:, k, :], CL("wr")[:, 8 * k:8 * k + 8], CL("rscale")[:, k:k + 1], None, ALU.mult))
                for k in range(4)][-1]
            ssq = []
            for b in range(NBATCH):
                norm_t(b, [x_ready[b], fence], 4 + b % 2)
                k = (ncount[0] - 1) % 2
                o = act(lambda e, b=b, k=k: e.activation(sq[0:S, :], xn[0:S, k, :], ACT.Square,
                                                         accum_out=ss8[0:S, b:b + 1]), read_x[b], f_act, ssq[-1:])
                xn_free[k] = [xn_free[k], o]
                ssq.append(o)
            for b in range(NBATCH):
                for k in range(4):
                    o = mm(PS[0:S, 6, b * 8:b * 8 + 8], xT[:, k, b * S:(b + 1) * S], wr2[:, k, :], k == 0, k == 3,
                           xT_ready[b], wr_o, free[6])

            def r8(n):
                return rt[0:S, n, :].rearrange("p (b n) -> p b n", b=8)

            def b8(ap):
                return ap.unsqueeze(2).to_broadcast([S, 8, 8])

            d = dve(lambda e: e.tensor_scalar(rt[0:S, 8, 0:8], ss8[0:S, :], 1.0 / D, 1e-6, ALU.mult, ALU.add), ssq)
            d = pool(lambda e: e.tensor_tensor(rt[0:S, 8, 8:16], rt[0:S, 8, 0:8], mhalf[0:S, 0:8], ALU.pow), d)
            d = dve(lambda e: e.tensor_scalar(rt[0:S, 8, 8:16], rt[0:S, 8, 8:16], float(np.float32(D) ** -0.5), None,
                                              ALU.mult), d)
            d = dve(lambda e: e.tensor_tensor(r8(0), PS[0:S, 6, 0:64].rearrange("p (b n) -> p b n", b=8),
                                              b8(rt[0:S, 8, 8:16]), ALU.mult), d, o, fence)
            free[6] = d
            dl = d
            o_rank = pool(lambda e: e.memset(r8(9)[:, :, 0:1], 8.0), fence)
            for n in range(1, 8):
                o_rank = pool(lambda e, n=n: e.memset(r8(9)[:, :, n:n + 1], 8.0 - n))
            cur = 0
            sel = []
            for step in range(2):
                m = rt[0:S, 8, 16 + 8 * step:24 + 8 * step]
                m2 = rt[0:S, 8, 32 + 8 * step:40 + 8 * step]
                d = dve(lambda e, m=m, cur=cur: e.tensor_reduce(m, r8(cur), AX.X, ALU.max), d)
                if step == 0:
                    dm = d
                d = dve(lambda e, m=m, cur=cur: e.tensor_tensor(r8(2), r8(cur), b8(m), ALU.is_equal), d)
                d = dve(lambda e: e.tensor_tensor(r8(2), r8(2), r8(9), ALU.mult), d, o_rank)
                d = dve(lambda e, m2=m2: e.tensor_reduce(m2, r8(2), AX.X, ALU.max), d)
                d = dve(lambda e, m2=m2, step=step: e.tensor_tensor(r8(3 + step), r8(2), b8(m2), ALU.is_equal), d)
                sel.append(d)
                if step == 0:
                    d = dve(lambda e: e.tensor_scalar(r8(1), r8(3), -3.0e38, None, ALU.mult), d)
                    d = dve(lambda e: e.tensor_tensor(r8(1), r8(1), r8(0), ALU.add), d)
                cur = 1
            d = dve(lambda e: e.tensor_tensor(r8(5), r8(3), r8(4), ALU.add), d)
            d = dve(lambda e: e.tensor_tensor(r8(6), r8(0), b8(rt[0:S, 8, 16:24]), ALU.subtract), d)
            d = act(lambda e: e.activation(rt[0:S, 6, :], rt[0:S, 6, :], ACT.Exp), d)
            d = dve(lambda e: e.tensor_reduce(rt[0:S, 8, 48:56], r8(6), AX.X, ALU.add), d)
            d = dve(lambda e: e.reciprocal(rt[0:S, 8, 48:56], rt[0:S, 8, 48:56]), d)
            d = dve(lambda e: e.tensor_tensor(r8(6), r8(6), b8(rt[0:S, 8, 48:56]), ALU.mult), d)
            d = dve(lambda e: e.tensor_tensor(r8(7), r8(6), r8(5), ALU.mult), d)
            d = dve(lambda e: e.tensor_reduce(rt[0:S, 8, 56:64], r8(7), AX.X, ALU.add), d)
            d = dve(lambda e: e.tensor_scalar(rt[0:S, 10, 0:8], rt[0:S, 8, 56:64], 0.0, None, ALU.is_le), d)
            d = dve(lambda e: e.tensor_tensor(rt[0:S, 8, 56:64], rt[0:S, 8, 56:64], rt[0:S, 10, 0:8], ALU.add), d)
            d = dve(lambda e: e.reciprocal(rt[0:S, 8, 56:64], rt[0:S, 8, 56:64]), d)
            d = dve(lambda e: e.tensor_tensor(r8(7), r8(7), b8(rt[0:S, 8, 56:64]), ALU.mult), d)
            cw = dve(lambda e: e.tensor_tensor(r8(11), r8(7), RW("pes").unsqueeze(1).to_broadcast([S, 8, 8]),
                                               ALU.mult), d)
            gs_free, ga_free = [None, None], [None, None]
            accd = list(x_ready)
            nb = [0]

            def nbank():
                nb[0] += 1
                return nb[0] % 8

            for e_ in range(8):
                Wg = W[:, 3 * (e_ % 2):3 * (e_ % 2) + 2, :].rearrange("p a (k n) -> p (a k) n", k=2)
                Wl = W[:, 3 * (e_ % 2) + 2, :].rearrange("p (k n) -> p k n", k=4)
                for h in range(2):
                    z = (e_ * 2 + h) % 2
                    tok = slice(h * 448, (h + 1) * 448)
                    ga = []
                    for c in range(4):
                        bg, bu = nbank(), nbank()
                        for bank, off in ((bg, 0), (bu, 512)):
                            for k in range(4):
                                o = mm(PS[:, bank, 0:448], Wg[:, k, off + c * 128:off + c * 128 + 128], xT[:, k, tok],
                                       k == 0, k == 3, l_we[e_], xT_ready[4 * h:4 * h + 4], free[bank])
                            if off == 0:
                                og = o
                        zs = c % 2
                        o1 = act(lambda e, bg=bg, zs=zs: e.activation(GS[:, zs, :], PS[:, bg, 0:448],
                                                                      ACT.Gelu_apprx_tanh), og, gs_free[zs], f_act)
                        free[bg] = o1
                        o2 = dve(lambda e, bu=bu, zs=zs, z=z, c=c: e.tensor_tensor(
                            GA[:, z, c, :], GS[:, zs, :], PS[:, bu, 0:448], ALU.mult), o1, o, ga_free[z], f_dve)
                        free[bu] = o2
                        gs_free[zs] = o2
                        ga.append(o2)
                    for i in range(4):
                        b = h * 4 + i
                        bank = nbank()
                        for k in range(4):
                            o = mm(PS[0:S, bank, :], GA[:, z, k, i * S:(i + 1) * S], Wl[:, k, :], k == 0, k == 3,
                                   ga, free[bank])
                        sc = rt[0:S, 11, b * 8 + e_:b * 8 + e_ + 1]
                        oa = dve(lambda e, bank=bank, b=b, sc=sc: e.scalar_tensor_tensor(
                            x[0:S, b, :], PS[0:S, bank, :], sc, x[0:S, b, :], ALU.mult, ALU.add), o, cw, accd[b])
                        free[bank] = oa
                        accd[b] = oa
                    ga_free[z] = o
                if e_ + 2 < 8:
                    load_e(e_ + 2, o)
            for b in range(NBATCH):
                x_ready[b] = accd[b]
                xT_free[b] = o

        if stop >= 4:
            fence = last()
            at[0] = 0
            LQ = carve(2 * 16 * UT).rearrange("p (z c a n) -> p z c a n", z=2, c=8, a=2)
            LK = carve(2 * 4 * UT).rearrange("p (z c a n) -> p z c a n", z=2, c=2, a=2)
            LV = carve(2 * UB * 512).rearrange("p (z b n) -> p z b n", z=2, b=UB)
            LT = carve(2 * UT).rearrange("p (k n) -> p k n", k=2)
            t4_buf[0] = carve(4 * UT).rearrange("p (k n) -> p k n", k=4)
            t4_free[0] = fence
            LS = carve(2 * 896).rearrange("p (z n) -> p z n", z=2)
            LP = carve(4 * 448).rearrange("p (z n) -> p z n", z=4)
            LO = carve(1024)
            LOT = carve(8 * S).rearrange("p (t n) -> p t n", t=8)
            ls = sb("ls", [128, 2, 3, 8])
            l_lq = [wload(f"w1q{n}", n, a["w1q"][:, n:n + 1, :], 1, fence) for n in range(4)]
            l_ls = load("w1s", [(W[:, 8, 0:1664], a["w1s"])], fence)
            l_lo = wload("w1o", 4, a["w1o"], 4, fence)
            f_act = act(lambda e: e.activation(LT[0:1, 0, 0:1], cst[0:1, 0:1], ACT.Copy), fence)
            f_dve = dve(lambda e: e.tensor_copy(veps[0:1, 0:1], veps[0:1, 0:1]), fence)
            f_pool = pool(lambda e: e.memset(veps[0:1, 1:2], 0.0), fence)
            Wlq = W[:, 0:4, :].rearrange("p a (c k n) -> p (a c) k n", c=2, k=4)
            Wlo = W[:, 4:8, :].rearrange("p a (t n) -> p (a t) n", n=D)
            kd_w = W[:, 8, 0:256].rearrange("p (k n) -> p k n", k=4)
            vd_w = W[:, 8, 256:640].rearrange("p (k n) -> p k n", k=4)
            ku_w = W[0:64, 8, 640:1152]
            vu_w = W[0:96, 8, 1152:1664]
            l_free = [None, None]
            l_done = [None] * NU
            lt_free = [None]

            def projectl(u):
                z = u % 2
                tok = slice(u * UT, (u + 1) * UT)
                xr = [xT_ready[u * UB + i] for i in range(UB)]
                kr, vr, qr = [None] * 2, [None] * UB, [None] * 8
                td = []
                for n, (w, m) in enumerate(((kd_w, 64), (vd_w, 96))):
                    for k in range(4):
                        o = mm(PS[0:m, 7, 0:UT], w[:, k, :], xT[:, k, tok], k == 0, k == 3, xr, l_ls, free[7])
                    o = act(lambda e, n=n, m=m: e.activation(LT[0:m, n, :], PS[0:m, 7, 0:UT], ACT.Copy), o,
                            lt_free[0], f_act)
                    free[7] = o
                    td.append(o)
                    yield
                for c in range(2):
                    for ab in range(2):
                        lo = (c * 2 + ab) * 128
                        o = mm(PS[:, 7, ab * UT:(ab + 1) * UT], ku_w[:, lo:lo + 128], LT[0:64, 0, :], True, True,
                               td, free[7])
                    bk = CL("kanch")
                    kr[c] = rope(7, bk[:, 2 * c:2 * c + 1], bk[:, 2 * c + 1:2 * c + 2], C("l1cos"), C("l1sin"),
                                 LK[:, z, c, 0, :], LK[:, z, c, 1, :], [l_free[z], f_pool], o)
                    yield
                for i in range(UB):
                    o = mm(PS[0:S, 7, :], LT[0:96, 1, i * S:(i + 1) * S], vu_w, True, True, td, free[7])
                    vr[i] = dve(lambda e, i=i: e.tensor_tensor(LV[0:S, z, i, :], PS[0:S, 7, :], RW("vanch"), ALU.add),
                                o, l_free[z], f_dve)
                    free[7] = vr[i]
                lt_free[0] = o
                yield
                for c in range(8):
                    for ab in range(2):
                        for k in range(4):
                            o = mm(PS[:, 7, ab * UT:(ab + 1) * UT], Wlq[:, c, k, ab * 128:ab * 128 + 128],
                                   xT[:, k, tok], k == 0, k == 3, xr, l_lq[c // 2], free[7])
                    qr[c] = rope(7, 0.0, 0.0, C("l1cos"), C("l1sin"), LQ[:, z, c, 0, :], LQ[:, z, c, 1, :],
                                 [l_free[z], f_pool], o)
                    yield
                l_done[u] = (kr, vr, qr)
                for i in range(UB):
                    xT_free[u * UB + i] = o

            lss_free, lp_free = [None, None], [None] * 4
            lo_free, lot_free = [None], [None]
            lp_n = [0]
            scale1 = float(np.float32(1.0) / np.sqrt(np.float32(128)))

            def attendl(u):
                z = u % 2
                kr, vr, qr = l_done[u]
                todo = [(i, g) for i in range(UB) for g in range(2)]
                state = {}

                def scores(n):
                    i, g = todo[n]
                    tk = slice(i * S, (i + 1) * S)
                    zz = n % 2
                    for j in range(4):
                        for ab in range(2):
                            for r in range(2):
                                ro = slice(64 * r, 64 * r + 64)
                                o = mm(PS[0:S, 2 * zz + r, j * S:(j + 1) * S], LQ[ro, z, 4 * g + j, ab, tk],
                                       LK[ro, z, g, ab, tk], ab == 0, ab == 1, qr[4 * g + j], kr[g],
                                       free[2 * zz + r])
                    sm = ls[0:S, zz]
                    v3 = LS[0:S, zz, :].rearrange("p (h n) -> p h n", h=8)
                    o1 = dve(lambda e: e.tensor_tensor(
                        LS[0:S, zz, :].rearrange("p (r j n) -> p r j n", r=2, j=4),
                        PS[0:S, 2 * zz:2 * zz + 2, 0:448].rearrange("p r (j n) -> p r j n", j=4),
                        C("causal", 0, S).unsqueeze(1).unsqueeze(1).to_broadcast([S, 2, 4, S]), ALU.add),
                        o, lss_free[zz], f_dve)
                    for r in range(2):
                        free[2 * zz + r] = o1
                    o2 = dve(lambda e: e.tensor_reduce(sm[:, 0, :], v3, AX.X, ALU.max, negate=True), o1,
                             lss_free[zz])
                    o3 = dve(lambda e: e.tensor_scalar(sm[:, 1, :], sm[:, 0, :], scale1, None, ALU.mult), o2)
                    for h in range(8):
                        o4 = act(lambda e, h=h: e.activation(
                            v3[:, h, :], v3[:, h, :], ACT.Exp, bias=sm[:, 1, h:h + 1], scale=scale1,
                            accum_out=sm[:, 2, h:h + 1]), o3, f_act)
                    state[n] = o4

                def values(n):
                    i, g = todo[n]
                    b = u * UB + i
                    zz = n % 2
                    o4 = state[n]
                    sm = ls[0:S, zz]
                    rc = dve(lambda e: e.reciprocal(sm[:, 2, :], sm[:, 2, :]), o4)
                    got = []
                    for r in range(2):
                        bank = 4 + r
                        slot = lp_n[0] % 4
                        lp_n[0] += 1
                        for j in range(4):
                            h = 4 * r + j
                            t = tr(PS[0:S, bank, j * S:(j + 1) * S], LS[0:S, zz, h * S:(h + 1) * S], S, o4, free[bank])
                        oe = evac(r, LP[0:S, slot, :], PS[0:S, bank, 0:448], t, lp_free[slot])
                        free[bank] = oe
                        got.append((oe, slot))
                    yield
                    for r in range(2):
                        oe, slot = got[r]
                        kv = 2 * g + r
                        for j in range(4):
                            o = mm(PS[0:S, 6, j * 128:(j + 1) * 128], LP[0:S, slot, j * S:(j + 1) * S],
                                   LV[0:S, z, i, kv * 128:(kv + 1) * 128], True, True, oe, vr[i], free[6])
                        lp_free[slot] = o
                        d3 = dve(lambda e, r=r: e.tensor_tensor(
                            LO[0:S, r * 512:(r + 1) * 512].rearrange("p (h n) -> p h n", h=4),
                            PS[0:S, 6, :].rearrange("p (h n) -> p h n", h=4),
                            sm[:, 2, 4 * r:4 * r + 4].unsqueeze(2).to_broadcast([S, 4, 128]), ALU.mult),
                            o, rc, lo_free[0])
                        free[6] = d3
                        yield
                    lss_free[zz] = [t, d3]
                    lastpv = o
                    oes = []
                    for half in range(2):
                        bank = 4 + half
                        for c in range(4):
                            cc = half * 4 + c
                            t = tr(PS[:, bank, c * S:(c + 1) * S], LO[0:S, cc * 128:(cc + 1) * 128], S, d3,
                                   free[bank])
                        oe = evac(half, LOT[:, half * 4:half * 4 + 4, :],
                                  PS[:, bank, 0:448].rearrange("p (c n) -> p c n", c=4), t, lot_free[0])
                        free[bank] = oe
                        oes.append(oe)
                    lo_free[0] = t
                    yield
                    for c in range(8):
                        o = mm(PS[0:S, 7, :], LOT[:, c, :], Wlo[:, g * 8 + c, :], c == 0, c == 7, oes, l_lo, free[7])
                    lot_free[0] = o
                    xa = dve(lambda e: e.tensor_tensor(x[0:S, b, :], x[0:S, b, :], PS[0:S, 7, :], ALU.add),
                             o, x_ready[b])
                    free[7] = xa
                    x_ready[b] = xa
                    return lastpv

                for n in range(5):
                    if n < 4:
                        scores(n)
                        yield
                    if n >= 1:
                        lp = yield from values(n - 1)
                        yield
                l_free[z] = lp

            def prepl(u):
                for i in range(UB):
                    norm_t(u * UB + i, [x_ready[u * UB + i]], 4 + i % 2)
                    yield

            for _ in chain(prepl(0), projectl(0)):
                pass
            for u in range(NU):
                fill = chain(prepl(u + 1), projectl(u + 1)) if u + 1 < NU else iter(())
                weave(attendl(u), fill, 0.6)

        if stop >= 5:
            fence = last()
            at[0] = 0
            C5 = carve(3 * 1500).rearrange("p (z k n) -> p z k n", z=3, k=4)
            M5 = carve(3 * 1536).rearrange("p (z t n) -> p z t n", z=3, t=3)
            MF = carve(3000).rearrange("p (b n) -> p b n", b=8)
            NB = carve(3000).rearrange("p (b n) -> p b n", b=8)
            S5 = carve(2 * SC).rearrange("p (z n) -> p z n", z=2)
            P5 = carve(2 * 3 * S).rearrange("p (z t n) -> p z t n", z=2, t=3)
            mu = carve(8 * SC // 4).bitcast(U8)
            s5 = sb("s5", [128, 8, 4])
            scale5 = float(np.float32(1.0) / np.sqrt(np.float32(512)))
            l_mu = load("mu", [(mu[0:S, :], a["cmask"])], fence)
            l_c5 = [None] * 8
            c5_free = [None] * 3

            def load5(b):
                l_c5[b] = load(f"c5{b}", [(C5[:, b % 3], a["ctxT"][b]), (M5[0:KC, b % 3], a["ctx"][b])],
                               fence, c5_free[b % 3])

            for b in range(3):
                load5(b)
            m1 = dve(lambda e: e.tensor_copy(MF[0:S, :, :], mu[0:S, :].rearrange("p (b n) -> p b n", b=8)),
                     l_mu, fence)
            m2 = dve(lambda e: e.tensor_scalar(NB[0:S, :, :], MF[0:S, :, :], -1.0, 1e30, ALU.add, ALU.mult), m1)
            m3 = dve(lambda e: e.tensor_reduce(s5[0:S, :, 3], MF[0:S, :, :], AX.X, ALU.max), m1)
            s5_free = [None, None]
            p5_free = [None, None]
            st5 = {}

            def scores5(b):
                z = b % 2
                bank = z
                norm_t(b, [x_ready[b]], 4 + z)
                for k in range(4):
                    o = mm(PS[0:S, bank, 0:SC], xT[:, k, b * S:(b + 1) * S], C5[:, b % 3, k, :], k == 0, k == 3,
                           xT_ready[b], l_c5[b], free[bank])
                xT_free[b] = o
                sv = S5[0:S, z, :]
                o = dve(lambda e: e.tensor_tensor(sv, PS[0:S, bank, 0:SC], MF[0:S, b, :], ALU.mult), o, m2,
                        s5_free[z])
                free[bank] = o
                o = dve(lambda e: e.tensor_tensor(sv, sv, NB[0:S, b, :], ALU.add), o)
                o = dve(lambda e: e.tensor_reduce(s5[0:S, b, 0:1], sv, AX.X, ALU.max, negate=True), o)
                o = dve(lambda e: e.tensor_scalar(s5[0:S, b, 1:2], s5[0:S, b, 0:1], scale5, None, ALU.mult), o)
                o = act(lambda e: e.activation(sv, sv, ACT.Exp, bias=s5[0:S, b, 1:2], scale=scale5,
                                               accum_out=s5[0:S, b, 2:3]), o)
                q = dve(lambda e: e.reciprocal(s5[0:S, b, 2:3], s5[0:S, b, 2:3]), o)
                q = dve(lambda e: e.tensor_tensor(s5[0:S, b, 2:3], s5[0:S, b, 2:3], s5[0:S, b, 3:4], ALU.mult),
                        q, m3)
                st5[b] = (o, q)

            def values5(b):
                z = b % 2
                o, q = st5[b]
                for t_ in range(3):
                    t = tr(PS[0:KC, 2 + z, t_ * S:(t_ + 1) * S], S5[0:S, z, t_ * KC:(t_ + 1) * KC], S, o,
                           free[2 + z])
                s5_free[z] = t
                oe = act(lambda e: e.activation(P5[0:KC, z, :, :].rearrange("p t n -> p (t n)"),
                                                PS[0:KC, 2 + z, 0:3 * S], ACT.Copy), t, p5_free[z], fence)
                free[2 + z] = oe
                bank = 6 + z
                for t_ in range(3):
                    o = mm(PS[0:S, bank, :], P5[0:KC, z, t_, :], M5[0:KC, b % 3, t_, :], t_ == 0, t_ == 2, oe,
                           free[bank])
                p5_free[z] = o
                c5_free[b % 3] = o
                xa = dve(lambda e: e.scalar_tensor_tensor(x[0:S, b, :], PS[0:S, bank, :], s5[0:S, b, 2:3],
                                                          x[0:S, b, :], ALU.mult, ALU.add), o, q, x_ready[b])
                free[bank] = xa
                x_ready[b] = xa
                if b + 3 < NBATCH:
                    load5(b + 3)

            for b in range(NBATCH + 1):
                if b < NBATCH:
                    scores5(b)
                if b >= 1:
                    values5(b - 1)

        if stop >= 6:
            fence = last()
            at[0] = 0
            RB = carve(20 * D).rearrange("p (k n) -> p k n", k=20)
            H = carve(NBATCH * D).rearrange("p (b n) -> p b n", b=NBATCH)
            EB = carve(16 * S).rearrange("p (k n) -> p k n", k=16)
            MD = carve(2 * D).rearrange("p (k n) -> p k n", k=2)
            TS = carve(3 * D).rearrange("p (k n) -> p k n", k=3)
            f_act = act(lambda e: e.activation(MD[0:1, 0, 0:1], cst[0:1, 0:1], ACT.Copy), fence)
            f_dve = dve(lambda e: e.tensor_copy(veps[0:1, 0:1], veps[0:1, 0:1]), fence)
            f_pool = pool(lambda e: e.memset(veps[0:1, 1:2], 0.0), fence)
            l_rb = load("rows2", [(RB, a["rows2"])], fence)

            def rb(name, hi=S):
                return RB[0:hi, ROW2.index(name), :]

            def load_ent(l, *after):
                return [load(f"ent{l}", [(W[:, 0:4, :], a["entwT"][l]), (W[:, 4:8, :], a["entpw"][l])], *after)]

            bcomb = []
            le = load_ent(0, fence)
            for l in range(2):
                wT = W[:, 0:4, :].rearrange("p a (k n) -> p (a k) n", k=4)
                pw = W[:, 4:8, :].rearrange("p a (k n) -> p (a k) n", k=4)
                eb = dve(lambda e, l=l: e.tensor_copy(
                    EB, CL("entb")[:, 16 * l:16 * l + 16].unsqueeze(2).to_broadcast([128, 16, S])),
                    bcomb, free[4])
                for m in range(4):
                    for k in range(16):
                        o = mm(PS[:, m, :], wT[:, k, m * 128:(m + 1) * 128], pw[:, k, :], k == 0, k == 15, le,
                               free[m], fence)
                    oe = evac(m, W[:, 8 + l, m * 512:(m + 1) * 512], PS[:, m, :], o, f_act, f_dve)
                    free[m] = oe
                for k in range(16):
                    o = mm(PS[0:S, 4, :], EB[:, k, :], pw[:, k, :], k == 0, k == 15, eb, free[4])
                d = dve(lambda e, l=l: e.tensor_tensor(rb(f"entpb{l}"), PS[0:S, 4, :], rb(f"entpb{l}"), ALU.add),
                        o, l_rb)
                free[4] = d
                bcomb = [d]
                wc_done = [oe, d, act.ops[-1], dve.ops[-1]] if l == 1 else None
                if l == 0:
                    le = load_ent(1, o)
            after_comb = o
            l_ap = load("ampph", [(W[:, 0:2, :], a["ampph"])], after_comb)
            l_pw = [load(f"path{l}", [(W[:, 2 + 2 * l:4 + 2 * l, :], a["pathw"][l])], after_comb) for l in range(2)]
            AMP = W[:, 6:8, :].rearrange("p a (b n) -> p (a b) n", n=D)

            def cos_sin(v, s_, c_, scale, ops, w=None):
                hi = v.shape[0]
                o1 = act(lambda e: e.activation(s_, v, ACT.Sin, scale=scale / 2), ops, w, f_act)
                o2 = act(lambda e: e.activation(c_, v, ACT.Abs), ops, w, f_act)
                o3 = act(lambda e: e.activation(c_, c_, ACT.Sin, bias=C("halfpi", 0, hi), scale=-scale / 2), o2)
                o4 = dve(lambda e: e.tensor_tensor(c_, c_, s_, ALU.subtract), o3, o1)
                o5 = dve(lambda e: e.tensor_tensor(c_, c_, s_, ALU.mult), o4)
                return dve(lambda e: e.tensor_scalar(v, c_, 2.0, 1.0, ALU.mult, ALU.add), o5)

            PH = RB[:, ROW2.index("ph00"):ROW2.index("ph00") + 4, :]
            G4 = H[:, 0:4, :]
            magic = 12582912.0
            c1 = 6.28125
            c2 = float(2 * np.pi - 6.28125)
            d = dve(lambda e: e.tensor_scalar(G4, PH, float(1 / (2 * np.pi)), magic, ALU.mult, ALU.add), l_rb, f_dve)
            d = dve(lambda e: e.tensor_scalar(G4, G4, -magic, None, ALU.add), d)
            d = dve(lambda e: e.scalar_tensor_tensor(PH, G4, -c1, PH, ALU.mult, ALU.add), d)
            d = dve(lambda e: e.scalar_tensor_tensor(PH, G4, -c2, PH, ALU.mult, ALU.add), d)
            mod = cos_sin(PH, G4, H[:, 4:8, :], 1.0, d)
            wp_done = []
            for l in range(2):
                p0 = W[:, 2 + 2 * l, :].rearrange("p (k n) -> p k n", k=4)
                p1 = W[:, 3 + 2 * l, :].rearrange("p (k n) -> p k n", k=4)
                m0 = rb(f"ph{l}0", 128).unsqueeze(1).to_broadcast([128, 4, D])
                m1_ = rb(f"ph{l}1", 128).unsqueeze(1).to_broadcast([128, 4, D])
                d0 = dve(lambda e, p0=p0, m0=m0: e.tensor_tensor(p0, p0, m0, ALU.mult), mod, l_pw[l])
                q0 = pool(lambda e, p1=p1, m1_=m1_: e.tensor_tensor(p1, p1, m1_, ALU.mult), mod, l_pw[l])
                wp = dve(lambda e, p0=p0, p1=p1: e.tensor_tensor(p0, p0, p1, ALU.add), d0, q0)
                d0 = pool(lambda e, l=l: e.tensor_tensor(rb(f"pb{l}0"), rb(f"pb{l}0"), rb(f"ph{l}0"), ALU.mult), mod)
                d1 = pool(lambda e, l=l: e.tensor_tensor(rb(f"pb{l}1"), rb(f"pb{l}1"), rb(f"ph{l}1"), ALU.mult), mod)
                d2 = pool(lambda e, l=l: e.tensor_tensor(rb(f"pb{l}0"), rb(f"pb{l}0"), rb(f"pb{l}1"), ALU.add),
                          d0, d1)
                wp_done.append([wp, d2])

            hr = [None] * NBATCH
            Wa = W[:, 0, :].rearrange("p (k n) -> p k n", k=4)
            Wp_ = W[:, 1, :].rearrange("p (k n) -> p k n", k=4)
            for b in range(NBATCH):
                norm_t(b, [x_ready[b]], 5)
                ba, bp = 2 * (b % 2), 2 * (b % 2) + 1
                for bank, w in ((ba, Wa), (bp, Wp_)):
                    for k in range(4):
                        o = mm(PS[0:S, bank, :], xT[:, k, b * S:(b + 1) * S], w[:, k, :], k == 0, k == 3,
                               xT_ready[b], l_ap, free[bank])
                    if bank == ba:
                        oa = o
                xT_free[b] = o
                d1 = dve(lambda e, b=b, ba=ba: e.tensor_tensor(AMP[0:S, b, :], PS[0:S, ba, :], rb("ampb"), ALU.add),
                         oa, after_comb)
                free[ba] = d1
                d2 = dve(lambda e, b=b, bp=bp: e.tensor_tensor(H[0:S, b, :], PS[0:S, bp, :], rb("phb"), ALU.add),
                         o, mod)
                free[bp] = d2
                a1 = act(lambda e, b=b: e.activation(AMP[0:S, b, :], AMP[0:S, b, :], ACT.Sigmoid), d1)
                a2 = act(lambda e, b=b: e.activation(H[0:S, b, :], H[0:S, b, :], ACT.Tanh), d2)
                hr[b] = [a1, a2]
            cs_free = None
            for b in range(NBATCH):
                hb = H[0:S, b, :]
                a3 = cos_sin(hb, TS[0:S, 0, :], TS[0:S, 1, :], float(np.pi), hr[b], cs_free)
                cs_free = a3
                hr[b] = pool(lambda e, b=b: e.tensor_tensor(H[0:S, b, :], H[0:S, b, :], AMP[0:S, b, :], ALU.mult),
                             a3, hr[b])
            yn = [0]
            y_free = [None, None, None]
            for l in range(2):
                for part in range(2):
                    w = W[:, 8 + l, :] if part == 0 else W[:, 2 + 2 * l, :]
                    w = w.rearrange("p (k n) -> p k n", k=4)
                    wd = wc_done if part == 0 else wp_done[l]
                    bias = f"entpb{l}" if part == 0 else f"pb{l}0"
                    gn, bn = (f"g3{l}", f"b3{l}") if part == 0 else (f"g4{l}", f"b4{l}")
                    for b in range(NBATCH):
                        hb = H[0:S, b, :]
                        put_t(b, hb, [hr[b]], 4 + b % 2)
                        z = yn[0] % 3
                        yn[0] += 1
                        r1 = pool(lambda e, z=z, hb=hb, bias=bias: e.tensor_tensor(TS[0:S, z, :], hb, rb(bias),
                                                                                  ALU.add),
                                  hr[b], y_free[z], cs_free, bcomb, wp_done[l])
                        bank = b % 4
                        for k in range(4):
                            o = mm(PS[0:S, bank, :], xT[:, k, b * S:(b + 1) * S], w[:, k, :], k == 0, k == 3,
                                   xT_ready[b], wd, free[bank])
                        xT_free[b] = o
                        r2 = dve(lambda e, z=z, bank=bank: e.tensor_tensor(TS[0:S, z, :], PS[0:S, bank, :],
                                                                           TS[0:S, z, :], ALU.add), o, r1)
                        free[bank] = r2
                        o5, _, _ = norm(b, [r2], TS[0:S, z, :], TS[0:S, z, :])
                        r3 = dve(lambda e, z=z, gn=gn: e.tensor_tensor(TS[0:S, z, :], TS[0:S, z, :], rb(gn),
                                                                       ALU.mult), o5, l_rb)
                        r4 = pool(lambda e, z=z, hb=hb, bn=bn: e.tensor_tensor(hb, TS[0:S, z, :], rb(bn), ALU.add),
                                  r3, xT_ready[b])
                        y_free[z] = r4
                        hr[b] = r4
            for b in range(NBATCH):
                x_ready[b] = dve(lambda e, b=b: e.tensor_tensor(x[0:S, b, :], x[0:S, b, :], H[0:S, b, :], ALU.add),
                                 hr[b], x_ready[b])

        store = Load(sp, sem("d_out"), [
            (lambda e, u=u: e.dma_start(out[:, u * UB:(u + 1) * UB, :], x[0:S, u * UB:(u + 1) * UB, :]))
            for u in range(NU)], [x_ready])

        count(queues)
        block = ctx.enter_context(nc.Block())

        @block.sync
        def _(e):
            play(e, sp)
            e.wait_ge(store.sem, store.value)

        @block.tensor
        def _(e):
            play(e, pe)

        @block.vector
        def _(e):
            play(e, dve)

        @block.scalar
        def _(e):
            play(e, act)

        @block.gpsimd
        def _(e):
            play(e, pool)


def kmaj(w):
    k, n = w.shape
    return w.reshape(k // 128, 128, n).transpose(1, 0, 2)


def slots(w):
    return np.ascontiguousarray(w.reshape(128, -1, 2048))


def layout(i):
    o = {"consts": CONSTS}
    o["x"] = i["x"].transpose(1, 0, 2)
    q = kmaj(i["L0_attn_Wq"].reshape(512, 2048)).reshape(128, 4, 2, 4, 4, 32, 2)
    q = q.transpose(0, 2, 4, 1, 6, 3, 5)
    o["w0q"] = slots(q)
    k = kmaj(i["L0_attn_Wk"].reshape(512, 512)).reshape(128, 4, 2, 4, 32, 2).transpose(0, 1, 2, 5, 3, 4)
    v = kmaj(i["L0_attn_Wv"].reshape(512, 512))
    o["w0kv"] = np.ascontiguousarray(np.stack([k.reshape(128, 2048), v.reshape(128, 2048)], 1))
    o["w0o"] = slots(kmaj(i["L0_attn_Wo"].reshape(2048, 512)))
    o["wx"] = np.stack([kmaj(i["L0_xattn_" + w]).reshape(128, 2048) for w in ("Wq", "Wk", "Wv", "Wo")], 1)
    o["mask"] = i["mask_Bx1xSxS_fk0"][:, 0].transpose(1, 0, 2)
    o["ctxT"] = i["ctx_2048"].transpose(0, 2, 1).reshape(8, 4, 128, SC).transpose(0, 2, 1, 3)
    g = i["L0_ffn_gating_einsum"].transpose(0, 3, 1, 2).reshape(8, 4, 128, 1024).transpose(0, 2, 1, 3)
    ln = i["L0_ffn_linear"].reshape(8, 4, 128, 512).transpose(0, 2, 1, 3)
    o["we"] = np.concatenate([g.reshape(8, 128, 4096), ln.reshape(8, 128, 2048)], 2).reshape(8, 128, 3, 2048)
    q = kmaj(i["L1_attn_Wq"].T).reshape(128, 4, 2, 2, 4, 2, 64).transpose(0, 2, 4, 1, 5, 3, 6)
    o["w1q"] = slots(q)
    o["w1o"] = slots(kmaj(i["L1_attn_Wo"].T))
    ku = i["L1_attn_Wk_up"].reshape(2, 2, 2, 64, 64).transpose(4, 0, 2, 1, 3).reshape(64, 512)
    small = np.zeros((128, 1664), np.float32)
    small[:, 0:256] = kmaj(i["L1_attn_Wk_down"].T).reshape(128, 256)
    small[:, 256:640] = kmaj(i["L1_attn_Wv_down"].T).reshape(128, 384)
    small[0:64, 640:1152] = ku
    small[0:96, 1152:1664] = i["L1_attn_Wv_up"].T
    o["w1s"] = small
    o["ctx"] = i["ctx_2048"].reshape(8, 3, KC, D).transpose(0, 2, 1, 3)
    o["cmask"] = np.broadcast_to(i["mask_BxS2_bk0"].reshape(1, 8 * SC), (S, 8 * SC))
    o["entwT"] = np.stack([kmaj(w.T).reshape(128, 4, 2048) for w in i["L1_ffn_ent_w"]])
    o["entpw"] = np.stack([kmaj(w).reshape(128, 4, 2048) for w in i["L1_ffn_ent_pw"]])
    o["ampph"] = np.stack([kmaj(i[n]).reshape(128, 2048) for n in ("L1_ffn_amp_w", "L1_ffn_ph_w")], 1)
    o["pathw"] = np.stack([np.stack([kmaj(w).reshape(128, 2048) for w in wl], 1) for wl in i["L1_ffn_path_w"]])
    r2 = [i["L1_ffn_amp_b"], i["L1_ffn_ph_b"], *i["L1_ffn_ent_pb"], *i["L1_ffn_path_b"].reshape(4, 512),
          *i["L1_ffn_phase"].reshape(4, 512)]
    for n in "34":
        for l in range(2):
            r2 += [i[f"L1_ffn_ln{n}_g"][l], i[f"L1_ffn_ln{n}_b"][l]]
    o["rows2"] = np.broadcast_to(np.stack(r2), (128, 20, D))
    cols = [
        i["L0_attn_bq"].reshape(2, 4, 4, 32, 2).transpose(1, 3, 0, 2, 4).reshape(128, 16),
        i["L0_attn_bk"].reshape(2, 4, 32, 2).transpose(1, 2, 0, 3).reshape(128, 4),
        i["L0_ffn_router_scale"].reshape(4, 128).T,
        i["L1_attn_k_anchor"].reshape(2, 2, 2, 64).transpose(1, 3, 0, 2).reshape(128, 4),
        kmaj(i["L0_ffn_router_logits"]).reshape(128, 32),
        i["L1_ffn_ent_b"].reshape(2, 16, 128).transpose(2, 0, 1).reshape(128, 32)]
    o["cols"] = np.concatenate(cols, 1)
    rows = [i["L0_attn_bv"].ravel(), i["L0_attn_bo"], i["L0_attn_sinks"], i["L0_xattn_gate"].ravel(),
            i["L0_ffn_per_expert_scale"], i["L1_attn_v_anchor"]]
    o["rows"] = np.broadcast_to(np.concatenate(rows), (128, NROW))
    return {k: np.ascontiguousarray(v) for k, v in o.items()}


def kernel(**inputs):
    import concourse.bacc as bacc
    from concourse.bass_utils import run_bass_kernel_spmd as run

    arrays = layout({k: np.asarray(v) for k, v in inputs.items()})
    nc = bacc.Bacc("TRN2", target_bir_lowering=False, num_devices=1)
    aps = {k: nc.dram_tensor("in_" + k, v.shape, mybir.dt.from_np(v.dtype), kind="ExternalInput").ap()
           for k, v in arrays.items()}
    out = nc.dram_tensor("out", (S, NBATCH, D), F32, kind="ExternalOutput").ap()
    program(nc, aps, out)
    r = run(nc, [{"in_" + k: v for k, v in arrays.items()}], core_ids=[0])
    return np.ascontiguousarray(r.results[0]["out"].transpose(1, 0, 2))
```

```python
from contextlib import ExitStack

import numpy as np
import concourse.bass as bass
from concourse import mybir

F32 = mybir.dt.float32
U8 = mybir.dt.uint8
ALU = mybir.AluOpType
ACT = mybir.ActivationFunctionType
AX = mybir.AxisListType

NBATCH = 8
S = 112
D = 512
SC = 375
KC = 125
UB = 2
NU = NBATCH // UB
UT = UB * S
FMIN = float(np.finfo(np.float32).min)


def size(ap):
    n = 1
    for d in ap.shape[1:]:
        n *= d
    return n


class Price:

    def __init__(self, fixed, each):
        self.fixed, self.each = fixed, each

    def of(self, n):
        return self.fixed + n * self.each

    def matmul(self, o, l, r, start=None, stop=None):
        return max(size(o), size(l)) * 4 / 2300.0

    def transpose(self, o, i, ident):
        return size(o) * 2 / 2300.0

    def activation(self, o, i, f, **k):
        return self.of(size(i))

    def memset(self, o, v):
        return self.of(size(o))

    def tensor_copy(self, o, i):
        return self.of(size(o))

    def tensor_reduce(self, o, i, *_, **k):
        return self.of(size(i))

    def tensor_scalar(self, o, i, *_, **k):
        return self.of(size(i))

    def tensor_tensor(self, o, i, j, *_, **k):
        return self.of(size(o))

    def scalar_tensor_tensor(self, o, i, s, j, *_, **k):
        return self.of(size(o))

    def reciprocal(self, o, i):
        return self.of(size(i))

    def bn_stats(self, o, i):
        return self.of(size(i))

    def bn_aggr(self, o, i):
        return self.of(size(i))

    def dma_start(self, o, i):
        return 0.0


PRICES = {"pe": Price(0, 0), "dve": Price(0.07, 0.00105), "act": Price(0.2, 0.00075), "pool": Price(0.1, 0.0022),
          "sp": Price(0, 0)}
HOP = {"pe": 0.25, "dve": 0.15, "act": 0.25, "pool": 0.15, "sp": 0.2}


class Op:

    def __init__(self, queue, issue, after):
        self.queue, self.issue, self.after = queue, issue, after
        self.used = False
        self.value = 0
        self.sem = None


class Queue:

    def __init__(self, name, sem):
        self.name, self.sem, self.ops = name, sem, []
        self.time = 0.0

    def __call__(self, issue, *after):
        op = Op(self, issue, flat(after))
        op.sem = self.sem
        self.ops.append(op)
        self.time = max([self.time] + [when(a) for a in op.after]) + issue(PRICES[self.name])
        op.end = self.time + HOP[self.name]
        return op


class Load:

    def __init__(self, queue, sem, issues, after, mb=0.0):
        self.queue, self.sem, self.used = queue, sem, True
        self.value = 16 * len(issues)
        self.end = max([LOADS[0]] + [when(a) for a in flat(after)]) + 2.0 + mb * 5.5
        LOADS[0] = self.end - 2.0
        for n, issue in enumerate(issues):
            op = Op(queue, issue, flat(after) if n == 0 else [])
            op.sem, op.dma = sem, True
            queue.ops.append(op)


LOADS = [0.0]


def when(a):
    if a is None:
        return 0.0
    if isinstance(a, (list, tuple)):
        return max([0.0] + [when(b) for b in a])
    return a.end


def flat(after):
    out = []
    for a in after:
        if a is None:
            continue
        if isinstance(a, (list, tuple)):
            out += flat(a)
        else:
            out.append(a)
    return out


def count(queues):
    for q in queues:
        for op in q.ops:
            for a in op.after:
                a.used = True
    for q in queues:
        n = 0
        for op in q.ops:
            if op.sem is q.sem and op.used:
                n += 1
                op.value = n


def play(engine, queue):
    seen = {}
    for op in queue.ops:
        need = {}
        for a in op.after:
            key = a.sem.name
            if key not in need or need[key][1] < a.value:
                need[key] = (a.sem, a.value)
        for key, (sem, value) in need.items():
            if seen.get(key, 0) < value:
                engine.wait_ge(sem, value)
                seen[key] = value
        ins = op.issue(engine)
        if op.sem is not queue.sem:
            ins.then_inc(op.sem, 16)
        elif op.used:
            ins.then_inc(op.sem, 1)


CST = {}


def constants():
    parts = []

    def add(name, a):
        at = sum(p.shape[1] for p in parts)
        CST[name] = (at, a.shape[1])
        parts.append(a.astype(np.float32))

    f = np.float32
    p = np.arange(128)
    add("ident", np.eye(128))
    rot = np.zeros((128, 128), f)
    for j in range(128):
        if j % 16 < 8:
            rot[j + 8, j] = -1.0
        else:
            rot[j - 8, j] = 1.0
    add("rot", rot)
    t = np.arange(S, dtype=f)
    inv = f(1.0) / np.power(f(150000.0), np.arange(32, dtype=f) * f(2.0) / f(64))
    ang = (t[:, None] * inv[None, :]).astype(f).T[p % 32]
    c0, s0 = np.cos(ang), np.sin(ang)
    add("q0cos", c0 * f(0.125))
    add("q0sin", s0 * f(0.125))
    add("k0cos", c0)
    add("k0sin", s0)
    inv = f(1.0) / f(10000.0) ** (np.arange(0, 16, 2, dtype=f) / f(16))
    ang = np.outer(t, inv).astype(f).T[p % 8]
    c1, s1 = np.cos(ang), np.sin(ang)
    add("qxcos", c1 * f(0.25))
    add("qxsin", s1 * f(0.25))
    add("kxcos", c1)
    add("kxsin", s1)
    inv = f(1.0) / np.power(f(10000.0), np.arange(0, 128, 2, dtype=f) / f(128))
    ang = (t[:, None] * inv[None, :]).astype(f).T[p % 64]
    add("l1cos", np.cos(ang))
    add("l1sin", np.sin(ang))
    add("heads", p[:, None] // 16 == np.arange(8)[None, :])
    k = np.arange(S)
    causal = np.where(k[None, :] <= k[:, None], 0.0, -1e9)
    add("causal", np.concatenate([causal, np.zeros((16, S))], 0))
    add("halfpi", np.full((128, 1), np.pi / 2))
    strict = np.zeros((128, S))
    strict[:S] = (k[:, None] < k[None, :])
    add("strict", strict)
    return np.ascontiguousarray(np.concatenate(parts, 1))


CONSTS = constants()
NCST = CONSTS.shape[1]
COLS = {"bq": (0, 16), "bk": (16, 4), "rscale": (20, 4), "kanch": (24, 4), "wr": (28, 32), "entb": (60, 32)}
NCOL = 92
ROWS = {"bv": (0, 512), "bo": (512, 512), "sinks": (1024, 32), "gate": (1056, 32), "pes": (1088, 8),
        "vanch": (1096, 512)}
NROW = 1608
ROW2 = ["ampb", "phb", "entpb0", "entpb1", "pb00", "pb01", "pb10", "pb11", "ph00", "ph01", "ph10", "ph11",
        "g30", "b30", "g31", "b31", "g40", "b40", "g41", "b41"]
WSLOTS = 10
LEAD = 8000
SHARE0 = 0.6
SHAREX = 0.75
SHAREL = 0.5
RSIZE = 18816


def program(nc, a, out, stop=9):
    with ExitStack() as ctx:
        def sb(name, shape, dt=F32):
            return ctx.enter_context(nc.sbuf_tensor(name, shape, dt))

        def sem(name):
            return ctx.enter_context(nc.semaphore(name))

        PS = ctx.enter_context(nc.psum_tensor("PS", [128, 8, 512], F32))
        x = sb("x", [128, NBATCH, D])
        xT = sb("xT", [128, 4, NBATCH * S])
        W = sb("W", [128, WSLOTS, 2048])
        R = sb("R", [128, RSIZE])
        cst = sb("cst", [128, NCST])
        col = sb("col", [128, NCOL])
        row = sb("row", [128, NROW])
        st = sb("st", [128, NBATCH, 6])
        mv = sb("mv", [128, NBATCH, 2])
        rstd = sb("rstd", [128, NBATCH])
        veps = sb("veps", [128, NBATCH])
        mhalf = sb("mhalf", [128, 16])
        xn = sb("xn", [128, 2, D])

        pe = Queue("pe", sem("s_pe"))
        dve = Queue("dve", sem("s_dve"))
        act = Queue("act", sem("s_act"))
        pool = Queue("pool", sem("s_pool"))
        sp = Queue("sp", sem("s_sp"))
        queues = [pe, dve, act, pool, sp]

        def load(name, pairs, *after, q=sp):
            return Load(q, sem("d_" + name), [
                (lambda e, d=d, s=s: e.dma_start(d, s)) for d, s in pairs], after,
                sum(d.shape[0] * size(d) * 4e-6 for d, s in pairs))

        def last():
            return [q.ops[-1] for q in (pe, dve, act, pool) if q.ops]

        def C(name, lo=0, hi=128):
            at, n = CST[name]
            return cst[lo:hi, at:at + n]

        def CL(name):
            at, n = COLS[name]
            return col[:, at:at + n]

        def RW(name, hi=S):
            at, n = ROWS[name]
            return row[0:hi, at:at + n]

        work = [0]

        def mm(o, l, r, start, stop_, *after):
            work[0] += 4 * size(o)
            return pe(lambda e: e.matmul(o, l, r, start=start, stop=stop_), *after)

        def tr(o, i, n, *after):
            work[0] += 2 * size(o)
            return pe(lambda e: e.transpose(o, i, C("ident", 0, n)[:, 0:n]), *after)

        free = [None] * 8

        def pick(banks):
            return min(banks, key=lambda n: when(free[n]))

        LOADS[0] = 0.0

        l_c = load("cst", [(cst[:, :], a["consts"]), (col[:, :], a["cols"]), (row[:, :], a["rows"])])
        l_x = [load(f"x{u}", [(x[0:S, u * UB:(u + 1) * UB, :], a["x"][:, u * UB:(u + 1) * UB, :])])
               for u in range(NU)]
        c_mh = pool(lambda e: e.memset(mhalf[:, :], -0.5))

        xn_free = [None, None]
        xT_ready = [None] * NBATCH
        read_x = [None] * NBATCH
        ncount = [0]

        def norm(b, deps, src=None, dst=None):
            src = x[0:S, b, :] if src is None else src
            k = ncount[0] % 2
            ncount[0] += 1
            dst_, w = (xn[0:S, k, :], xn_free[k]) if dst is None else (dst, None)
            o1 = dve(lambda e: e.bn_stats(st[0:S, b, :], src), deps)
            o2 = dve(lambda e: e.bn_aggr(mv[0:S, b, :], st[0:S, b, :]), o1)
            o3 = dve(lambda e: e.tensor_scalar(veps[0:S, b:b + 1], mv[0:S, b, 1:2], 1e-5, None, ALU.add), o2)
            o4 = pool(lambda e: e.tensor_tensor(rstd[0:S, b:b + 1], veps[0:S, b:b + 1], mhalf[0:S, 0:1],
                                                ALU.pow), o3, c_mh)
            o5 = dve(lambda e: e.tensor_scalar(dst_, src, mv[0:S, b, 0:1], rstd[0:S, b:b + 1],
                                               ALU.subtract, ALU.mult), o4, w)
            return o5, k, dst_

        def norm_t(b, deps, bank, src=None):
            o5, k, v = norm(b, deps, src)
            read_x[b] = o5
            return put_t(b, v, [o5], bank, k)

        def put_t(b, v, deps, bank, k=None, eng=None):
            for c in range(4):
                t = tr(PS[:, bank, c * S:(c + 1) * S], v[:, c * 128:(c + 1) * 128], S, deps, free[bank], l_c)
            if k is not None:
                xn_free[k] = t
            e_ = act if eng is None else eng
            src_ = PS[:, bank, 0:4 * S].rearrange("p (c n) -> p c n", c=4)
            dst_ = xT[:, :, b * S:(b + 1) * S]
            if e_ is act:
                o = act(lambda e: e.activation(dst_, src_, ACT.Copy), t, xT_free[b])
            else:
                o = dve(lambda e: e.tensor_copy(dst_, src_), t, xT_free[b])
            free[bank] = o
            xT_ready[b] = o
            return o

        xT_free = [None] * NBATCH
        x_ready = [l_x[b // UB] for b in range(NBATCH)]

        def wload(name, slot, src, n, *after):
            return load(name, [(W[:, slot:slot + n, :], src)], *after)

        l_kv = wload("w0kv", 4, a["w0kv"], 2)
        l_q = [wload(f"w0q{n}", n, a["w0q"][:, n:n + 1, :], 1) for n in range(4)]
        l_o = wload("w0o", 6, a["w0o"], 4)
        Wq = W[:, 0:4, :].rearrange("p a (c k n) -> p (a c) k n", c=2, k=4)
        Wk = W[:, 4, :].rearrange("p (k n) -> p k n", k=4)
        Wv = W[:, 5, :].rearrange("p (k n) -> p k n", k=4)
        Wo = W[:, 6:10, :].rearrange("p a (t n) -> p (a t) n", n=D)

        at = [0]

        def carve(n):
            o = at[0]
            at[0] += n
            assert at[0] <= RSIZE, at[0]
            return R[:, o:o + n]

        Q = carve(2 * 16 * UT).rearrange("p (z c a n) -> p z c a n", z=2, c=8, a=2)
        K = carve(2 * 4 * UT).rearrange("p (z c a n) -> p z c a n", z=2, c=2, a=2)
        V = carve(2 * UB * 520).rearrange("p (z b h n) -> p z b h n", z=2, b=UB, h=8)
        T4 = carve(4 * UT).rearrange("p (k n) -> p k n", k=4)
        SS = carve(2 * 1792).rearrange("p (z n) -> p z n", z=2)
        PT = carve(3 * 448).rearrange("p (z n) -> p z n", z=3)
        O = carve(1024)
        OT = carve(8 * S).rearrange("p (t n) -> p t n", t=8)
        small = sb("small", [128, 2, 5, 32])
        rec4 = sb("rec4", [128, 16])
        any0 = [4, 5, 6, 7]
        ones_v = pool(lambda e: e.memset(V[0:S, :, :, :, 64:65], 1.0))

        def bc(t, n):
            return t.unsqueeze(1).to_broadcast([128, n, S])

        t4_free = [None]
        t4_buf = [T4]
        q_free = [None, None]

        def rope(bank, ba, bb, cos, sin, da, db, w_out, mmop):
            T4 = t4_buf[0]
            A = PS[:, bank, 0:UT].rearrange("p (b n) -> p b n", b=UB)
            B = PS[:, bank, UT:2 * UT].rearrange("p (b n) -> p b n", b=UB)

            def half(k, src, bias, tab, *w):
                o = T4[:, k, :].rearrange("p (b n) -> p b n", b=UB)
                return dve(lambda e: e.scalar_tensor_tensor(o, src, bias, bc(tab, UB), ALU.add, ALU.mult), *w)

            half(0, A, ba, cos, mmop, t4_free[0], l_c)
            o1 = half(1, B, bb, sin)
            half(2, B, bb, cos)
            o3 = half(3, A, ba, sin)
            free[bank] = o3
            p1 = pool(lambda e: e.tensor_tensor(da, T4[:, 0, :], T4[:, 1, :], ALU.subtract), o1, w_out)
            p2 = pool(lambda e: e.tensor_tensor(db, T4[:, 2, :], T4[:, 3, :], ALU.add), o3)
            t4_free[0] = p2
            return p2

        def project0(u, banks):
            tok = slice(u * UT, (u + 1) * UT)
            xr = [xT_ready[u * UB + i] for i in range(UB)]
            kr, vr, qr = [None] * 2, [None] * UB, [None] * 8
            n = 0
            for c in range(2):
                bank = pick(banks)
                for ab in range(2):
                    for k in range(4):
                        lo = (c * 2 + ab) * 128
                        o = mm(PS[:, bank, ab * UT:(ab + 1) * UT], Wk[:, k, lo:lo + 128], xT[:, k, tok],
                               k == 0, k == 3, xr, l_kv, free[bank])
                bk = CL("bk")
                kr[c] = rope(bank, bk[:, 2 * c:2 * c + 1], bk[:, 2 * c + 1:2 * c + 2], C("k0cos"), C("k0sin"),
                             K[:, u % 2, c, 0, :], K[:, u % 2, c, 1, :], q_free[u % 2], o)
                yield
            for i in range(UB):
                bank = pick(banks)
                b = u * UB + i
                for k in range(4):
                    o = mm(PS[0:S, bank, :], xT[:, k, b * S:(b + 1) * S], Wv[:, k, :], k == 0, k == 3,
                           xr, free[bank])
                vr[i] = dve(lambda e, bank=bank, i=i: e.tensor_tensor(
                    V[0:S, u % 2, i, :, 0:64], PS[0:S, bank, :].rearrange("p (h n) -> p h n", h=8),
                    RW("bv").rearrange("p (h n) -> p h n", h=8), ALU.add), o, q_free[u % 2])
                free[bank] = vr[i]
                yield
            for c in range(8):
                bank = pick(banks)
                for ab in range(2):
                    for k in range(4):
                        o = mm(PS[:, bank, ab * UT:(ab + 1) * UT], Wq[:, c, k, ab * 128:ab * 128 + 128],
                               xT[:, k, tok], k == 0, k == 3, xr, l_q[c // 2], free[bank])
                bq = CL("bq")
                qr[c] = rope(bank, bq[:, 2 * c:2 * c + 1], bq[:, 2 * c + 1:2 * c + 2], C("q0cos"), C("q0sin"),
                             Q[:, u % 2, c, 0, :], Q[:, u % 2, c, 1, :], q_free[u % 2], o)
                yield
            done0[u] = (kr, vr, qr)
            for i in range(UB):
                xT_free[u * UB + i] = o
            return

        done0 = [None] * NU
        ss_free = [None, None]
        pt_free = [None] * 3
        o_free, ot_free = [None], [None]
        pt_n = [0]

        def evac(k, dst, src, *w):
            if k % 2 == 0:
                return act(lambda e: e.activation(dst, src, ACT.Copy), *w)
            return dve(lambda e: e.tensor_copy(dst, src), *w)

        def attend0(u):
            kr, vr, qr = done0[u]
            todo = [(i, g) for i in range(UB) for g in range(2)]
            state = {}

            def scores(n):
                i, g = todo[n]
                tk = slice(i * S, (i + 1) * S)
                z = n % 2
                for j in range(4):
                    for ab in range(2):
                        for r in range(4):
                            ro = slice(32 * r, 32 * r + 32)
                            o = mm(PS[0:S, r, j * S:(j + 1) * S], Q[ro, u % 2, 4 * g + j, ab, tk],
                                   K[ro, u % 2, g, ab, tk], ab == 0, ab == 1, qr[4 * g + j], kr[g], free[r])
                    yield
                sm = small[0:S, z]
                pss = PS[0:S, 0:4, 0:448]
                o1 = dve(lambda e: e.tensor_reduce(sm[:, 0, 0:16], pss.rearrange("p r (j n) -> p r j n", j=4),
                                                   AX.X, ALU.max), o)
                sk = RW("sinks")[:, 16 * g:16 * g + 16]
                o2 = dve(lambda e: e.tensor_tensor(sm[:, 1, 0:16], sm[:, 0, 0:16], sk, ALU.max), o1)
                o3 = dve(lambda e: e.tensor_tensor(
                    SS[0:S, z, :].rearrange("p (r j n) -> p r j n", r=4, j=4),
                    pss.rearrange("p r (j n) -> p r j n", j=4),
                    sm[:, 1, 0:16].rearrange("p (r j) -> p r j", r=4).unsqueeze(3).to_broadcast([S, 4, 4, S]),
                    ALU.subtract), o2, ss_free[z])
                for r in range(4):
                    free[r] = o3
                o4 = dve(lambda e: e.tensor_tensor(sm[:, 2, 0:16], sk, sm[:, 1, 0:16], ALU.subtract), o2)
                o5 = act(lambda e: e.activation(SS[0:S, z, :], SS[0:S, z, :], ACT.Exp), o3)
                o6 = act(lambda e: e.activation(sm[:, 3, 0:16], sm[:, 2, 0:16], ACT.Exp), o4)
                state[n] = (o5, o6)

            def values(n):
                i, g = todo[n]
                b = u * UB + i
                z = n % 2
                o5, o6 = state[n]
                sm = small[0:S, z]
                def pv(q, oe, slot):
                    bank = pick(any0)
                    for h in range(4):
                        kvh = 4 * g + q
                        o = mm(PS[0:S, bank, h * 65:h * 65 + 65], PT[0:S, slot, h * S:(h + 1) * S],
                               V[0:S, u % 2, i, kvh, :], True, True, oe, vr[i], ones_v, free[bank])
                    pt_free[slot] = o
                    pv_ = PS[0:S, bank, 0:260].rearrange("p (h n) -> p h n", h=4)
                    rec = rec4[0:S, 4 * q:4 * q + 4]
                    d1 = dve(lambda e: e.tensor_tensor(rec, pv_[:, :, 64], sm[:, 3, 4 * q:4 * q + 4],
                                                       ALU.add), o, o6)
                    d2 = dve(lambda e: e.reciprocal(rec, rec), d1)
                    d3 = dve(lambda e: e.tensor_tensor(
                        O[0:S, q * 256:(q + 1) * 256].rearrange("p (h n) -> p h n", h=4), pv_[:, :, 0:64],
                        rec.unsqueeze(2).to_broadcast([S, 4, 64]), ALU.mult), d2, o_free[0])
                    free[bank] = d3
                    return o, d3

                def probs(q):
                    bank = pick(any0)
                    slot = pt_n[0] % 3
                    pt_n[0] += 1
                    for h in range(4):
                        at_ = (q * 4 + h) * S
                        t = tr(PS[0:S, bank, h * S:(h + 1) * S], SS[0:S, z, at_:at_ + S], S, o5, free[bank])
                    oe = evac(q, PT[0:S, slot, :], PS[0:S, bank, 0:448], t, pt_free[slot])
                    free[bank] = oe
                    return t, oe, slot

                def outs(half, d3):
                    bank = pick(any0)
                    for c in range(4):
                        cc = half * 4 + c
                        t = tr(PS[:, bank, c * S:(c + 1) * S], O[0:S, cc * 128:(cc + 1) * 128], S, d3, free[bank])
                    oe = evac(half, OT[:, half * 4:half * 4 + 4, :],
                              PS[:, bank, 0:448].rearrange("p (c n) -> p c n", c=4), t, ot_free[0])
                    free[bank] = oe
                    return t, oe

                _, e0, s0 = probs(0)
                _, e1, s1 = probs(1)
                yield [e0, pt_free[(pt_n[0]) % 3]]
                _, e2, s2 = probs(2)
                pv(0, e0, s0)
                yield [e1]
                ss_free[z], e3, s3 = probs(3)
                _, d3 = pv(1, e1, s1)
                yield e2
                pv(2, e2, s2)
                yield [e3, d3]
                lastpv, d4 = pv(3, e3, s3)
                _, oa = outs(0, d3)
                yield [d4]
                t, ob = outs(1, d4)
                o_free[0] = t
                yield [oa, ob]
                bank = pick(any0)
                for c in range(8):
                    o = mm(PS[0:S, bank, :], OT[:, c, :], Wo[:, g * 8 + c, :], c == 0, c == 7, oa, ob, l_o,
                           free[bank])
                ot_free[0] = o
                xa = dve(lambda e: e.tensor_tensor(x[0:S, b, :], x[0:S, b, :], PS[0:S, bank, :], ALU.add),
                         o, x_ready[b])
                free[bank] = xa
                x_ready[b] = xa
                return lastpv

            for n in range(5):
                if n < 4:
                    yield free[0:4]
                    yield from scores(n)
                if n >= 1:
                    yield state[n - 1]
                    lp = yield from values(n - 1)
            q_free[u % 2] = lp

        def weave(main, fill, share, lead=LEAD, anyb=(4, 5, 6, 7)):
            def step(g):
                w = next(g, False)
                cost = work[0]
                work[0] = 0
                return w, cost

            work[0] = 0
            md = fd = 0
            wm, c = step(main)
            wf, c = step(fill)
            while wm is not False:
                turn = False
                if wf is not False:
                    behind = md * share - fd
                    tm = max(when(wm), pe.time)
                    tf = max(when(wf), pe.time)
                    turn = behind > lead or (tm > tf + 0.1 and behind > -2 * lead)
                if turn:
                    wf, c = step(fill)
                    fd += c
                else:
                    wm, c = step(main)
                    md += c
            for _ in fill:
                pass
            work[0] = 0

        def chain(*gens):
            for g in gens:
                yield from g

        def prep(u, banks, extra=None):
            got = []
            for i in range(UB):
                b = u * UB + i
                o5, k, v = norm(b, [x_ready[b]])
                read_x[b] = o5
                if extra:
                    extra(b)
                got.append((b, v, o5, k))
            for b, v, o5, k in got:
                yield [o5]
                put_t(b, v, [o5], pick(banks), k)
            yield [xT_ready[b]]

        def add_bo(b):
            x_ready[b] = pool(lambda e, b=b: e.tensor_tensor(x[0:S, b, :], x[0:S, b, :], RW("bo"), ALU.add),
                              read_x[b], l_c)

        for _ in chain(prep(0, any0, add_bo), prep(1, any0, add_bo), project0(0, list(range(8)))):
            pass
        for u in range(NU):
            fill = []
            if u + 2 < NU:
                fill.append(prep(u + 2, any0, add_bo))
            if u + 1 < NU:
                fill.append(project0(u + 1, any0))
            weave(attend0(u), chain(*fill), SHARE0)

        if stop >= 2:
            fence = last()
            last_q0 = [done for done in xT_free]
            l_xw = [wload(f"wx{n}", n, a["wx"][:, n:n + 1, :], 1, last_q0) for n in range(4)]
            at[0] = 0
            X0 = W[:, 4:10, :].rearrange("p a n -> p (a n)")
            KcT = X0[:, 0:3000].rearrange("p (z c n) -> p z c n", z=2, c=4)
            Vc = X0[:, 3000:6072].rearrange("p (z t n) -> p z t n", z=2, t=3)
            CT = X0[:, 6072:9072].rearrange("p (z c n) -> p z c n", z=2, c=4)
            P = X0[:, 9072:12072].rearrange("p (z r n) -> p z r n", z=2, r=4)
            QX = carve(2 * 4 * UT).rearrange("p (z c n) -> p z c n", z=2, c=4)
            QM = carve(2 * 8 * S).rearrange("p (z h n) -> p z h n", z=2, h=8)
            KX = carve(2 * 4 * UT).rearrange("p (z c n) -> p z c n", z=2, c=4)
            VX = carve(2 * UB * 544).rearrange("p (z b h n) -> p z b h n", z=2, b=UB, h=32)
            MK = carve(NBATCH * S).rearrange("p (b n) -> p b n", b=NBATCH)
            SX = carve(2 * 896).rearrange("p (z n) -> p z n", z=2)
            PX = carve(8 * 448).rearrange("p (z n) -> p z n", z=8)
            OX = carve(D)
            OXT = carve(4 * S).rearrange("p (t n) -> p t n", t=4)
            RT = carve(12 * UT).rearrange("p (z k n) -> p z k n", z=4, k=3)
            anyx = [0, 1, 2, 3, 4, 5]
            rt_n = [0]
            tg = sb("tg", [128, 32])
            sx = sb("sx", [128, 2, 2, 8])
            nmx = sb("nmx", [128, 2, 4])
            sumc = sb("sumc", [128, 2, 8])
            fx = sb("fx", [128, 2, 8])
            t128 = sb("t128", [128, 128])
            Wx = [W[:, n, :].rearrange("p (k n) -> p k n", k=4) for n in range(4)]

            l_mk = load("mask", [(MK[0:S], a["mask"])], fence)
            o_tg = act(lambda e: e.activation(tg[:, :], RW("gate", 128), ACT.Tanh), fence)
            ones_x = pool(lambda e: e.memset(VX[0:S, :, :, :, 16:17], 1.0), fence)
            f_dve = dve(lambda e: e.tensor_copy(veps[0:1, 0:1], veps[0:1, 0:1]), fence)
            l_ct = [None] * NBATCH
            ct_free = [None, None]
            kc_free = [None, None]
            qx_free = [None, None]
            rt_free = [None] * 4
            kc_done = [None] * NBATCH
            qx_done = [None] * NU

            def load_ct(b):
                l_ct[b] = load(f"ct{b}", [(CT[:, b % 2], a["ctxT"][b])], fence, ct_free[b % 2])

            load_ct(0)
            load_ct(1)

            def context(b):
                z = b % 2
                kd, vd = [], []
                for c in range(4):
                    bank = pick(anyx)
                    for k in range(4):
                        o = mm(PS[:, bank, 0:SC], Wx[1][:, k, c * 128:(c + 1) * 128], CT[:, z, k, :], k == 0,
                               k == 3, l_ct[b], l_xw[1], free[bank])
                    oe = evac(c, KcT[:, z, c, :], PS[:, bank, 0:SC], o, kc_free[z], f_dve, fence)
                    free[bank] = oe
                    kd.append(oe)
                    yield
                for t in range(3):
                    bank = pick(anyx)
                    for k in range(4):
                        o = mm(PS[0:KC, bank, :], CT[:, z, k, t * KC:(t + 1) * KC], Wx[2][:, k, :], k == 0, k == 3,
                               l_xw[2], free[bank])
                    oe = evac(t, Vc[0:KC, z, t, :], PS[0:KC, bank, :], o)
                    free[bank] = oe
                    vd.append(oe)
                    yield
                ct_free[z] = o
                if b + 2 < NBATCH:
                    load_ct(b + 2)
                kc_done[b] = kd + vd

            def projectx(u):
                z = u % 2
                tok = slice(u * UT, (u + 1) * UT)
                xr = [xT_ready[u * UB + i] for i in range(UB)]
                done = []

                def b3(t):
                    return t.rearrange("p (b n) -> p b n", b=UB)

                def first(c, which):
                    bank = pick(anyx)
                    r = rt_n[0] % 4
                    rt_n[0] += 1
                    for k in range(4):
                        o = mm(PS[:, bank, 0:UT], Wx[which][:, k, c * 128:(c + 1) * 128], xT[:, k, tok],
                               k == 0, k == 3, xr, l_xw[which], free[bank])
                    e1 = act(lambda e: e.activation(RT[:, r, 0, :], PS[:, bank, 0:UT], ACT.Copy), o, rt_free[r],
                             fence)
                    free[bank] = e1
                    return c, which, r, e1

                def second(c, which, r, e1):
                    cos, sin = (("qxcos", "qxsin"), ("kxcos", "kxsin"))[which]
                    t1 = pool(lambda e: e.tensor_tensor(
                        b3(RT[:, r, 1, :]), b3(RT[:, r, 0, :]), bc(C(cos), UB), ALU.mult), e1)
                    bank = pick(anyx)
                    o = mm(PS[:, bank, 0:UT], C("rot"), RT[:, r, 0, :], True, True, e1, free[bank])
                    t2 = dve(lambda e: e.tensor_tensor(
                        b3(RT[:, r, 2, :]), b3(PS[:, bank, 0:UT]), bc(C(sin), UB), ALU.mult), o, rt_free[r])
                    free[bank] = t2
                    dst = (QX, KX)[which]
                    t3 = pool(lambda e: e.tensor_tensor(dst[:, z, c, :], RT[:, r, 1, :], RT[:, r, 2, :],
                                                        ALU.add), t2, t1, qx_free[z])
                    rt_free[r] = t3
                    done.append(t3)

                behind = None
                for c in range(4):
                    for which in range(2):
                        now_ = first(c, which)
                        if behind:
                            second(*behind)
                        behind = now_
                        yield
                second(*behind)
                for i in range(UB):
                    b = u * UB + i
                    bank = pick(anyx)
                    for k in range(4):
                        o = mm(PS[0:S, bank, :], xT[:, k, b * S:(b + 1) * S], Wx[2][:, k, :], k == 0, k == 3,
                               xr, l_xw[2], free[bank])
                    oe = act(lambda e, i=i, bank=bank: e.activation(
                        VX[0:S, z, i, :, 0:16], PS[0:S, bank, :].rearrange("p (h n) -> p h n", h=32), ACT.Copy),
                        o, qx_free[z], fence)
                    free[bank] = oe
                    done.append(oe)
                    xT_free[b] = o
                    yield
                qx_done[u] = done

            sx_free = [None, None]
            p_free = [None, None]
            px_free = [None] * 8
            px_n = [0]
            ox_free, oxt_free = [None], [None]
            small_free = [None, None]
            tb = [0]
            qm_free, qm_done = [None, None], [None, None]

            def attendx(b):
                u, i = b // UB, b % UB
                z = u % 2
                tk = slice(i * S, (i + 1) * S)
                zc = b % 2
                tasks = [(c, kind) for c in range(4) for kind in range(3)]
                state = {}

                def masks(c):
                    if c < 4:
                        zz = c % 2
                        qm_done[zz] = pool(lambda e: e.tensor_tensor(
                            QM[:, zz, :, :], QX[:, z, c, tk].unsqueeze(1).to_broadcast([128, 8, S]),
                            C("heads").unsqueeze(2).to_broadcast([128, 8, S]), ALU.mult),
                            qx_done[u], qm_free[zz])

                def scores(n):
                    c, kind = tasks[n]
                    if kind == 0:
                        zz = c % 2
                        v3 = SX[0:S, zz, :].rearrange("p (h n) -> p h n", h=8)
                        sm = sx[0:S, zz]
                        o1 = []
                        for half in range(2):
                            bank = pick(anyx)
                            for h in range(4):
                                o = mm(PS[0:S, bank, h * S:(h + 1) * S], QM[:, zz, 4 * half + h, :],
                                       KX[:, z, c, tk], True, True, qm_done[zz], free[bank])
                            o1.append(dve(lambda e, half=half, bank=bank: e.tensor_tensor(
                                v3[:, 4 * half:4 * half + 4, :],
                                PS[0:S, bank, 0:448].rearrange("p (h n) -> p h n", h=4),
                                MK[0:S, b, :].unsqueeze(1).to_broadcast([S, 4, S]), ALU.add),
                                o, l_mk, sx_free[zz], fence))
                            free[bank] = o1[-1]
                            yield
                        o2 = dve(lambda e: e.tensor_reduce(sm[:, 0, :], v3, AX.X, ALU.max), o1)
                        o3 = dve(lambda e: e.tensor_scalar(sm[:, 1, :], sm[:, 0, :], FMIN, None, ALU.max), o2)
                        o4 = dve(lambda e: e.scalar_tensor_tensor(
                            v3, v3, FMIN, sm[:, 1, :].unsqueeze(2).to_broadcast([S, 8, S]),
                            ALU.max, ALU.subtract), o3)
                        o5 = act(lambda e: e.activation(SX[0:S, zz, :], SX[0:S, zz, :], ACT.Exp), o4)
                        state[n] = o5
                    else:
                        par = kind - 1
                        zz = (c * 2 + par) % 2
                        ops = []
                        for r in range(4):
                            bank = pick(anyx)
                            o = mm(PS[0:S, bank, 0:SC], QM[:, c % 2, 2 * r + par, :], KcT[:, zc, c, :],
                                   True, True, kc_done[b], free[bank])
                            o1 = dve(lambda e, r=r, bank=bank: e.tensor_reduce(
                                nmx[0:S, zz, r:r + 1], PS[0:S, bank, 0:SC], AX.X, ALU.max, negate=True), o,
                                p_free[zz])
                            o2 = act(lambda e, r=r, bank=bank: e.activation(
                                P[0:S, zz, r, :], PS[0:S, bank, 0:SC], ACT.Exp, bias=nmx[0:S, zz, r:r + 1],
                                accum_out=sumc[0:S, c % 2, 2 * r + par:2 * r + par + 1]),
                                o1, p_free[zz], small_free[c % 2], fence)
                            free[bank] = o2
                            ops.append(o2)
                            yield
                        if par == 1:
                            qm_free[c % 2] = o
                            masks(c + 2)
                        state[n] = ops

                def values(n):
                    c, kind = tasks[n]
                    pvb = 6 + c % 2
                    if kind == 0:
                        zz = c % 2
                        o5 = state[n]
                        got = []
                        for half in range(2):
                            bank = pick(anyx)
                            slot = px_n[0] % 8
                            px_n[0] += 1
                            for h in range(4):
                                e_ = half * 4 + h
                                t = tr(PS[0:S, bank, h * S:(h + 1) * S], SX[0:S, zz, e_ * S:(e_ + 1) * S], S,
                                       o5, free[bank])
                            oe = evac(half, PX[0:S, slot, :], PS[0:S, bank, 0:448], t, px_free[slot])
                            free[bank] = oe
                            got.append((oe, slot))
                        sx_free[zz] = t
                        for half in range(2):
                            oe, slot = got[half]
                            yield oe
                            for h in range(4):
                                ln = 4 * half + h
                                o = mm(PS[0:S, pvb, ln * 17:ln * 17 + 17], PX[0:S, slot, h * S:(h + 1) * S],
                                       VX[0:S, z, i, 8 * c + ln, :], True, True, oe, ones_x, free[pvb])
                            px_free[slot] = o
                        return
                    par = kind - 1
                    zz = (c * 2 + par) % 2
                    ops = state[n]
                    got = []
                    for t_ in range(3):
                        bank = pick(anyx)
                        slot = px_n[0] % 8
                        px_n[0] += 1
                        for r in range(4):
                            t = tr(PS[0:KC, bank, r * S:(r + 1) * S], P[0:S, zz, r, t_ * KC:(t_ + 1) * KC], S,
                                   ops[r], free[bank])
                        tb[0] += 1
                        oe = evac(tb[0], PX[0:KC, slot, :], PS[0:KC, bank, 0:448], t, px_free[slot])
                        free[bank] = oe
                        got.append((oe, slot))
                        yield
                    p_free[zz] = t
                    yield oe
                    for r in range(4):
                        ln = 2 * r + par
                        for t_ in range(3):
                            oe, slot = got[t_]
                            o = mm(PS[0:S, pvb, 256 + ln * 16:272 + ln * 16], PX[0:KC, slot, r * S:(r + 1) * S],
                                   Vc[0:KC, zc, t_, (8 * c + ln) * 16:(8 * c + ln) * 16 + 16], t_ == 0, t_ == 2,
                                   oe)
                    for _, slot in got:
                        px_free[slot] = o
                    if par == 0:
                        return
                    k = c % 2
                    sp_ = PS[0:S, pvb, 0:136].rearrange("p (h n) -> p h n", h=8)
                    cp_ = PS[0:S, pvb, 256:384].rearrange("p (h n) -> p h n", h=8)
                    d1 = dve(lambda e: e.reciprocal(fx[0:S, 0, :], sp_[:, :, 16]), o, fence)
                    d2 = dve(lambda e: e.reciprocal(fx[0:S, 1, :], sumc[0:S, k, :]), ops)
                    ov = OX[0:S, c * 128:(c + 1) * 128].rearrange("p (h n) -> p h n", h=8)
                    d3 = dve(lambda e: e.tensor_tensor(
                        ov, sp_[:, :, 0:16], fx[0:S, 0, :].unsqueeze(2).to_broadcast([S, 8, 16]), ALU.mult),
                        d1, ox_free[0])
                    d4 = dve(lambda e: e.tensor_tensor(fx[0:S, 1, :], fx[0:S, 1, :], tg[0:S, 8 * c:8 * c + 8],
                                                       ALU.mult), d2, o_tg)
                    d5 = dve(lambda e: e.tensor_tensor(
                        t128[0:S, :].rearrange("p (h n) -> p h n", h=8), cp_,
                        fx[0:S, 1, :].unsqueeze(2).to_broadcast([S, 8, 16]), ALU.mult), d4)
                    small_free[k] = d2
                    free[pvb] = d5
                    d6 = dve(lambda e: e.tensor_tensor(OX[0:S, c * 128:(c + 1) * 128],
                                                       OX[0:S, c * 128:(c + 1) * 128], t128[0:S, :], ALU.add),
                             d5, d3)
                    state["o"] = d6

                masks(0)
                masks(1)
                for n in range(len(tasks) + 1):
                    if n < len(tasks):
                        if tasks[n][1] == 0:
                            yield qm_done[tasks[n][0] % 2]
                        yield from scores(n)
                    if n >= 1:
                        yield state[n - 1]
                        yield from values(n - 1)
                yield state["o"]
                bank = pick(anyx)
                for c in range(4):
                    t = tr(PS[:, bank, c * S:(c + 1) * S], OX[0:S, c * 128:(c + 1) * 128], S, state["o"], free[bank])
                ox_free[0] = t
                oe = act(lambda e: e.activation(OXT[:, :, :], PS[:, bank, 0:448].rearrange("p (c n) -> p c n", c=4),
                                                ACT.Copy), t, oxt_free[0])
                free[bank] = oe
                yield oe
                bk2 = pick(anyx)
                for c in range(4):
                    o = mm(PS[0:S, bk2, :], OXT[:, c, :], Wx[3][:, c, :], c == 0, c == 3, oe, l_xw[3], free[bk2])
                oxt_free[0] = o
                xa = dve(lambda e: e.tensor_tensor(x[0:S, b, :], x[0:S, b, :], PS[0:S, bk2, :], ALU.add), o,
                         x_ready[b])
                free[bk2] = xa
                x_ready[b] = xa
                kc_free[zc] = px_free[(px_n[0] - 1) % 8]
                qx_free[z] = px_free[(px_n[0] - 1) % 8]

            for _ in chain(prep(0, anyx), projectx(0), context(0)):
                pass
            for b in range(NBATCH):
                fills = []
                if b + 1 < NBATCH:
                    fills.append(context(b + 1))
                if b % UB == 0 and b // UB + 1 < NU:
                    fills += [prep(b // UB + 1, anyx), projectx(b // UB + 1)]
                weave(attendx(b), chain(*fills), SHAREX if len(fills) > 1 else 0.5 * SHAREX)

        if stop >= 3:
            fence = last()
            at[0] = 0
            ACC = carve(NBATCH * D).rearrange("p (b n) -> p b n", b=NBATCH)
            GA = carve(2 * 4 * 448).rearrange("p (z c n) -> p z c n", z=2, c=4)
            GS = carve(2 * 448).rearrange("p (z n) -> p z n", z=2)
            sq = carve(D)
            rt = sb("rt", [128, 12, 64])
            wr2 = sb("wr2", [128, 4, 8])
            ss8 = sb("ss8", [128, 8])
            f_act = act(lambda e: e.activation(sq[0:1, 0:1], cst[0:1, 0:1], ACT.Copy), fence)
            f_dve = dve(lambda e: e.tensor_copy(veps[0:1, 0:1], veps[0:1, 0:1]), fence)
            l_we = [None] * 8

            def load_e(x_, *after):
                l_we[x_] = wload(f"we{x_}", 3 * (x_ % 2), a["we"][x_], 3, *after)

            load_e(0, fence)
            load_e(1, fence)
            wr_o = [dve(lambda e, k=k: e.tensor_scalar(
                wr2[:, k, :], CL("wr")[:, 8 * k:8 * k + 8], CL("rscale")[:, k:k + 1], None, ALU.mult))
                for k in range(4)][-1]
            ssq = []
            for b in range(NBATCH):
                norm_t(b, [x_ready[b], fence], 4 + b % 2)
                k = (ncount[0] - 1) % 2
                o = act(lambda e, b=b, k=k: e.activation(sq[0:S, :], xn[0:S, k, :], ACT.Square,
                                                         accum_out=ss8[0:S, b:b + 1]), read_x[b], f_act, ssq[-1:])
                xn_free[k] = [xn_free[k], o]
                ssq.append(o)
            for b in range(NBATCH):
                for k in range(4):
                    o = mm(PS[0:S, 6, b * 8:b * 8 + 8], xT[:, k, b * S:(b + 1) * S], wr2[:, k, :], k == 0, k == 3,
                           xT_ready[b], wr_o, free[6])

            def r8(n):
                return rt[0:S, n, :].rearrange("p (b n) -> p b n", b=8)

            def b8(ap):
                return ap.unsqueeze(2).to_broadcast([S, 8, 8])

            d = dve(lambda e: e.tensor_scalar(rt[0:S, 8, 0:8], ss8[0:S, :], 1.0 / D, 1e-6, ALU.mult, ALU.add), ssq)
            d = pool(lambda e: e.tensor_tensor(rt[0:S, 8, 8:16], rt[0:S, 8, 0:8], mhalf[0:S, 0:8], ALU.pow), d)
            d = dve(lambda e: e.tensor_scalar(rt[0:S, 8, 8:16], rt[0:S, 8, 8:16], float(np.float32(D) ** -0.5), None,
                                              ALU.mult), d)
            d = dve(lambda e: e.tensor_tensor(r8(0), PS[0:S, 6, 0:64].rearrange("p (b n) -> p b n", b=8),
                                              b8(rt[0:S, 8, 8:16]), ALU.mult), d, o, fence)
            free[6] = d
            dl = d
            o_rank = pool(lambda e: e.memset(r8(9)[:, :, 0:1], 8.0), fence)
            for n in range(1, 8):
                o_rank = pool(lambda e, n=n: e.memset(r8(9)[:, :, n:n + 1], 8.0 - n))
            cur = 0
            sel = []
            for step in range(2):
                m = rt[0:S, 8, 16 + 8 * step:24 + 8 * step]
                m2 = rt[0:S, 8, 32 + 8 * step:40 + 8 * step]
                d = dve(lambda e, m=m, cur=cur: e.tensor_reduce(m, r8(cur), AX.X, ALU.max), d)
                if step == 0:
                    dm = d
                d = dve(lambda e, m=m, cur=cur: e.tensor_tensor(r8(2), r8(cur), b8(m), ALU.is_equal), d)
                d = dve(lambda e: e.tensor_tensor(r8(2), r8(2), r8(9), ALU.mult), d, o_rank)
                d = dve(lambda e, m2=m2: e.tensor_reduce(m2, r8(2), AX.X, ALU.max), d)
                d = dve(lambda e, m2=m2, step=step: e.tensor_tensor(r8(3 + step), r8(2), b8(m2), ALU.is_equal), d)
                sel.append(d)
                if step == 0:
                    d = dve(lambda e: e.tensor_scalar(r8(1), r8(3), -3.0e38, None, ALU.mult), d)
                    d = dve(lambda e: e.tensor_tensor(r8(1), r8(1), r8(0), ALU.add), d)
                cur = 1
            d = dve(lambda e: e.tensor_tensor(r8(5), r8(3), r8(4), ALU.add), d)
            d = dve(lambda e: e.tensor_tensor(r8(6), r8(0), b8(rt[0:S, 8, 16:24]), ALU.subtract), d)
            d = act(lambda e: e.activation(rt[0:S, 6, :], rt[0:S, 6, :], ACT.Exp), d)
            d = dve(lambda e: e.tensor_reduce(rt[0:S, 8, 48:56], r8(6), AX.X, ALU.add), d)
            d = dve(lambda e: e.reciprocal(rt[0:S, 8, 48:56], rt[0:S, 8, 48:56]), d)
            d = dve(lambda e: e.tensor_tensor(r8(6), r8(6), b8(rt[0:S, 8, 48:56]), ALU.mult), d)
            d = dve(lambda e: e.tensor_tensor(r8(7), r8(6), r8(5), ALU.mult), d)
            d = dve(lambda e: e.tensor_reduce(rt[0:S, 8, 56:64], r8(7), AX.X, ALU.add), d)
            d = dve(lambda e: e.tensor_scalar(rt[0:S, 10, 0:8], rt[0:S, 8, 56:64], 0.0, None, ALU.is_le), d)
            d = dve(lambda e: e.tensor_tensor(rt[0:S, 8, 56:64], rt[0:S, 8, 56:64], rt[0:S, 10, 0:8], ALU.add), d)
            d = dve(lambda e: e.reciprocal(rt[0:S, 8, 56:64], rt[0:S, 8, 56:64]), d)
            d = dve(lambda e: e.tensor_tensor(r8(7), r8(7), b8(rt[0:S, 8, 56:64]), ALU.mult), d)
            cw = dve(lambda e: e.tensor_tensor(r8(11), r8(7), RW("pes").unsqueeze(1).to_broadcast([S, 8, 8]),
                                               ALU.mult), d)
            gs_free, ga_free = [None, None], [None, None]
            accd = list(x_ready)
            nb = [0]

            def nbank():
                nb[0] += 1
                return nb[0] % 8

            for e_ in range(8):
                Wg = W[:, 3 * (e_ % 2):3 * (e_ % 2) + 2, :].rearrange("p a (k n) -> p (a k) n", k=2)
                Wl = W[:, 3 * (e_ % 2) + 2, :].rearrange("p (k n) -> p k n", k=4)
                for h in range(2):
                    z = (e_ * 2 + h) % 2
                    tok = slice(h * 448, (h + 1) * 448)
                    ga = []
                    for c in range(4):
                        bg, bu = nbank(), nbank()
                        for bank, off in ((bg, 0), (bu, 512)):
                            for k in range(4):
                                o = mm(PS[:, bank, 0:448], Wg[:, k, off + c * 128:off + c * 128 + 128], xT[:, k, tok],
                                       k == 0, k == 3, l_we[e_], xT_ready[4 * h:4 * h + 4], free[bank])
                            if off == 0:
                                og = o
                        zs = c % 2
                        o1 = act(lambda e, bg=bg, zs=zs: e.activation(GS[:, zs, :], PS[:, bg, 0:448],
                                                                      ACT.Gelu_apprx_tanh), og, gs_free[zs], f_act)
                        free[bg] = o1
                        o2 = dve(lambda e, bu=bu, zs=zs, z=z, c=c: e.tensor_tensor(
                            GA[:, z, c, :], GS[:, zs, :], PS[:, bu, 0:448], ALU.mult), o1, o, ga_free[z], f_dve)
                        free[bu] = o2
                        gs_free[zs] = o2
                        ga.append(o2)
                    for i in range(4):
                        b = h * 4 + i
                        bank = nbank()
                        for k in range(4):
                            o = mm(PS[0:S, bank, :], GA[:, z, k, i * S:(i + 1) * S], Wl[:, k, :], k == 0, k == 3,
                                   ga, free[bank])
                        sc = rt[0:S, 11, b * 8 + e_:b * 8 + e_ + 1]
                        oa = dve(lambda e, bank=bank, b=b, sc=sc: e.scalar_tensor_tensor(
                            x[0:S, b, :], PS[0:S, bank, :], sc, x[0:S, b, :], ALU.mult, ALU.add), o, cw, accd[b])
                        free[bank] = oa
                        accd[b] = oa
                    ga_free[z] = o
                if e_ + 2 < 8:
                    load_e(e_ + 2, o)
            for b in range(NBATCH):
                x_ready[b] = accd[b]
                xT_free[b] = o

        if stop >= 4:
            fence = last()
            at[0] = 0
            LQ = carve(2 * 16 * UT).rearrange("p (z c a n) -> p z c a n", z=2, c=8, a=2)
            LK = carve(2 * 4 * UT).rearrange("p (z c a n) -> p z c a n", z=2, c=2, a=2)
            LV = carve(2 * UB * 512).rearrange("p (z b n) -> p z b n", z=2, b=UB)
            LT = carve(2 * UT).rearrange("p (k n) -> p k n", k=2)
            t4_buf[0] = carve(4 * UT).rearrange("p (k n) -> p k n", k=4)
            t4_free[0] = fence
            LS = carve(2 * 896).rearrange("p (z n) -> p z n", z=2)
            LP = carve(4 * 448).rearrange("p (z n) -> p z n", z=4)
            LO = carve(1024)
            LOT = carve(8 * S).rearrange("p (t n) -> p t n", t=8)
            ls = sb("ls", [128, 2, 3, 8])
            l_lq = [wload(f"w1q{n}", n, a["w1q"][:, n:n + 1, :], 1, fence) for n in range(4)]
            l_ls = load("w1s", [(W[:, 8, 0:1664], a["w1s"])], fence)
            l_lo = wload("w1o", 4, a["w1o"], 4, fence)
            f_act = act(lambda e: e.activation(LT[0:1, 0, 0:1], cst[0:1, 0:1], ACT.Copy), fence)
            f_dve = dve(lambda e: e.tensor_copy(veps[0:1, 0:1], veps[0:1, 0:1]), fence)
            f_pool = pool(lambda e: e.memset(veps[0:1, 1:2], 0.0), fence)
            Wlq = W[:, 0:4, :].rearrange("p a (c k n) -> p (a c) k n", c=2, k=4)
            Wlo = W[:, 4:8, :].rearrange("p a (t n) -> p (a t) n", n=D)
            kd_w = W[:, 8, 0:256].rearrange("p (k n) -> p k n", k=4)
            vd_w = W[:, 8, 256:640].rearrange("p (k n) -> p k n", k=4)
            ku_w = W[0:64, 8, 640:1152]
            vu_w = W[0:96, 8, 1152:1664]
            l_free = [None, None]
            anyl = [4, 5, 6, 7]
            l_done = [None] * NU
            lt_free = [None]

            def projectl(u):
                z = u % 2
                tok = slice(u * UT, (u + 1) * UT)
                xr = [xT_ready[u * UB + i] for i in range(UB)]
                kr, vr, qr = [None] * 2, [None] * UB, [None] * 8
                td = []
                for n, (w, m) in enumerate(((kd_w, 64), (vd_w, 96))):
                    bank = pick(anyl)
                    for k in range(4):
                        o = mm(PS[0:m, bank, 0:UT], w[:, k, :], xT[:, k, tok], k == 0, k == 3, xr, l_ls, free[bank])
                    o = act(lambda e, n=n, m=m, bank=bank: e.activation(LT[0:m, n, :], PS[0:m, bank, 0:UT],
                                                                        ACT.Copy), o, lt_free[0], f_act)
                    free[bank] = o
                    td.append(o)
                yield td
                for c in range(2):
                    bank = pick(anyl)
                    for ab in range(2):
                        lo = (c * 2 + ab) * 128
                        o = mm(PS[:, bank, ab * UT:(ab + 1) * UT], ku_w[:, lo:lo + 128], LT[0:64, 0, :], True, True,
                               td, free[bank])
                    bk = CL("kanch")
                    kr[c] = rope(bank, bk[:, 2 * c:2 * c + 1], bk[:, 2 * c + 1:2 * c + 2], C("l1cos"), C("l1sin"),
                                 LK[:, z, c, 0, :], LK[:, z, c, 1, :], [l_free[z], f_pool], o)
                    yield
                for i in range(UB):
                    bank = pick(anyl)
                    o = mm(PS[0:S, bank, :], LT[0:96, 1, i * S:(i + 1) * S], vu_w, True, True, td, free[bank])
                    vr[i] = dve(lambda e, i=i, bank=bank: e.tensor_tensor(LV[0:S, z, i, :], PS[0:S, bank, :],
                                                                          RW("vanch"), ALU.add),
                                o, l_free[z], f_dve)
                    free[bank] = vr[i]
                lt_free[0] = o
                yield
                for c in range(8):
                    bank = pick(anyl)
                    for ab in range(2):
                        for k in range(4):
                            o = mm(PS[:, bank, ab * UT:(ab + 1) * UT], Wlq[:, c, k, ab * 128:ab * 128 + 128],
                                   xT[:, k, tok], k == 0, k == 3, xr, l_lq[c // 2], free[bank])
                    qr[c] = rope(bank, 0.0, 0.0, C("l1cos"), C("l1sin"), LQ[:, z, c, 0, :], LQ[:, z, c, 1, :],
                                 [l_free[z], f_pool], o)
                    yield
                l_done[u] = (kr, vr, qr)
                for i in range(UB):
                    xT_free[u * UB + i] = o

            lss_free, lp_free = [None, None], [None] * 4
            lo_free, lot_free = [None], [None]
            lp_n = [0]
            scale1 = float(np.float32(1.0) / np.sqrt(np.float32(128)))

            def attendl(u):
                z = u % 2
                kr, vr, qr = l_done[u]
                todo = [(i, g) for i in range(UB) for g in range(2)]
                state = {}

                def scores(n):
                    i, g = todo[n]
                    tk = slice(i * S, (i + 1) * S)
                    zz = n % 2
                    for j in range(4):
                        for ab in range(2):
                            for r in range(2):
                                ro = slice(64 * r, 64 * r + 64)
                                o = mm(PS[0:S, 2 * zz + r, j * S:(j + 1) * S], LQ[ro, z, 4 * g + j, ab, tk],
                                       LK[ro, z, g, ab, tk], ab == 0, ab == 1, qr[4 * g + j], kr[g],
                                       free[2 * zz + r])
                        yield
                    sm = ls[0:S, zz]
                    v3 = LS[0:S, zz, :].rearrange("p (h n) -> p h n", h=8)
                    o1 = dve(lambda e: e.tensor_tensor(
                        LS[0:S, zz, :].rearrange("p (r j n) -> p r j n", r=2, j=4),
                        PS[0:S, 2 * zz:2 * zz + 2, 0:448].rearrange("p r (j n) -> p r j n", j=4),
                        C("causal", 0, S).unsqueeze(1).unsqueeze(1).to_broadcast([S, 2, 4, S]), ALU.add),
                        o, lss_free[zz], f_dve)
                    for r in range(2):
                        free[2 * zz + r] = o1
                    o2 = dve(lambda e: e.tensor_reduce(sm[:, 0, :], v3, AX.X, ALU.max, negate=True), o1,
                             lss_free[zz])
                    o3 = dve(lambda e: e.tensor_scalar(sm[:, 1, :], sm[:, 0, :], scale1, None, ALU.mult), o2)
                    for h in range(8):
                        o4 = act(lambda e, h=h: e.activation(
                            v3[:, h, :], v3[:, h, :], ACT.Exp, bias=sm[:, 1, h:h + 1], scale=scale1,
                            accum_out=sm[:, 2, h:h + 1]), o3, f_act)
                    state[n] = o4

                def values(n):
                    i, g = todo[n]
                    b = u * UB + i
                    zz = n % 2
                    o4 = state[n]
                    sm = ls[0:S, zz]
                    rc = dve(lambda e: e.reciprocal(sm[:, 2, :], sm[:, 2, :]), o4)
                    got = []
                    for r in range(2):
                        bank = pick(anyl)
                        slot = lp_n[0] % 4
                        lp_n[0] += 1
                        for j in range(4):
                            h = 4 * r + j
                            t = tr(PS[0:S, bank, j * S:(j + 1) * S], LS[0:S, zz, h * S:(h + 1) * S], S, o4, free[bank])
                        oe = evac(r, LP[0:S, slot, :], PS[0:S, bank, 0:448], t, lp_free[slot])
                        free[bank] = oe
                        got.append((oe, slot))
                    dd = []
                    for r in range(2):
                        oe, slot = got[r]
                        yield oe
                        kv = 2 * g + r
                        bank = pick(anyl)
                        for j in range(4):
                            o = mm(PS[0:S, bank, j * 128:(j + 1) * 128], LP[0:S, slot, j * S:(j + 1) * S],
                                   LV[0:S, z, i, kv * 128:(kv + 1) * 128], True, True, oe, vr[i], free[bank])
                        lp_free[slot] = o
                        d3 = dve(lambda e, r=r, bank=bank: e.tensor_tensor(
                            LO[0:S, r * 512:(r + 1) * 512].rearrange("p (h n) -> p h n", h=4),
                            PS[0:S, bank, :].rearrange("p (h n) -> p h n", h=4),
                            sm[:, 2, 4 * r:4 * r + 4].unsqueeze(2).to_broadcast([S, 4, 128]), ALU.mult),
                            o, rc, lo_free[0])
                        free[bank] = d3
                        dd.append(d3)
                    lss_free[zz] = [t, d3]
                    lastpv = o
                    oes = []
                    for half in range(2):
                        yield dd[half]
                        bank = pick(anyl)
                        for c in range(4):
                            cc = half * 4 + c
                            t = tr(PS[:, bank, c * S:(c + 1) * S], LO[0:S, cc * 128:(cc + 1) * 128], S, dd[half],
                                   free[bank])
                        oe = evac(half, LOT[:, half * 4:half * 4 + 4, :],
                                  PS[:, bank, 0:448].rearrange("p (c n) -> p c n", c=4), t, lot_free[0])
                        free[bank] = oe
                        oes.append(oe)
                    lo_free[0] = t
                    yield oes
                    bo_ = pick(anyl)
                    for c in range(8):
                        o = mm(PS[0:S, bo_, :], LOT[:, c, :], Wlo[:, g * 8 + c, :], c == 0, c == 7, oes, l_lo,
                               free[bo_])
                    lot_free[0] = o
                    xa = dve(lambda e: e.tensor_tensor(x[0:S, b, :], x[0:S, b, :], PS[0:S, bo_, :], ALU.add),
                             o, x_ready[b])
                    free[bo_] = xa
                    x_ready[b] = xa
                    return lastpv

                for n in range(5):
                    if n < 4:
                        yield [free[2 * (n % 2)], free[2 * (n % 2) + 1]]
                        yield from scores(n)
                    if n >= 1:
                        yield state[n - 1]
                        lp = yield from values(n - 1)
                l_free[z] = lp

            for _ in chain(prep(0, anyl), projectl(0)):
                pass
            for u in range(NU):
                fill = chain(prep(u + 1, anyl), projectl(u + 1)) if u + 1 < NU else iter(())
                weave(attendl(u), fill, SHAREL)

        if stop >= 5:
            fence = last()
            at[0] = 0
            C5 = carve(3 * 1500).rearrange("p (z k n) -> p z k n", z=3, k=4)
            M5 = carve(3 * 1536).rearrange("p (z t n) -> p z t n", z=3, t=3)
            MF = carve(3000).rearrange("p (b n) -> p b n", b=8)
            NB = carve(3000).rearrange("p (b n) -> p b n", b=8)
            S5 = carve(2 * SC).rearrange("p (z n) -> p z n", z=2)
            P5 = carve(2 * 3 * S).rearrange("p (z t n) -> p z t n", z=2, t=3)
            mu = carve(8 * SC // 4).bitcast(U8)
            s5 = sb("s5", [128, 8, 4])
            scale5 = float(np.float32(1.0) / np.sqrt(np.float32(512)))
            l_mu = load("mu", [(mu[0:S, :], a["cmask"])], fence)
            l_c5 = [None] * 8
            c5_free = [None] * 3

            def load5(b):
                l_c5[b] = load(f"c5{b}", [(C5[:, b % 3], a["ctxT"][b]), (M5[0:KC, b % 3], a["ctx"][b])],
                               fence, c5_free[b % 3])

            for b in range(3):
                load5(b)
            m1 = dve(lambda e: e.tensor_copy(MF[0:S, :, :], mu[0:S, :].rearrange("p (b n) -> p b n", b=8)),
                     l_mu, fence)
            m2 = dve(lambda e: e.tensor_scalar(NB[0:S, :, :], MF[0:S, :, :], -1.0, 1e30, ALU.add, ALU.mult), m1)
            m3 = dve(lambda e: e.tensor_reduce(s5[0:S, :, 3], MF[0:S, :, :], AX.X, ALU.max), m1)
            s5_free = [None, None]
            p5_free = [None, None]
            st5 = {}

            def scores5(b):
                z = b % 2
                bank = z
                norm_t(b, [x_ready[b]], 4 + z)
                for k in range(4):
                    o = mm(PS[0:S, bank, 0:SC], xT[:, k, b * S:(b + 1) * S], C5[:, b % 3, k, :], k == 0, k == 3,
                           xT_ready[b], l_c5[b], free[bank])
                xT_free[b] = o
                sv = S5[0:S, z, :]
                o = dve(lambda e: e.tensor_tensor(sv, PS[0:S, bank, 0:SC], MF[0:S, b, :], ALU.mult), o, m2,
                        s5_free[z])
                free[bank] = o
                o = dve(lambda e: e.tensor_tensor(sv, sv, NB[0:S, b, :], ALU.add), o)
                o = dve(lambda e: e.tensor_reduce(s5[0:S, b, 0:1], sv, AX.X, ALU.max, negate=True), o)
                o = dve(lambda e: e.tensor_scalar(s5[0:S, b, 1:2], s5[0:S, b, 0:1], scale5, None, ALU.mult), o)
                o = act(lambda e: e.activation(sv, sv, ACT.Exp, bias=s5[0:S, b, 1:2], scale=scale5,
                                               accum_out=s5[0:S, b, 2:3]), o)
                q = dve(lambda e: e.reciprocal(s5[0:S, b, 2:3], s5[0:S, b, 2:3]), o)
                q = dve(lambda e: e.tensor_tensor(s5[0:S, b, 2:3], s5[0:S, b, 2:3], s5[0:S, b, 3:4], ALU.mult),
                        q, m3)
                st5[b] = (o, q)

            def values5(b):
                z = b % 2
                o, q = st5[b]
                for t_ in range(3):
                    t = tr(PS[0:KC, 2 + z, t_ * S:(t_ + 1) * S], S5[0:S, z, t_ * KC:(t_ + 1) * KC], S, o,
                           free[2 + z])
                s5_free[z] = t
                oe = act(lambda e: e.activation(P5[0:KC, z, :, :].rearrange("p t n -> p (t n)"),
                                                PS[0:KC, 2 + z, 0:3 * S], ACT.Copy), t, p5_free[z], fence)
                free[2 + z] = oe
                bank = 6 + z
                for t_ in range(3):
                    o = mm(PS[0:S, bank, :], P5[0:KC, z, t_, :], M5[0:KC, b % 3, t_, :], t_ == 0, t_ == 2, oe,
                           free[bank])
                p5_free[z] = o
                c5_free[b % 3] = o
                xa = dve(lambda e: e.scalar_tensor_tensor(x[0:S, b, :], PS[0:S, bank, :], s5[0:S, b, 2:3],
                                                          x[0:S, b, :], ALU.mult, ALU.add), o, q, x_ready[b])
                free[bank] = xa
                x_ready[b] = xa
                if b + 3 < NBATCH:
                    load5(b + 3)

            for b in range(NBATCH + 1):
                if b < NBATCH:
                    scores5(b)
                if b >= 1:
                    values5(b - 1)

        if stop >= 6:
            fence = last()
            at[0] = 0
            RB = carve(20 * D).rearrange("p (k n) -> p k n", k=20)
            H = carve(NBATCH * D).rearrange("p (b n) -> p b n", b=NBATCH)
            EB = carve(16 * S).rearrange("p (k n) -> p k n", k=16)
            MD = carve(2 * D).rearrange("p (k n) -> p k n", k=2)
            TS = carve(3 * D).rearrange("p (k n) -> p k n", k=3)
            f_act = act(lambda e: e.activation(MD[0:1, 0, 0:1], cst[0:1, 0:1], ACT.Copy), fence)
            f_dve = dve(lambda e: e.tensor_copy(veps[0:1, 0:1], veps[0:1, 0:1]), fence)
            f_pool = pool(lambda e: e.memset(veps[0:1, 1:2], 0.0), fence)
            l_rb = load("rows2", [(RB, a["rows2"])], fence)

            def rb(name, hi=S):
                return RB[0:hi, ROW2.index(name), :]

            def load_ent(l, *after):
                return [load(f"ent{l}", [(W[:, 0:4, :], a["entwT"][l]), (W[:, 4:8, :], a["entpw"][l])], *after)]

            bcomb = []
            le = load_ent(0, fence)
            for l in range(2):
                wT = W[:, 0:4, :].rearrange("p a (k n) -> p (a k) n", k=4)
                pw = W[:, 4:8, :].rearrange("p a (k n) -> p (a k) n", k=4)
                eb = dve(lambda e, l=l: e.tensor_copy(
                    EB, CL("entb")[:, 16 * l:16 * l + 16].unsqueeze(2).to_broadcast([128, 16, S])),
                    bcomb, free[4])
                for m in range(4):
                    for k in range(16):
                        o = mm(PS[:, m, :], wT[:, k, m * 128:(m + 1) * 128], pw[:, k, :], k == 0, k == 15, le,
                               free[m], fence)
                    oe = evac(m, W[:, 8 + l, m * 512:(m + 1) * 512], PS[:, m, :], o, f_act, f_dve)
                    free[m] = oe
                for k in range(16):
                    o = mm(PS[0:S, 4, :], EB[:, k, :], pw[:, k, :], k == 0, k == 15, eb, free[4])
                d = dve(lambda e, l=l: e.tensor_tensor(rb(f"entpb{l}"), PS[0:S, 4, :], rb(f"entpb{l}"), ALU.add),
                        o, l_rb)
                free[4] = d
                bcomb = [d]
                wc_done = [oe, d, act.ops[-1], dve.ops[-1]] if l == 1 else None
                if l == 0:
                    le = load_ent(1, o)
            after_comb = o
            l_ap = load("ampph", [(W[:, 0:2, :], a["ampph"])], after_comb)
            l_pw = [load(f"path{l}", [(W[:, 2 + 2 * l:4 + 2 * l, :], a["pathw"][l])], after_comb) for l in range(2)]
            AMP = W[:, 6:8, :].rearrange("p a (b n) -> p (a b) n", n=D)

            def cos_sin(v, s_, c_, scale, ops, w=None):
                hi = v.shape[0]
                o1 = act(lambda e: e.activation(s_, v, ACT.Sin, scale=scale / 2), ops, w, f_act)
                o2 = act(lambda e: e.activation(c_, v, ACT.Abs), ops, w, f_act)
                o3 = act(lambda e: e.activation(c_, c_, ACT.Sin, bias=C("halfpi", 0, hi), scale=-scale / 2), o2)
                o4 = dve(lambda e: e.tensor_tensor(c_, c_, s_, ALU.subtract), o3, o1)
                o5 = dve(lambda e: e.tensor_tensor(c_, c_, s_, ALU.mult), o4)
                return dve(lambda e: e.tensor_scalar(v, c_, 2.0, 1.0, ALU.mult, ALU.add), o5)

            PH = RB[:, ROW2.index("ph00"):ROW2.index("ph00") + 4, :]
            G4 = H[:, 0:4, :]
            magic = 12582912.0
            c1 = 6.28125
            c2 = float(2 * np.pi - 6.28125)
            d = dve(lambda e: e.tensor_scalar(G4, PH, float(1 / (2 * np.pi)), magic, ALU.mult, ALU.add), l_rb, f_dve)
            d = dve(lambda e: e.tensor_scalar(G4, G4, -magic, None, ALU.add), d)
            d = dve(lambda e: e.scalar_tensor_tensor(PH, G4, -c1, PH, ALU.mult, ALU.add), d)
            d = dve(lambda e: e.scalar_tensor_tensor(PH, G4, -c2, PH, ALU.mult, ALU.add), d)
            mod = cos_sin(PH, G4, H[:, 4:8, :], 1.0, d)
            wp_done = []
            for l in range(2):
                p0 = W[:, 2 + 2 * l, :].rearrange("p (k n) -> p k n", k=4)
                p1 = W[:, 3 + 2 * l, :].rearrange("p (k n) -> p k n", k=4)
                m0 = rb(f"ph{l}0", 128).unsqueeze(1).to_broadcast([128, 4, D])
                m1_ = rb(f"ph{l}1", 128).unsqueeze(1).to_broadcast([128, 4, D])
                d0 = dve(lambda e, p0=p0, m0=m0: e.tensor_tensor(p0, p0, m0, ALU.mult), mod, l_pw[l])
                q0 = pool(lambda e, p1=p1, m1_=m1_: e.tensor_tensor(p1, p1, m1_, ALU.mult), mod, l_pw[l])
                wp = dve(lambda e, p0=p0, p1=p1: e.tensor_tensor(p0, p0, p1, ALU.add), d0, q0)
                d0 = pool(lambda e, l=l: e.tensor_tensor(rb(f"pb{l}0"), rb(f"pb{l}0"), rb(f"ph{l}0"), ALU.mult), mod)
                d1 = pool(lambda e, l=l: e.tensor_tensor(rb(f"pb{l}1"), rb(f"pb{l}1"), rb(f"ph{l}1"), ALU.mult), mod)
                d2 = pool(lambda e, l=l: e.tensor_tensor(rb(f"pb{l}0"), rb(f"pb{l}0"), rb(f"pb{l}1"), ALU.add),
                          d0, d1)
                wp_done.append([wp, d2])

            hr = [None] * NBATCH
            Wa = W[:, 0, :].rearrange("p (k n) -> p k n", k=4)
            Wp_ = W[:, 1, :].rearrange("p (k n) -> p k n", k=4)
            for b in range(NBATCH):
                norm_t(b, [x_ready[b]], 5)
                ba, bp = 2 * (b % 2), 2 * (b % 2) + 1
                for bank, w in ((ba, Wa), (bp, Wp_)):
                    for k in range(4):
                        o = mm(PS[0:S, bank, :], xT[:, k, b * S:(b + 1) * S], w[:, k, :], k == 0, k == 3,
                               xT_ready[b], l_ap, free[bank])
                    if bank == ba:
                        oa = o
                xT_free[b] = o
                d1 = dve(lambda e, b=b, ba=ba: e.tensor_tensor(AMP[0:S, b, :], PS[0:S, ba, :], rb("ampb"), ALU.add),
                         oa, after_comb)
                free[ba] = d1
                d2 = dve(lambda e, b=b, bp=bp: e.tensor_tensor(H[0:S, b, :], PS[0:S, bp, :], rb("phb"), ALU.add),
                         o, mod)
                free[bp] = d2
                a1 = act(lambda e, b=b: e.activation(AMP[0:S, b, :], AMP[0:S, b, :], ACT.Sigmoid), d1)
                a2 = act(lambda e, b=b: e.activation(H[0:S, b, :], H[0:S, b, :], ACT.Tanh), d2)
                hr[b] = [a1, a2]
            cs_free = None
            for b in range(NBATCH):
                hb = H[0:S, b, :]
                a3 = cos_sin(hb, TS[0:S, 0, :], TS[0:S, 1, :], float(np.pi), hr[b], cs_free)
                cs_free = a3
                hr[b] = pool(lambda e, b=b: e.tensor_tensor(H[0:S, b, :], H[0:S, b, :], AMP[0:S, b, :], ALU.mult),
                             a3, hr[b])
            yn = [0]
            y_free = [None, None, None]
            for l in range(2):
                for part in range(2):
                    w = W[:, 8 + l, :] if part == 0 else W[:, 2 + 2 * l, :]
                    w = w.rearrange("p (k n) -> p k n", k=4)
                    wd = wc_done if part == 0 else wp_done[l]
                    bias = f"entpb{l}" if part == 0 else f"pb{l}0"
                    gn, bn = (f"g3{l}", f"b3{l}") if part == 0 else (f"g4{l}", f"b4{l}")
                    for b in range(NBATCH):
                        hb = H[0:S, b, :]
                        put_t(b, hb, [hr[b]], 4 + b % 2)
                        z = yn[0] % 3
                        yn[0] += 1
                        r1 = pool(lambda e, z=z, hb=hb, bias=bias: e.tensor_tensor(TS[0:S, z, :], hb, rb(bias),
                                                                                  ALU.add),
                                  hr[b], y_free[z], cs_free, bcomb, wp_done[l])
                        bank = b % 4
                        for k in range(4):
                            o = mm(PS[0:S, bank, :], xT[:, k, b * S:(b + 1) * S], w[:, k, :], k == 0, k == 3,
                                   xT_ready[b], wd, free[bank])
                        xT_free[b] = o
                        r2 = dve(lambda e, z=z, bank=bank: e.tensor_tensor(TS[0:S, z, :], PS[0:S, bank, :],
                                                                           TS[0:S, z, :], ALU.add), o, r1)
                        free[bank] = r2
                        o5, _, _ = norm(b, [r2], TS[0:S, z, :], TS[0:S, z, :])
                        r3 = dve(lambda e, z=z, gn=gn: e.tensor_tensor(TS[0:S, z, :], TS[0:S, z, :], rb(gn),
                                                                       ALU.mult), o5, l_rb)
                        r4 = pool(lambda e, z=z, hb=hb, bn=bn: e.tensor_tensor(hb, TS[0:S, z, :], rb(bn), ALU.add),
                                  r3, xT_ready[b])
                        y_free[z] = r4
                        hr[b] = r4
            for b in range(NBATCH):
                x_ready[b] = dve(lambda e, b=b: e.tensor_tensor(x[0:S, b, :], x[0:S, b, :], H[0:S, b, :], ALU.add),
                                 hr[b], x_ready[b])

        store = Load(sp, sem("d_out"), [
            (lambda e, u=u: e.dma_start(out[:, u * UB:(u + 1) * UB, :], x[0:S, u * UB:(u + 1) * UB, :]))
            for u in range(NU)], [x_ready])

        count(queues)
        block = ctx.enter_context(nc.Block())

        @block.sync
        def _(e):
            play(e, sp)
            e.wait_ge(store.sem, store.value)

        @block.tensor
        def _(e):
            play(e, pe)

        @block.vector
        def _(e):
            play(e, dve)

        @block.scalar
        def _(e):
            play(e, act)

        @block.gpsimd
        def _(e):
            play(e, pool)


def kmaj(w):
    k, n = w.shape
    return w.reshape(k // 128, 128, n).transpose(1, 0, 2)


def slots(w):
    return np.ascontiguousarray(w.reshape(128, -1, 2048))


def layout(i):
    o = {"consts": CONSTS}
    o["x"] = i["x"].transpose(1, 0, 2)
    q = kmaj(i["L0_attn_Wq"].reshape(512, 2048)).reshape(128, 4, 2, 4, 4, 32, 2)
    q = q.transpose(0, 2, 4, 1, 6, 3, 5)
    o["w0q"] = slots(q)
    k = kmaj(i["L0_attn_Wk"].reshape(512, 512)).reshape(128, 4, 2, 4, 32, 2).transpose(0, 1, 2, 5, 3, 4)
    v = kmaj(i["L0_attn_Wv"].reshape(512, 512))
    o["w0kv"] = np.ascontiguousarray(np.stack([k.reshape(128, 2048), v.reshape(128, 2048)], 1))
    o["w0o"] = slots(kmaj(i["L0_attn_Wo"].reshape(2048, 512)))
    o["wx"] = np.stack([kmaj(i["L0_xattn_" + w]).reshape(128, 2048) for w in ("Wq", "Wk", "Wv", "Wo")], 1)
    o["mask"] = i["mask_Bx1xSxS_fk0"][:, 0].transpose(1, 0, 2)
    o["ctxT"] = i["ctx_2048"].transpose(0, 2, 1).reshape(8, 4, 128, SC).transpose(0, 2, 1, 3)
    g = i["L0_ffn_gating_einsum"].transpose(0, 3, 1, 2).reshape(8, 4, 128, 1024).transpose(0, 2, 1, 3)
    ln = i["L0_ffn_linear"].reshape(8, 4, 128, 512).transpose(0, 2, 1, 3)
    o["we"] = np.concatenate([g.reshape(8, 128, 4096), ln.reshape(8, 128, 2048)], 2).reshape(8, 128, 3, 2048)
    q = kmaj(i["L1_attn_Wq"].T).reshape(128, 4, 2, 2, 4, 2, 64).transpose(0, 2, 4, 1, 5, 3, 6)
    o["w1q"] = slots(q)
    o["w1o"] = slots(kmaj(i["L1_attn_Wo"].T))
    ku = i["L1_attn_Wk_up"].reshape(2, 2, 2, 64, 64).transpose(4, 0, 2, 1, 3).reshape(64, 512)
    small = np.zeros((128, 1664), np.float32)
    small[:, 0:256] = kmaj(i["L1_attn_Wk_down"].T).reshape(128, 256)
    small[:, 256:640] = kmaj(i["L1_attn_Wv_down"].T).reshape(128, 384)
    small[0:64, 640:1152] = ku
    small[0:96, 1152:1664] = i["L1_attn_Wv_up"].T
    o["w1s"] = small
    o["ctx"] = i["ctx_2048"].reshape(8, 3, KC, D).transpose(0, 2, 1, 3)
    o["cmask"] = np.broadcast_to(i["mask_BxS2_bk0"].reshape(1, 8 * SC), (S, 8 * SC))
    o["entwT"] = np.stack([kmaj(w.T).reshape(128, 4, 2048) for w in i["L1_ffn_ent_w"]])
    o["entpw"] = np.stack([kmaj(w).reshape(128, 4, 2048) for w in i["L1_ffn_ent_pw"]])
    o["ampph"] = np.stack([kmaj(i[n]).reshape(128, 2048) for n in ("L1_ffn_amp_w", "L1_ffn_ph_w")], 1)
    o["pathw"] = np.stack([np.stack([kmaj(w).reshape(128, 2048) for w in wl], 1) for wl in i["L1_ffn_path_w"]])
    r2 = [i["L1_ffn_amp_b"], i["L1_ffn_ph_b"], *i["L1_ffn_ent_pb"], *i["L1_ffn_path_b"].reshape(4, 512),
          *i["L1_ffn_phase"].reshape(4, 512)]
    for n in "34":
        for l in range(2):
            r2 += [i[f"L1_ffn_ln{n}_g"][l], i[f"L1_ffn_ln{n}_b"][l]]
    o["rows2"] = np.broadcast_to(np.stack(r2), (128, 20, D))
    cols = [
        i["L0_attn_bq"].reshape(2, 4, 4, 32, 2).transpose(1, 3, 0, 2, 4).reshape(128, 16),
        i["L0_attn_bk"].reshape(2, 4, 32, 2).transpose(1, 2, 0, 3).reshape(128, 4),
        i["L0_ffn_router_scale"].reshape(4, 128).T,
        i["L1_attn_k_anchor"].reshape(2, 2, 2, 64).transpose(1, 3, 0, 2).reshape(128, 4),
        kmaj(i["L0_ffn_router_logits"]).reshape(128, 32),
        i["L1_ffn_ent_b"].reshape(2, 16, 128).transpose(2, 0, 1).reshape(128, 32)]
    o["cols"] = np.concatenate(cols, 1)
    rows = [i["L0_attn_bv"].ravel(), i["L0_attn_bo"], i["L0_attn_sinks"], i["L0_xattn_gate"].ravel(),
            i["L0_ffn_per_expert_scale"], i["L1_attn_v_anchor"]]
    o["rows"] = np.broadcast_to(np.concatenate(rows), (128, NROW))
    return {k: np.ascontiguousarray(v) for k, v in o.items()}


def kernel(**inputs):
    import concourse.bacc as bacc
    from concourse.bass_utils import run_bass_kernel_spmd as run

    arrays = layout({k: np.asarray(v) for k, v in inputs.items()})
    nc = bacc.Bacc("TRN2", target_bir_lowering=False, num_devices=1)
    aps = {k: nc.dram_tensor("in_" + k, v.shape, mybir.dt.from_np(v.dtype), kind="ExternalInput").ap()
           for k, v in arrays.items()}
    out = nc.dram_tensor("out", (S, NBATCH, D), F32, kind="ExternalOutput").ap()
    program(nc, aps, out)
    r = run(nc, [{"in_" + k: v for k, v in arrays.items()}], core_ids=[0])
    return np.ascontiguousarray(r.results[0]["out"].transpose(1, 0, 2))
```

```python
from contextlib import ExitStack

import numpy as np
import concourse.bass as bass
from concourse import mybir

F32 = mybir.dt.float32
U8 = mybir.dt.uint8
ALU = mybir.AluOpType
ACT = mybir.ActivationFunctionType
AX = mybir.AxisListType

NBATCH = 8
S = 112
D = 512
SC = 375
KC = 125
UB = 2
NU = NBATCH // UB
UT = UB * S
FMIN = float(np.finfo(np.float32).min)


def size(ap):
    n = 1
    for d in ap.shape[1:]:
        n *= d
    return n


class Price:

    def __init__(self, fixed, each):
        self.fixed, self.each = fixed, each

    def of(self, n):
        return self.fixed + n * self.each

    def matmul(self, o, l, r, start=None, stop=None):
        return max(size(o), size(l)) * 4 / 2300.0

    def transpose(self, o, i, ident):
        return size(o) * 2 / 2300.0

    def activation(self, o, i, f, **k):
        return self.of(size(i))

    def memset(self, o, v):
        return self.of(size(o))

    def tensor_copy(self, o, i):
        return self.of(size(o))

    def tensor_reduce(self, o, i, *_, **k):
        return self.of(size(i))

    def tensor_scalar(self, o, i, *_, **k):
        return self.of(size(i))

    def tensor_tensor(self, o, i, j, *_, **k):
        return self.of(size(o))

    def scalar_tensor_tensor(self, o, i, s, j, *_, **k):
        return self.of(size(o))

    def reciprocal(self, o, i):
        return self.of(size(i))

    def bn_stats(self, o, i):
        return self.of(size(i))

    def bn_aggr(self, o, i):
        return self.of(size(i))

    def dma_start(self, o, i):
        return 0.0


PRICES = {"pe": Price(0, 0), "dve": Price(0.07, 0.00105), "act": Price(0.2, 0.00075), "pool": Price(0.1, 0.0022),
          "sp": Price(0, 0)}
HOP = {"pe": 0.25, "dve": 0.15, "act": 0.25, "pool": 0.15, "sp": 0.2}


class Op:

    def __init__(self, queue, issue, after):
        self.queue, self.issue, self.after = queue, issue, after
        self.used = False
        self.value = 0
        self.sem = None


class Queue:

    def __init__(self, name, sem):
        self.name, self.sem, self.ops = name, sem, []
        self.time = 0.0

    def __call__(self, issue, *after):
        op = Op(self, issue, flat(after))
        op.sem = self.sem
        self.ops.append(op)
        self.time = max([self.time] + [when(a) for a in op.after]) + issue(PRICES[self.name])
        op.end = self.time + HOP[self.name]
        return op


class Load:

    def __init__(self, queue, sem, issues, after, mb=0.0):
        self.queue, self.sem, self.used = queue, sem, True
        self.value = 16 * len(issues)
        self.end = max([LOADS[0]] + [when(a) for a in flat(after)]) + 2.0 + mb * 5.5
        LOADS[0] = self.end - 2.0
        for n, issue in enumerate(issues):
            op = Op(queue, issue, flat(after) if n == 0 else [])
            op.sem, op.dma = sem, True
            queue.ops.append(op)


LOADS = [0.0]


def when(a):
    if a is None:
        return 0.0
    if isinstance(a, (list, tuple)):
        return max([0.0] + [when(b) for b in a])
    return a.end


def flat(after):
    out = []
    for a in after:
        if a is None:
            continue
        if isinstance(a, (list, tuple)):
            out += flat(a)
        else:
            out.append(a)
    return out


def count(queues):
    for q in queues:
        for op in q.ops:
            for a in op.after:
                a.used = True
    for q in queues:
        n = 0
        for op in q.ops:
            if op.sem is q.sem and op.used:
                n += 1
                op.value = n


def play(engine, queue):
    seen = {}
    for op in queue.ops:
        need = {}
        for a in op.after:
            key = a.sem.name
            if key not in need or need[key][1] < a.value:
                need[key] = (a.sem, a.value)
        for key, (sem, value) in need.items():
            if seen.get(key, 0) < value:
                engine.wait_ge(sem, value)
                seen[key] = value
        ins = op.issue(engine)
        if op.sem is not queue.sem:
            ins.then_inc(op.sem, 16)
        elif op.used:
            ins.then_inc(op.sem, 1)


CST = {}


def constants():
    parts = []

    def add(name, a):
        at = sum(p.shape[1] for p in parts)
        CST[name] = (at, a.shape[1])
        parts.append(a.astype(np.float32))

    f = np.float32
    p = np.arange(128)
    add("ident", np.eye(128))
    rot = np.zeros((128, 128), f)
    for j in range(128):
        if j % 16 < 8:
            rot[j + 8, j] = -1.0
        else:
            rot[j - 8, j] = 1.0
    add("rot", rot)
    t = np.arange(S, dtype=f)
    inv = f(1.0) / np.power(f(150000.0), np.arange(32, dtype=f) * f(2.0) / f(64))
    ang = (t[:, None] * inv[None, :]).astype(f).T[p % 32]
    c0, s0 = np.cos(ang), np.sin(ang)
    add("q0cos", c0 * f(0.125))
    add("q0sin", s0 * f(0.125))
    add("k0cos", c0)
    add("k0sin", s0)
    inv = f(1.0) / f(10000.0) ** (np.arange(0, 16, 2, dtype=f) / f(16))
    ang = np.outer(t, inv).astype(f).T[p % 8]
    c1, s1 = np.cos(ang), np.sin(ang)
    add("qxcos", c1 * f(0.25))
    add("qxsin", s1 * f(0.25))
    add("kxcos", c1)
    add("kxsin", s1)
    inv = f(1.0) / np.power(f(10000.0), np.arange(0, 128, 2, dtype=f) / f(128))
    ang = (t[:, None] * inv[None, :]).astype(f).T[p % 64]
    add("l1cos", np.cos(ang))
    add("l1sin", np.sin(ang))
    add("heads", p[:, None] // 16 == np.arange(8)[None, :])
    k = np.arange(S)
    causal = np.where(k[None, :] <= k[:, None], 0.0, -1e9)
    add("causal", np.concatenate([causal, np.zeros((16, S))], 0))
    add("halfpi", np.full((128, 1), np.pi / 2))
    strict = np.zeros((128, S))
    strict[:S] = (k[:, None] < k[None, :])
    add("strict", strict)
    return np.ascontiguousarray(np.concatenate(parts, 1))


CONSTS = constants()
NCST = CONSTS.shape[1]
COLS = {"bq": (0, 16), "bk": (16, 4), "rscale": (20, 4), "kanch": (24, 4), "wr": (28, 32), "entb": (60, 32)}
NCOL = 92
ROWS = {"bv": (0, 512), "bo": (512, 512), "sinks": (1024, 32), "gate": (1056, 32), "pes": (1088, 8),
        "vanch": (1096, 512)}
NROW = 1608
ROW2 = ["ampb", "phb", "ph00", "ph01", "ph10", "ph11", "entpb0", "entpb1", "pb00", "pb01", "pb10", "pb11",
        "g30", "b30", "g31", "b31", "g40", "b40", "g41", "b41"]
WSLOTS = 10
LEAD = 8000
SHARE0 = 0.6
SHAREX = 0.75
SHARE5 = 2.7
SHAREL = 0.5
RSIZE = 18816


def program(nc, a, out, stop=9):
    with ExitStack() as ctx:
        def sb(name, shape, dt=F32):
            return ctx.enter_context(nc.sbuf_tensor(name, shape, dt))

        def sem(name):
            return ctx.enter_context(nc.semaphore(name))

        PS = ctx.enter_context(nc.psum_tensor("PS", [128, 8, 512], F32))
        x = sb("x", [128, NBATCH, D])
        xT = sb("xT", [128, 4, NBATCH * S])
        W = sb("W", [128, WSLOTS, 2048])
        R = sb("R", [128, RSIZE])
        cst = sb("cst", [128, NCST])
        col = sb("col", [128, NCOL])
        row = sb("row", [128, NROW])
        st = sb("st", [128, NBATCH, 6])
        mv = sb("mv", [128, NBATCH, 2])
        rstd = sb("rstd", [128, NBATCH])
        veps = sb("veps", [128, NBATCH])
        mhalf = sb("mhalf", [128, 16])
        pad = sb("pad", [128, 4])
        xn = sb("xn", [128, 2, D])

        pe = Queue("pe", sem("s_pe"))
        dve = Queue("dve", sem("s_dve"))
        act = Queue("act", sem("s_act"))
        pool = Queue("pool", sem("s_pool"))
        sp = Queue("sp", sem("s_sp"))
        queues = [pe, dve, act, pool, sp]

        def load(name, pairs, *after, q=sp):
            return Load(q, sem("d_" + name), [
                (lambda e, d=d, s=s: e.dma_start(d, s)) for d, s in pairs], after,
                sum(d.shape[0] * size(d) * 4e-6 for d, s in pairs))

        def last():
            return [q.ops[-1] for q in (pe, dve, act, pool) if q.ops]

        def C(name, lo=0, hi=128):
            at, n = CST[name]
            return cst[lo:hi, at:at + n]

        def CL(name):
            at, n = COLS[name]
            return col[:, at:at + n]

        def RW(name, hi=S):
            at, n = ROWS[name]
            return row[0:hi, at:at + n]

        work = [0]

        def mm(o, l, r, start, stop_, *after):
            work[0] += 4 * size(o)
            return pe(lambda e: e.matmul(o, l, r, start=start, stop=stop_), *after)

        def tr(o, i, n, *after):
            work[0] += 2 * size(o)
            return pe(lambda e: e.transpose(o, i, C("ident", 0, n)[:, 0:n]), *after)

        free = [None] * 8

        def pick(banks):
            return min(banks, key=lambda n: when(free[n]))

        LOADS[0] = 0.0

        l_c = load("cst", [(cst[:, :], a["consts"]), (col[:, :], a["cols"]), (row[:, :], a["rows"])])
        l_x = [load(f"x{u}", [(x[0:S, u * UB:(u + 1) * UB, :], a["x"][:, u * UB:(u + 1) * UB, :])])
               for u in range(NU)]
        c_pad = pool(lambda e: e.memset(pad[:, :], 0.0))
        c_mh = pool(lambda e: e.memset(mhalf[:, :], -0.5))

        xn_free = [None, None]
        xT_ready = [None] * NBATCH
        read_x = [None] * NBATCH
        ncount = [0]

        def norm(b, deps, src=None, dst=None):
            src = x[0:S, b, :] if src is None else src
            k = ncount[0] % 2
            ncount[0] += 1
            dst_, w = (xn[0:S, k, :], xn_free[k]) if dst is None else (dst, None)
            o1 = dve(lambda e: e.bn_stats(st[0:S, b, :], src), deps)
            o2 = dve(lambda e: e.bn_aggr(mv[0:S, b, :], st[0:S, b, :]), o1)
            o3 = dve(lambda e: e.tensor_scalar(veps[0:S, b:b + 1], mv[0:S, b, 1:2], 1e-5, None, ALU.add), o2)
            o4 = pool(lambda e: e.tensor_tensor(rstd[0:S, b:b + 1], veps[0:S, b:b + 1], mhalf[0:S, 0:1],
                                                ALU.pow), o3, c_mh)
            o5 = dve(lambda e: e.tensor_scalar(dst_, src, mv[0:S, b, 0:1], rstd[0:S, b:b + 1],
                                               ALU.subtract, ALU.mult), o4, w)
            return o5, k, dst_

        def stats(b, deps):
            o1 = dve(lambda e: e.bn_stats(st[0:S, b, :], x[0:S, b, :]), deps)
            o2 = dve(lambda e: e.bn_aggr(mv[0:S, b, :], st[0:S, b, :]), o1)
            return dve(lambda e: e.tensor_scalar(veps[0:S, b:b + 1], mv[0:S, b, 1:2], 1e-5, None, ALU.add), o2)

        def scaled(b, deps):
            k = ncount[0] % 2
            ncount[0] += 1
            v = xn[0:S, k, :]
            o5 = dve(lambda e: e.tensor_scalar(v, x[0:S, b, :], mv[0:S, b, 0:1], rstd[0:S, b:b + 1],
                                               ALU.subtract, ALU.mult), deps, xn_free[k])
            return o5, k, v

        def put_t(b, v, deps, bank, k=None):
            for c in range(4):
                t = tr(PS[:, bank, c * S:(c + 1) * S], v[:, c * 128:(c + 1) * 128], S, deps, free[bank], l_c)
            if k is not None:
                xn_free[k] = t
            src_ = PS[:, bank, 0:4 * S].rearrange("p (c n) -> p c n", c=4)
            dst_ = xT[:, :, b * S:(b + 1) * S]
            o = act(lambda e: e.activation(dst_, src_, ACT.Copy), t, xT_free[b])
            free[bank] = o
            xT_ready[b] = o
            return o

        xT_free = [None] * NBATCH
        x_ready = [l_x[b // UB] for b in range(NBATCH)]

        def wload(name, slot, src, n, *after):
            return load(name, [(W[:, slot:slot + n, :], src)], *after)

        l_kv = wload("w0kv", 4, a["w0kv"], 2)
        l_q = [wload(f"w0q{n}", n, a["w0q"][:, n:n + 1, :], 1) for n in range(4)]
        l_o = wload("w0o", 6, a["w0o"], 4)
        Wq = W[:, 0:4, :].rearrange("p a (c k n) -> p (a c) k n", c=2, k=4)
        Wk = W[:, 4, :].rearrange("p (k n) -> p k n", k=4)
        Wv = W[:, 5, :].rearrange("p (k n) -> p k n", k=4)
        Wo = W[:, 6:10, :].rearrange("p a (t n) -> p (a t) n", n=D)

        at = [0]

        def carve(n):
            o = at[0]
            at[0] += n
            assert at[0] <= RSIZE, at[0]
            return R[:, o:o + n]

        Q = carve(2 * 16 * UT).rearrange("p (z c a n) -> p z c a n", z=2, c=8, a=2)
        K = carve(2 * 4 * UT).rearrange("p (z c a n) -> p z c a n", z=2, c=2, a=2)
        V = carve(2 * UB * 520).rearrange("p (z b h n) -> p z b h n", z=2, b=UB, h=8)
        T4 = carve(4 * UT).rearrange("p (k n) -> p k n", k=4)
        SS = carve(2 * 1792).rearrange("p (z n) -> p z n", z=2)
        PT = carve(3 * 448).rearrange("p (z n) -> p z n", z=3)
        O = carve(1024)
        OT = carve(8 * S).rearrange("p (t n) -> p t n", t=8)
        small = sb("small", [128, 2, 5, 32])
        rec4 = sb("rec4", [128, 16])
        any0 = [4, 5, 6, 7]
        ones_v = pool(lambda e: e.memset(V[0:S, :, :, :, 64:65], 1.0))

        def bc(t, n):
            return t.unsqueeze(1).to_broadcast([128, n, S])

        t4_free = [None]
        t4_buf = [T4]
        q_free = [None, None]

        def rope(bank, ba, bb, cos, sin, da, db, w_out, mmop):
            T4 = t4_buf[0]
            A = PS[:, bank, 0:UT].rearrange("p (b n) -> p b n", b=UB)
            B = PS[:, bank, UT:2 * UT].rearrange("p (b n) -> p b n", b=UB)

            def half(k, src, bias, tab, *w):
                o = T4[:, k, :].rearrange("p (b n) -> p b n", b=UB)
                return dve(lambda e: e.scalar_tensor_tensor(o, src, bias, bc(tab, UB), ALU.add, ALU.mult), *w)

            half(0, A, ba, cos, mmop, t4_free[0], l_c)
            o1 = half(1, B, bb, sin)
            half(2, B, bb, cos)
            o3 = half(3, A, ba, sin)
            free[bank] = o3
            p1 = pool(lambda e: e.tensor_tensor(da, T4[:, 0, :], T4[:, 1, :], ALU.subtract), o1, w_out)
            p2 = pool(lambda e: e.tensor_tensor(db, T4[:, 2, :], T4[:, 3, :], ALU.add), o3)
            t4_free[0] = p2
            return p2

        def project0(u, banks):
            tok = slice(u * UT, (u + 1) * UT)
            xr = [xT_ready[u * UB + i] for i in range(UB)]
            kr, vr, qr = [None] * 2, [None] * UB, [None] * 8
            n = 0
            for c in range(2):
                bank = pick(banks)
                for ab in range(2):
                    for k in range(4):
                        lo = (c * 2 + ab) * 128
                        o = mm(PS[:, bank, ab * UT:(ab + 1) * UT], Wk[:, k, lo:lo + 128], xT[:, k, tok],
                               k == 0, k == 3, xr, l_kv, free[bank])
                bk = CL("bk")
                kr[c] = rope(bank, bk[:, 2 * c:2 * c + 1], bk[:, 2 * c + 1:2 * c + 2], C("k0cos"), C("k0sin"),
                             K[:, u % 2, c, 0, :], K[:, u % 2, c, 1, :], q_free[u % 2], o)
                yield
            for i in range(UB):
                bank = pick(banks)
                b = u * UB + i
                for k in range(4):
                    o = mm(PS[0:S, bank, :], xT[:, k, b * S:(b + 1) * S], Wv[:, k, :], k == 0, k == 3,
                           xr, free[bank])
                vr[i] = dve(lambda e, bank=bank, i=i: e.tensor_tensor(
                    V[0:S, u % 2, i, :, 0:64], PS[0:S, bank, :].rearrange("p (h n) -> p h n", h=8),
                    RW("bv").rearrange("p (h n) -> p h n", h=8), ALU.add), o, q_free[u % 2])
                free[bank] = vr[i]
                yield
            for c in range(8):
                bank = pick(banks)
                for ab in range(2):
                    for k in range(4):
                        o = mm(PS[:, bank, ab * UT:(ab + 1) * UT], Wq[:, c, k, ab * 128:ab * 128 + 128],
                               xT[:, k, tok], k == 0, k == 3, xr, l_q[c // 2], free[bank])
                bq = CL("bq")
                qr[c] = rope(bank, bq[:, 2 * c:2 * c + 1], bq[:, 2 * c + 1:2 * c + 2], C("q0cos"), C("q0sin"),
                             Q[:, u % 2, c, 0, :], Q[:, u % 2, c, 1, :], q_free[u % 2], o)
                yield
            done0[u] = (kr, vr, qr)
            for i in range(UB):
                xT_free[u * UB + i] = o
            return

        done0 = [None] * NU
        ss_free = [None, None]
        pt_free = [None] * 3
        o_free, ot_free = [None], [None]
        pt_n = [0]

        def evac(k, dst, src, *w):
            if k % 2 == 0:
                return act(lambda e: e.activation(dst, src, ACT.Copy), *w)
            return dve(lambda e: e.tensor_copy(dst, src), *w)

        def attend0(u):
            kr, vr, qr = done0[u]
            todo = [(i, g) for i in range(UB) for g in range(2)]
            state = {}

            def scores(n):
                i, g = todo[n]
                tk = slice(i * S, (i + 1) * S)
                z = n % 2
                for j in range(4):
                    for ab in range(2):
                        for r in range(4):
                            ro = slice(32 * r, 32 * r + 32)
                            o = mm(PS[0:S, r, j * S:(j + 1) * S], Q[ro, u % 2, 4 * g + j, ab, tk],
                                   K[ro, u % 2, g, ab, tk], ab == 0, ab == 1, qr[4 * g + j], kr[g], free[r])
                    yield
                sm = small[0:S, z]
                pss = PS[0:S, 0:4, 0:448]
                o1 = dve(lambda e: e.tensor_reduce(sm[:, 0, 0:16], pss.rearrange("p r (j n) -> p r j n", j=4),
                                                   AX.X, ALU.max), o)
                sk = RW("sinks")[:, 16 * g:16 * g + 16]
                o2 = dve(lambda e: e.tensor_tensor(sm[:, 1, 0:16], sm[:, 0, 0:16], sk, ALU.max), o1)
                o3 = dve(lambda e: e.tensor_tensor(
                    SS[0:S, z, :].rearrange("p (r j n) -> p r j n", r=4, j=4),
                    pss.rearrange("p r (j n) -> p r j n", j=4),
                    sm[:, 1, 0:16].rearrange("p (r j) -> p r j", r=4).unsqueeze(3).to_broadcast([S, 4, 4, S]),
                    ALU.subtract), o2, ss_free[z])
                for r in range(4):
                    free[r] = o3
                o4 = dve(lambda e: e.tensor_tensor(sm[:, 2, 0:16], sk, sm[:, 1, 0:16], ALU.subtract), o2)
                o5 = act(lambda e: e.activation(SS[0:S, z, :], SS[0:S, z, :], ACT.Exp), o3)
                o6 = act(lambda e: e.activation(sm[:, 3, 0:16], sm[:, 2, 0:16], ACT.Exp), o4)
                state[n] = (o5, o6)

            def values(n):
                i, g = todo[n]
                b = u * UB + i
                z = n % 2
                o5, o6 = state[n]
                sm = small[0:S, z]
                def pv(q, oe, slot):
                    bank = pick(any0)
                    for h in range(4):
                        kvh = 4 * g + q
                        o = mm(PS[0:S, bank, h * 65:h * 65 + 65], PT[0:S, slot, h * S:(h + 1) * S],
                               V[0:S, u % 2, i, kvh, :], True, True, oe, vr[i], ones_v, free[bank])
                    pt_free[slot] = o
                    pv_ = PS[0:S, bank, 0:260].rearrange("p (h n) -> p h n", h=4)
                    rec = rec4[0:S, 4 * q:4 * q + 4]
                    d1 = dve(lambda e: e.tensor_tensor(rec, pv_[:, :, 64], sm[:, 3, 4 * q:4 * q + 4],
                                                       ALU.add), o, o6)
                    d2 = dve(lambda e: e.reciprocal(rec, rec), d1)
                    d3 = dve(lambda e: e.tensor_tensor(
                        O[0:S, q * 256:(q + 1) * 256].rearrange("p (h n) -> p h n", h=4), pv_[:, :, 0:64],
                        rec.unsqueeze(2).to_broadcast([S, 4, 64]), ALU.mult), d2, o_free[0])
                    free[bank] = d3
                    return o, d3

                def probs(q):
                    bank = pick(any0)
                    slot = pt_n[0] % 3
                    pt_n[0] += 1
                    for h in range(4):
                        at_ = (q * 4 + h) * S
                        t = tr(PS[0:S, bank, h * S:(h + 1) * S], SS[0:S, z, at_:at_ + S], S, o5, free[bank])
                    oe = evac(q, PT[0:S, slot, :], PS[0:S, bank, 0:448], t, pt_free[slot])
                    free[bank] = oe
                    return t, oe, slot

                def outs(half, d3):
                    bank = pick(any0)
                    for c in range(4):
                        cc = half * 4 + c
                        t = tr(PS[:, bank, c * S:(c + 1) * S], O[0:S, cc * 128:(cc + 1) * 128], S, d3, free[bank])
                    oe = evac(half, OT[:, half * 4:half * 4 + 4, :],
                              PS[:, bank, 0:448].rearrange("p (c n) -> p c n", c=4), t, ot_free[0])
                    free[bank] = oe
                    return t, oe

                _, e0, s0 = probs(0)
                _, e1, s1 = probs(1)
                yield [e0, pt_free[(pt_n[0]) % 3]]
                _, e2, s2 = probs(2)
                pv(0, e0, s0)
                yield [e1]
                ss_free[z], e3, s3 = probs(3)
                _, d3 = pv(1, e1, s1)
                yield e2
                pv(2, e2, s2)
                yield [e3, d3]
                lastpv, d4 = pv(3, e3, s3)
                _, oa = outs(0, d3)
                yield [d4]
                t, ob = outs(1, d4)
                o_free[0] = t
                yield [oa, ob]
                bank = pick(any0)
                for c in range(8):
                    o = mm(PS[0:S, bank, :], OT[:, c, :], Wo[:, g * 8 + c, :], c == 0, c == 7, oa, ob, l_o,
                           free[bank])
                ot_free[0] = o
                xa = dve(lambda e: e.tensor_tensor(x[0:S, b, :], x[0:S, b, :], PS[0:S, bank, :], ALU.add),
                         o, x_ready[b])
                free[bank] = xa
                x_ready[b] = xa
                return lastpv

            for n in range(5):
                if n < 4:
                    yield free[0:4]
                    yield from scores(n)
                if n >= 1:
                    yield state[n - 1]
                    lp = yield from values(n - 1)
            q_free[u % 2] = lp

        def weave(main, fill, share, lead=LEAD, anyb=(4, 5, 6, 7)):
            def step(g):
                w = next(g, False)
                cost = work[0]
                work[0] = 0
                return w, cost

            work[0] = 0
            md = fd = 0
            wm, c = step(main)
            wf, c = step(fill)
            while wm is not False:
                turn = False
                if wf is not False:
                    behind = md * share - fd
                    tm = max(when(wm), pe.time)
                    tf = max(when(wf), pe.time)
                    turn = behind > lead or (tm > tf + 0.1 and behind > -2 * lead)
                if turn:
                    wf, c = step(fill)
                    fd += c
                else:
                    wm, c = step(main)
                    md += c
            for _ in fill:
                pass
            work[0] = 0

        def chain(*gens):
            for g in gens:
                yield from g

        def prep(u, banks, extra=None):
            got = []
            for i in range(UB):
                b = u * UB + i
                o5, k, v = norm(b, [x_ready[b]])
                read_x[b] = o5
                if extra:
                    extra(b)
                got.append((b, v, o5, k))
            for b, v, o5, k in got:
                yield [o5]
                put_t(b, v, [o5], pick(banks), k)
            yield [xT_ready[b]]

        def add_bo(b):
            x_ready[b] = pool(lambda e, b=b: e.tensor_tensor(x[0:S, b, :], x[0:S, b, :], RW("bo"), ALU.add),
                              read_x[b], l_c)

        for _ in chain(prep(0, any0, add_bo), prep(1, any0, add_bo), project0(0, list(range(8)))):
            pass
        for u in range(NU):
            fill = []
            if u + 2 < NU:
                fill.append(prep(u + 2, any0, add_bo))
            if u + 1 < NU:
                fill.append(project0(u + 1, any0))
            elif stop >= 2:
                fill.append(prep(0, any0))
            weave(attend0(u), chain(*fill), SHARE0)

        if stop >= 2:
            fence = last()
            last_q0 = [done for done in xT_free]
            l_xw = [wload(f"wx{n}", n, a["wx"][:, n:n + 1, :], 1, last_q0) for n in range(4)]
            at[0] = 0
            X0 = W[:, 4:10, :].rearrange("p a n -> p (a n)")
            KcT = X0[:, 0:3000].rearrange("p (z c n) -> p z c n", z=2, c=4)
            Vc = X0[:, 3000:6072].rearrange("p (z t n) -> p z t n", z=2, t=3)
            CT = X0[:, 6072:9072].rearrange("p (z c n) -> p z c n", z=2, c=4)
            P = X0[:, 9072:12072].rearrange("p (z r n) -> p z r n", z=2, r=4)
            QX = carve(2 * 4 * UT).rearrange("p (z c n) -> p z c n", z=2, c=4)
            QM = carve(2 * 8 * S).rearrange("p (z h n) -> p z h n", z=2, h=8)
            KX = carve(2 * 4 * UT).rearrange("p (z c n) -> p z c n", z=2, c=4)
            VX = carve(2 * UB * 544).rearrange("p (z b h n) -> p z b h n", z=2, b=UB, h=32)
            MK = carve(NBATCH * S).rearrange("p (b n) -> p b n", b=NBATCH)
            SX = carve(2 * 896).rearrange("p (z n) -> p z n", z=2)
            PX = carve(8 * 448).rearrange("p (z n) -> p z n", z=8)
            OX = carve(D)
            OXT = carve(4 * S).rearrange("p (t n) -> p t n", t=4)
            RT = carve(12 * UT).rearrange("p (z k n) -> p z k n", z=4, k=3)
            anyx = [0, 1, 2, 3, 4, 5]
            rt_n = [0]
            tg = sb("tg", [128, 32])
            sx = sb("sx", [128, 2, 2, 8])
            nmx = sb("nmx", [128, 2, 4])
            sumc = sb("sumc", [128, 2, 8])
            fx = sb("fx", [128, 2, 8])
            t128 = sb("t128", [128, 128])
            Wx = [W[:, n, :].rearrange("p (k n) -> p k n", k=4) for n in range(4)]

            l_mk = load("mask", [(MK[0:S], a["mask"])], fence)
            o_tg = act(lambda e: e.activation(tg[:, :], RW("gate", 128), ACT.Tanh), fence)
            ones_x = pool(lambda e: e.memset(VX[0:S, :, :, :, 16:17], 1.0), fence)
            f_dve = dve(lambda e: e.tensor_copy(pad[0:1, 0:1], pad[0:1, 2:3]), fence, c_pad)
            l_ct = [None] * NBATCH
            ct_free = [None, None]
            kc_free = [None, None]
            qx_free = [None, None]
            rt_free = [None] * 4
            kc_done = [None] * NBATCH
            qx_done = [None] * NU

            def load_ct(b):
                l_ct[b] = load(f"ct{b}", [(CT[:, b % 2], a["ctxT"][b])], fence, ct_free[b % 2])

            load_ct(0)
            load_ct(1)

            def context(b):
                z = b % 2
                kd, vd = [], []
                for c in range(4):
                    bank = pick(anyx)
                    for k in range(4):
                        o = mm(PS[:, bank, 0:SC], Wx[1][:, k, c * 128:(c + 1) * 128], CT[:, z, k, :], k == 0,
                               k == 3, l_ct[b], l_xw[1], free[bank])
                    oe = evac(c, KcT[:, z, c, :], PS[:, bank, 0:SC], o, kc_free[z], f_dve, fence)
                    free[bank] = oe
                    kd.append(oe)
                    yield
                for t in range(3):
                    bank = pick(anyx)
                    for k in range(4):
                        o = mm(PS[0:KC, bank, :], CT[:, z, k, t * KC:(t + 1) * KC], Wx[2][:, k, :], k == 0, k == 3,
                               l_xw[2], free[bank])
                    oe = evac(t, Vc[0:KC, z, t, :], PS[0:KC, bank, :], o)
                    free[bank] = oe
                    vd.append(oe)
                    yield
                ct_free[z] = o
                if b + 2 < NBATCH:
                    load_ct(b + 2)
                kc_done[b] = kd + vd

            def projectx(u):
                z = u % 2
                tok = slice(u * UT, (u + 1) * UT)
                xr = [xT_ready[u * UB + i] for i in range(UB)]
                done = []

                def b3(t):
                    return t.rearrange("p (b n) -> p b n", b=UB)

                def first(c, which):
                    bank = pick(anyx)
                    r = rt_n[0] % 4
                    rt_n[0] += 1
                    for k in range(4):
                        o = mm(PS[:, bank, 0:UT], Wx[which][:, k, c * 128:(c + 1) * 128], xT[:, k, tok],
                               k == 0, k == 3, xr, l_xw[which], free[bank])
                    e1 = act(lambda e: e.activation(RT[:, r, 0, :], PS[:, bank, 0:UT], ACT.Copy), o, rt_free[r],
                             fence)
                    free[bank] = e1
                    return c, which, r, e1

                def second(c, which, r, e1):
                    cos, sin = (("qxcos", "qxsin"), ("kxcos", "kxsin"))[which]
                    t1 = pool(lambda e: e.tensor_tensor(
                        b3(RT[:, r, 1, :]), b3(RT[:, r, 0, :]), bc(C(cos), UB), ALU.mult), e1)
                    bank = pick(anyx)
                    o = mm(PS[:, bank, 0:UT], C("rot"), RT[:, r, 0, :], True, True, e1, free[bank])
                    t2 = dve(lambda e: e.tensor_tensor(
                        b3(RT[:, r, 2, :]), b3(PS[:, bank, 0:UT]), bc(C(sin), UB), ALU.mult), o, rt_free[r])
                    free[bank] = t2
                    dst = (QX, KX)[which]
                    t3 = pool(lambda e: e.tensor_tensor(dst[:, z, c, :], RT[:, r, 1, :], RT[:, r, 2, :],
                                                        ALU.add), t2, t1, qx_free[z])
                    rt_free[r] = t3
                    done.append(t3)

                behind = None
                for c in range(4):
                    for which in range(2):
                        now_ = first(c, which)
                        if behind:
                            second(*behind)
                        behind = now_
                        yield
                second(*behind)
                for i in range(UB):
                    b = u * UB + i
                    bank = pick(anyx)
                    for k in range(4):
                        o = mm(PS[0:S, bank, :], xT[:, k, b * S:(b + 1) * S], Wx[2][:, k, :], k == 0, k == 3,
                               xr, l_xw[2], free[bank])
                    oe = act(lambda e, i=i, bank=bank: e.activation(
                        VX[0:S, z, i, :, 0:16], PS[0:S, bank, :].rearrange("p (h n) -> p h n", h=32), ACT.Copy),
                        o, qx_free[z], fence)
                    free[bank] = oe
                    done.append(oe)
                    xT_free[b] = o
                    yield
                qx_done[u] = done

            sx_free = [None, None]
            p_free = [None, None]
            px_free = [None] * 8
            px_n = [0]
            ox_free, oxt_free = [None], [None]
            small_free = [None, None]
            tb = [0]
            qm_free, qm_done = [None, None], [None, None]

            def attendx(b):
                u, i = b // UB, b % UB
                z = u % 2
                tk = slice(i * S, (i + 1) * S)
                zc = b % 2
                tasks = [(c, kind) for c in range(4) for kind in range(3)]
                state = {}

                def masks(c):
                    if c < 4:
                        zz = c % 2
                        qm_done[zz] = pool(lambda e: e.tensor_tensor(
                            QM[:, zz, :, :], QX[:, z, c, tk].unsqueeze(1).to_broadcast([128, 8, S]),
                            C("heads").unsqueeze(2).to_broadcast([128, 8, S]), ALU.mult),
                            qx_done[u], qm_free[zz])

                def scores(n):
                    c, kind = tasks[n]
                    if kind == 0:
                        zz = c % 2
                        v3 = SX[0:S, zz, :].rearrange("p (h n) -> p h n", h=8)
                        sm = sx[0:S, zz]
                        o1 = []
                        for half in range(2):
                            bank = pick(anyx)
                            for h in range(4):
                                o = mm(PS[0:S, bank, h * S:(h + 1) * S], QM[:, zz, 4 * half + h, :],
                                       KX[:, z, c, tk], True, True, qm_done[zz], free[bank])
                            o1.append(dve(lambda e, half=half, bank=bank: e.tensor_tensor(
                                v3[:, 4 * half:4 * half + 4, :],
                                PS[0:S, bank, 0:448].rearrange("p (h n) -> p h n", h=4),
                                MK[0:S, b, :].unsqueeze(1).to_broadcast([S, 4, S]), ALU.add),
                                o, l_mk, sx_free[zz], fence))
                            free[bank] = o1[-1]
                            yield
                        o2 = dve(lambda e: e.tensor_reduce(sm[:, 0, :], v3, AX.X, ALU.max), o1)
                        o3 = dve(lambda e: e.tensor_scalar(sm[:, 1, :], sm[:, 0, :], FMIN, None, ALU.max), o2)
                        o4 = dve(lambda e: e.scalar_tensor_tensor(
                            v3, v3, FMIN, sm[:, 1, :].unsqueeze(2).to_broadcast([S, 8, S]),
                            ALU.max, ALU.subtract), o3)
                        o5 = act(lambda e: e.activation(SX[0:S, zz, :], SX[0:S, zz, :], ACT.Exp), o4)
                        state[n] = o5
                    else:
                        par = kind - 1
                        zz = (c * 2 + par) % 2
                        ops = []
                        for r in range(4):
                            bank = pick(anyx)
                            o = mm(PS[0:S, bank, 0:SC], QM[:, c % 2, 2 * r + par, :], KcT[:, zc, c, :],
                                   True, True, kc_done[b], free[bank])
                            o1 = dve(lambda e, r=r, bank=bank: e.tensor_reduce(
                                nmx[0:S, zz, r:r + 1], PS[0:S, bank, 0:SC], AX.X, ALU.max, negate=True), o,
                                p_free[zz])
                            o2 = act(lambda e, r=r, bank=bank: e.activation(
                                P[0:S, zz, r, :], PS[0:S, bank, 0:SC], ACT.Exp, bias=nmx[0:S, zz, r:r + 1],
                                accum_out=sumc[0:S, c % 2, 2 * r + par:2 * r + par + 1]),
                                o1, p_free[zz], small_free[c % 2], fence)
                            free[bank] = o2
                            ops.append(o2)
                            yield
                        if par == 1:
                            qm_free[c % 2] = o
                            masks(c + 2)
                        state[n] = ops

                def turned(n):
                    c, kind = tasks[n]
                    if kind == 0:
                        zz = c % 2
                        o5 = state[n]
                        got = []
                        for half in range(2):
                            bank = pick(anyx)
                            slot = px_n[0] % 8
                            px_n[0] += 1
                            for h in range(4):
                                e_ = half * 4 + h
                                t = tr(PS[0:S, bank, h * S:(h + 1) * S], SX[0:S, zz, e_ * S:(e_ + 1) * S], S,
                                       o5, free[bank])
                            oe = evac(half, PX[0:S, slot, :], PS[0:S, bank, 0:448], t, px_free[slot])
                            free[bank] = oe
                            got.append((oe, slot))
                        sx_free[zz] = t
                        return got
                    par = kind - 1
                    zz = (c * 2 + par) % 2
                    ops = state[n]
                    got = []
                    for t_ in range(3):
                        bank = pick(anyx)
                        slot = px_n[0] % 8
                        px_n[0] += 1
                        for r in range(4):
                            t = tr(PS[0:KC, bank, r * S:(r + 1) * S], P[0:S, zz, r, t_ * KC:(t_ + 1) * KC], S,
                                   ops[r], free[bank])
                        tb[0] += 1
                        oe = evac(tb[0], PX[0:KC, slot, :], PS[0:KC, bank, 0:448], t, px_free[slot])
                        free[bank] = oe
                        got.append((oe, slot))
                        yield
                    p_free[zz] = t
                    return got

                def values(n):
                    c, kind = tasks[n]
                    pvb = 6 + c % 2
                    got = turn[n]
                    if kind == 0:
                        for half in range(2):
                            oe, slot = got[half]
                            yield oe
                            for h in range(4):
                                ln = 4 * half + h
                                o = mm(PS[0:S, pvb, ln * 17:ln * 17 + 17], PX[0:S, slot, h * S:(h + 1) * S],
                                       VX[0:S, z, i, 8 * c + ln, :], True, True, oe, ones_x, free[pvb])
                            px_free[slot] = o
                        return
                    par = kind - 1
                    ops = state[n]
                    yield got[2][0]
                    for r in range(4):
                        ln = 2 * r + par
                        for t_ in range(3):
                            oe, slot = got[t_]
                            o = mm(PS[0:S, pvb, 256 + ln * 16:272 + ln * 16], PX[0:KC, slot, r * S:(r + 1) * S],
                                   Vc[0:KC, zc, t_, (8 * c + ln) * 16:(8 * c + ln) * 16 + 16], t_ == 0, t_ == 2,
                                   oe)
                    for _, slot in got:
                        px_free[slot] = o
                    if par == 0:
                        return
                    k = c % 2
                    sp_ = PS[0:S, pvb, 0:136].rearrange("p (h n) -> p h n", h=8)
                    cp_ = PS[0:S, pvb, 256:384].rearrange("p (h n) -> p h n", h=8)
                    d1 = dve(lambda e: e.reciprocal(fx[0:S, 0, :], sp_[:, :, 16]), o, fence)
                    d2 = dve(lambda e: e.reciprocal(fx[0:S, 1, :], sumc[0:S, k, :]), ops)
                    ov = OX[0:S, c * 128:(c + 1) * 128].rearrange("p (h n) -> p h n", h=8)
                    d3 = dve(lambda e: e.tensor_tensor(
                        ov, sp_[:, :, 0:16], fx[0:S, 0, :].unsqueeze(2).to_broadcast([S, 8, 16]), ALU.mult),
                        d1, ox_free[0])
                    d4 = dve(lambda e: e.tensor_tensor(fx[0:S, 1, :], fx[0:S, 1, :], tg[0:S, 8 * c:8 * c + 8],
                                                       ALU.mult), d2, o_tg)
                    d5 = dve(lambda e: e.tensor_tensor(
                        t128[0:S, :].rearrange("p (h n) -> p h n", h=8), cp_,
                        fx[0:S, 1, :].unsqueeze(2).to_broadcast([S, 8, 16]), ALU.mult), d4)
                    small_free[k] = d2
                    free[pvb] = d5
                    d6 = dve(lambda e: e.tensor_tensor(OX[0:S, c * 128:(c + 1) * 128],
                                                       OX[0:S, c * 128:(c + 1) * 128], t128[0:S, :], ALU.add),
                             d5, d3)
                    state["o"] = d6

                masks(0)
                masks(1)
                turn = {}
                for n in range(len(tasks) + 2):
                    if n < len(tasks):
                        if tasks[n][1] == 0:
                            yield qm_done[tasks[n][0] % 2]
                        yield from scores(n)
                    if 1 <= n <= len(tasks):
                        yield state[n - 1]
                        turn[n - 1] = yield from turned(n - 1)
                    if n >= 2:
                        yield from values(n - 2)
                yield state["o"]
                bank = pick(anyx)
                for c in range(4):
                    t = tr(PS[:, bank, c * S:(c + 1) * S], OX[0:S, c * 128:(c + 1) * 128], S, state["o"], free[bank])
                ox_free[0] = t
                oe = act(lambda e: e.activation(OXT[:, :, :], PS[:, bank, 0:448].rearrange("p (c n) -> p c n", c=4),
                                                ACT.Copy), t, oxt_free[0])
                free[bank] = oe
                yield oe
                bk2 = pick(anyx)
                for c in range(4):
                    o = mm(PS[0:S, bk2, :], OXT[:, c, :], Wx[3][:, c, :], c == 0, c == 3, oe, l_xw[3], free[bk2])
                oxt_free[0] = o
                xa = dve(lambda e: e.tensor_tensor(x[0:S, b, :], x[0:S, b, :], PS[0:S, bk2, :], ALU.add), o,
                         x_ready[b])
                free[bk2] = xa
                x_ready[b] = xa
                kc_free[zc] = px_free[(px_n[0] - 1) % 8]
                qx_free[z] = px_free[(px_n[0] - 1) % 8]

            weave(projectx(0), context(0), 1.5)
            moe_stats = []
            for b in range(NBATCH):
                fills = []
                if b + 1 < NBATCH:
                    fills.append(context(b + 1))
                if b % UB == 0 and b // UB + 1 < NU:
                    fills += [prep(b // UB + 1, anyx), projectx(b // UB + 1)]
                weave(attendx(b), chain(*fills), SHAREX if len(fills) > 1 else 0.5 * SHAREX)
                if b == NBATCH - 2:
                    l_e0 = wload("we0", 0, a["we"][0], 3, pe.ops[-1])
                moe_stats.append(stats(b, x_ready[b]))

        if stop >= 3:
            fence = last()
            at[0] = 0
            GA = carve(2 * 4 * 448).rearrange("p (z c n) -> p z c n", z=2, c=4)
            GS = carve(2 * 448).rearrange("p (z n) -> p z n", z=2)
            sq = carve(D)
            rt = sb("rt", [128, 12, 64])
            wr2 = sb("wr2", [128, 4, 8])
            ss8 = sb("ss8", [128, 8])
            f_act = act(lambda e: e.activation(sq[0:1, 0:1], cst[0:1, 0:1], ACT.Copy), fence)
            f_dve = dve(lambda e: e.tensor_copy(pad[0:1, 0:1], pad[0:1, 2:3]), fence, c_pad)
            l_we = [None] * 8

            def load_e(x_, *after):
                l_we[x_] = wload(f"we{x_}", 3 * (x_ % 2), a["we"][x_], 3, *after)

            l_we[0] = l_e0
            load_e(1, fence)
            o4 = pool(lambda e: e.tensor_tensor(rstd[0:S, 0:8], veps[0:S, 0:8], mhalf[0:S, 0:8], ALU.pow),
                      moe_stats, c_mh, fence)
            normed = {0: scaled(0, [o4, x_ready])}
            wr_o = [dve(lambda e, k=k: e.tensor_scalar(
                wr2[:, k, :], CL("wr")[:, 8 * k:8 * k + 8], CL("rscale")[:, k:k + 1], None, ALU.mult))
                for k in range(4)][-1]
            ssq = []
            for b in range(NBATCH):
                if b + 1 < NBATCH:
                    normed[b + 1] = scaled(b + 1, o4)
                o5, k, v = normed[b]
                read_x[b] = o5
                put_t(b, v, [o5], (b + 2) % 8, k)
                o = act(lambda e, b=b, k=k: e.activation(sq[0:S, :], xn[0:S, k, :], ACT.Square,
                                                         accum_out=ss8[0:S, b:b + 1]), read_x[b], f_act, ssq[-1:])
                xn_free[k] = [xn_free[k], o]
                ssq.append(o)
            for b in range(NBATCH):
                for k in range(4):
                    o = mm(PS[0:S, 6, b * 8:b * 8 + 8], xT[:, k, b * S:(b + 1) * S], wr2[:, k, :], k == 0, k == 3,
                           xT_ready[b], wr_o, free[6])

            def r8(n):
                return rt[0:S, n, :].rearrange("p (b n) -> p b n", b=8)

            def b8(ap):
                return ap.unsqueeze(2).to_broadcast([S, 8, 8])

            d = dve(lambda e: e.tensor_scalar(rt[0:S, 8, 0:8], ss8[0:S, :], 1.0 / D, 1e-6, ALU.mult, ALU.add), ssq)
            d = pool(lambda e: e.tensor_tensor(rt[0:S, 8, 8:16], rt[0:S, 8, 0:8], mhalf[0:S, 0:8], ALU.pow), d)
            d = dve(lambda e: e.tensor_scalar(rt[0:S, 8, 8:16], rt[0:S, 8, 8:16], float(np.float32(D) ** -0.5), None,
                                              ALU.mult), d)
            d = dve(lambda e: e.tensor_tensor(r8(0), PS[0:S, 6, 0:64].rearrange("p (b n) -> p b n", b=8),
                                              b8(rt[0:S, 8, 8:16]), ALU.mult), d, o, fence)
            free[6] = d
            dl = d
            o_rank = pool(lambda e: e.memset(r8(9)[:, :, 0:1], 8.0), fence)
            for n in range(1, 8):
                o_rank = pool(lambda e, n=n: e.memset(r8(9)[:, :, n:n + 1], 8.0 - n))
            cur = 0
            sel = []
            for step in range(2):
                m = rt[0:S, 8, 16 + 8 * step:24 + 8 * step]
                m2 = rt[0:S, 8, 32 + 8 * step:40 + 8 * step]
                d = dve(lambda e, m=m, cur=cur: e.tensor_reduce(m, r8(cur), AX.X, ALU.max), d)
                if step == 0:
                    dm = d
                d = dve(lambda e, m=m, cur=cur: e.tensor_tensor(r8(2), r8(cur), b8(m), ALU.is_equal), d)
                d = dve(lambda e: e.tensor_tensor(r8(2), r8(2), r8(9), ALU.mult), d, o_rank)
                d = dve(lambda e, m2=m2: e.tensor_reduce(m2, r8(2), AX.X, ALU.max), d)
                d = dve(lambda e, m2=m2, step=step: e.tensor_tensor(r8(3 + step), r8(2), b8(m2), ALU.is_equal), d)
                sel.append(d)
                if step == 0:
                    d = dve(lambda e: e.tensor_scalar(r8(1), r8(3), -3.0e38, None, ALU.mult), d)
                    d = dve(lambda e: e.tensor_tensor(r8(1), r8(1), r8(0), ALU.add), d)
                cur = 1
            d = dve(lambda e: e.tensor_tensor(r8(5), r8(3), r8(4), ALU.add), d)
            d = dve(lambda e: e.tensor_tensor(r8(6), r8(0), b8(rt[0:S, 8, 16:24]), ALU.subtract), d)
            d = act(lambda e: e.activation(rt[0:S, 6, :], rt[0:S, 6, :], ACT.Exp), d)
            d = dve(lambda e: e.tensor_reduce(rt[0:S, 8, 48:56], r8(6), AX.X, ALU.add), d)
            d = dve(lambda e: e.reciprocal(rt[0:S, 8, 48:56], rt[0:S, 8, 48:56]), d)
            d = dve(lambda e: e.tensor_tensor(r8(6), r8(6), b8(rt[0:S, 8, 48:56]), ALU.mult), d)
            d = dve(lambda e: e.tensor_tensor(r8(7), r8(6), r8(5), ALU.mult), d)
            d = dve(lambda e: e.tensor_reduce(rt[0:S, 8, 56:64], r8(7), AX.X, ALU.add), d)
            d = dve(lambda e: e.tensor_scalar(rt[0:S, 10, 0:8], rt[0:S, 8, 56:64], 0.0, None, ALU.is_le), d)
            d = dve(lambda e: e.tensor_tensor(rt[0:S, 8, 56:64], rt[0:S, 8, 56:64], rt[0:S, 10, 0:8], ALU.add), d)
            d = dve(lambda e: e.reciprocal(rt[0:S, 8, 56:64], rt[0:S, 8, 56:64]), d)
            d = dve(lambda e: e.tensor_tensor(r8(7), r8(7), b8(rt[0:S, 8, 56:64]), ALU.mult), d)
            cw = dve(lambda e: e.tensor_tensor(r8(11), r8(7), RW("pes").unsqueeze(1).to_broadcast([S, 8, 8]),
                                               ALU.mult), d)
            gs_free, ga_free = [None, None], [None, None]
            accd = list(x_ready)
            nb = [0]
            LQS, LOS = [6, 7, 8, 2], [0, 9, 3, 4]
            l_lq, l_lo = [None] * 4, [None] * 4

            def load_l(n, *after):
                l_lq[n] = wload(f"w1q{n}", LQS[n], a["w1q"][:, n:n + 1, :], 1, *after)

            def load_lo(n, *after):
                l_lo[n] = wload(f"w1o{n}", LOS[n], a["w1o"][:, n:n + 1, :], 1, *after)

            if stop >= 4:
                for n in range(3):
                    load_l(n, fence)
                load_lo(1, fence)

            def nbank():
                nb[0] += 1
                return nb[0] % 8

            for e_ in range(8):
                Wg = W[:, 3 * (e_ % 2):3 * (e_ % 2) + 2, :].rearrange("p a (k n) -> p (a k) n", k=2)
                Wl = W[:, 3 * (e_ % 2) + 2, :].rearrange("p (k n) -> p k n", k=4)
                for h in range(2):
                    z = (e_ * 2 + h) % 2
                    tok = slice(h * 448, (h + 1) * 448)
                    ga = []
                    for c in range(4):
                        bg, bu = nbank(), nbank()
                        for bank, off in ((bg, 0), (bu, 512)):
                            for k in range(4):
                                o = mm(PS[:, bank, 0:448], Wg[:, k, off + c * 128:off + c * 128 + 128], xT[:, k, tok],
                                       k == 0, k == 3, l_we[e_], xT_ready[4 * h:4 * h + 4], free[bank])
                            if off == 0:
                                og = o
                        zs = c % 2
                        o1 = act(lambda e, bg=bg, zs=zs: e.activation(GS[:, zs, :], PS[:, bg, 0:448],
                                                                      ACT.Gelu_apprx_tanh), og, gs_free[zs], f_act)
                        free[bg] = o1
                        o2 = dve(lambda e, bu=bu, zs=zs, z=z, c=c: e.tensor_tensor(
                            GA[:, z, c, :], GS[:, zs, :], PS[:, bu, 0:448], ALU.mult), o1, o, ga_free[z], f_dve)
                        free[bu] = o2
                        gs_free[zs] = o2
                        ga.append(o2)
                    if e_ == 7:
                        for n in range(4):
                            xT_free[4 * h + n] = o
                    for i in range(4):
                        b = h * 4 + i
                        bank = nbank()
                        for k in range(4):
                            o = mm(PS[0:S, bank, :], GA[:, z, k, i * S:(i + 1) * S], Wl[:, k, :], k == 0, k == 3,
                                   ga, free[bank])
                        sc = rt[0:S, 11, b * 8 + e_:b * 8 + e_ + 1]
                        oa = dve(lambda e, bank=bank, b=b, sc=sc: e.scalar_tensor_tensor(
                            x[0:S, b, :], PS[0:S, bank, :], sc, x[0:S, b, :], ALU.mult, ALU.add), o, cw, accd[b])
                        free[bank] = oa
                        accd[b] = oa
                    ga_free[z] = o
                    if e_ == 7:
                        for n in range(4):
                            x_ready[4 * h + n] = accd[4 * h + n]
                    if (e_, h) == (7, 0) and stop >= 4:
                        l_prep = prep(0, list(range(8)))
                        next(l_prep)
                if e_ + 2 < 8:
                    load_e(e_ + 2, o)
                if e_ == 6 and stop >= 4:
                    load_l(3, o)
                    l_ls = load("w1s", [(W[:, 1, 0:1664], a["w1s"])], o)
                    load_lo(0, o)

        if stop >= 4:
            fence = last()
            at[0] = 0
            LQ = carve(2 * 16 * UT).rearrange("p (z c a n) -> p z c a n", z=2, c=8, a=2)
            LK = carve(2 * 4 * UT).rearrange("p (z c a n) -> p z c a n", z=2, c=2, a=2)
            LV = carve(2 * UB * 512).rearrange("p (z b n) -> p z b n", z=2, b=UB)
            LT = carve(2 * UT).rearrange("p (k n) -> p k n", k=2)
            t4_buf[0] = carve(4 * UT).rearrange("p (k n) -> p k n", k=4)
            t4_free[0] = fence
            LS = carve(2 * 896).rearrange("p (z n) -> p z n", z=2)
            LP = carve(4 * 448).rearrange("p (z n) -> p z n", z=4)
            LO = carve(1024)
            LOT = carve(8 * S).rearrange("p (t n) -> p t n", t=8)
            ls = sb("ls", [128, 3, 3, 8])
            load_lo(2, fence)
            load_lo(3, fence)
            f_act = act(lambda e: e.activation(LT[0:1, 0, 0:1], cst[0:1, 0:1], ACT.Copy), fence)
            f_dve = dve(lambda e: e.tensor_copy(pad[0:1, 0:1], pad[0:1, 2:3]), fence, c_pad)
            f_pool = pool(lambda e: e.memset(pad[0:1, 1:2], 0.0), fence)
            Wlq = [W[:, n, :].rearrange("p (c k n) -> p c k n", c=2, k=4) for n in LQS]
            Wlo = [W[:, n, :].rearrange("p (t n) -> p t n", n=D) for n in LOS]
            kd_w = W[:, 1, 0:256].rearrange("p (k n) -> p k n", k=4)
            vd_w = W[:, 1, 256:640].rearrange("p (k n) -> p k n", k=4)
            ku_w = W[0:64, 1, 640:1152]
            vu_w = W[0:96, 1, 1152:1664]
            l_free = [None, None]
            anyl = [4, 5, 6, 7]
            l_done = [None] * NU
            lt_free = [None]

            def projectl(u):
                z = u % 2
                tok = slice(u * UT, (u + 1) * UT)
                xr = [xT_ready[u * UB + i] for i in range(UB)]
                kr, vr, qr = [None] * 2, [None] * UB, [None] * 8
                td = []
                for n, (w, m) in enumerate(((kd_w, 64), (vd_w, 96))):
                    bank = pick(anyl)
                    for k in range(4):
                        o = mm(PS[0:m, bank, 0:UT], w[:, k, :], xT[:, k, tok], k == 0, k == 3, xr, l_ls, free[bank])
                    o = act(lambda e, n=n, m=m, bank=bank: e.activation(LT[0:m, n, :], PS[0:m, bank, 0:UT],
                                                                        ACT.Copy), o, lt_free[0], f_act)
                    free[bank] = o
                    td.append(o)
                yield td
                for c in range(2):
                    bank = pick(anyl)
                    for ab in range(2):
                        lo = (c * 2 + ab) * 128
                        o = mm(PS[:, bank, ab * UT:(ab + 1) * UT], ku_w[:, lo:lo + 128], LT[0:64, 0, :], True, True,
                               td, free[bank])
                    bk = CL("kanch")
                    kr[c] = rope(bank, bk[:, 2 * c:2 * c + 1], bk[:, 2 * c + 1:2 * c + 2], C("l1cos"), C("l1sin"),
                                 LK[:, z, c, 0, :], LK[:, z, c, 1, :], [l_free[z], f_pool], o)
                    yield
                for i in range(UB):
                    bank = pick(anyl)
                    o = mm(PS[0:S, bank, :], LT[0:96, 1, i * S:(i + 1) * S], vu_w, True, True, td, free[bank])
                    vr[i] = dve(lambda e, i=i, bank=bank: e.tensor_tensor(LV[0:S, z, i, :], PS[0:S, bank, :],
                                                                          RW("vanch"), ALU.add),
                                o, l_free[z], f_dve)
                    free[bank] = vr[i]
                lt_free[0] = o
                yield
                for c in range(8):
                    bank = pick(anyl)
                    for ab in range(2):
                        for k in range(4):
                            o = mm(PS[:, bank, ab * UT:(ab + 1) * UT], Wlq[c // 2][:, c % 2, k, ab * 128:ab * 128 + 128],
                                   xT[:, k, tok], k == 0, k == 3, xr, l_lq[c // 2], free[bank])
                    qr[c] = rope(bank, 0.0, 0.0, C("l1cos"), C("l1sin"), LQ[:, z, c, 0, :], LQ[:, z, c, 1, :],
                                 [l_free[z], f_pool], o)
                    yield
                l_done[u] = (kr, vr, qr)
                for i in range(UB):
                    xT_free[u * UB + i] = o

            lss_free, lp_free = [None, None], [None] * 4
            sm_free = [None] * 3
            lo_free, lot_free = [None], [None]
            lp_n = [0]
            scale1 = float(np.float32(1.0) / np.sqrt(np.float32(128)))

            def attendl(u):
                z = u % 2
                kr, vr, qr = l_done[u]
                todo = [(i, g) for i in range(UB) for g in range(2)]
                state = {}

                def scores(n):
                    i, g = todo[n]
                    tk = slice(i * S, (i + 1) * S)
                    zz = n % 2
                    for j in range(4):
                        for ab in range(2):
                            for r in range(2):
                                ro = slice(64 * r, 64 * r + 64)
                                o = mm(PS[0:S, 2 * zz + r, j * S:(j + 1) * S], LQ[ro, z, 4 * g + j, ab, tk],
                                       LK[ro, z, g, ab, tk], ab == 0, ab == 1, qr[4 * g + j], kr[g],
                                       free[2 * zz + r])
                        yield
                    sm = ls[0:S, n % 3]
                    v3 = LS[0:S, zz, :].rearrange("p (h n) -> p h n", h=8)
                    o1 = dve(lambda e: e.tensor_tensor(
                        LS[0:S, zz, :].rearrange("p (r j n) -> p r j n", r=2, j=4),
                        PS[0:S, 2 * zz:2 * zz + 2, 0:448].rearrange("p r (j n) -> p r j n", j=4),
                        C("causal", 0, S).unsqueeze(1).unsqueeze(1).to_broadcast([S, 2, 4, S]), ALU.add),
                        o, lss_free[zz], f_dve)
                    for r in range(2):
                        free[2 * zz + r] = o1
                    o2 = dve(lambda e: e.tensor_reduce(sm[:, 0, :], v3, AX.X, ALU.max, negate=True), o1,
                             sm_free[n % 3])
                    o3 = dve(lambda e: e.tensor_scalar(sm[:, 1, :], sm[:, 0, :], scale1, None, ALU.mult), o2)
                    for h in range(8):
                        o4 = act(lambda e, h=h: e.activation(
                            v3[:, h, :], v3[:, h, :], ACT.Exp, bias=sm[:, 1, h:h + 1], scale=scale1,
                            accum_out=sm[:, 2, h:h + 1]), o3, f_act)
                    state[n] = o4

                def turned(n):
                    zz = n % 2
                    o4 = state[n]
                    sm = ls[0:S, n % 3]
                    rc = dve(lambda e: e.reciprocal(sm[:, 2, :], sm[:, 2, :]), o4)
                    got = []
                    for r in range(2):
                        bank = pick(anyl)
                        slot = lp_n[0] % 4
                        lp_n[0] += 1
                        for j in range(4):
                            h = 4 * r + j
                            t = tr(PS[0:S, bank, j * S:(j + 1) * S], LS[0:S, zz, h * S:(h + 1) * S], S, o4, free[bank])
                        oe = evac(r, LP[0:S, slot, :], PS[0:S, bank, 0:448], t, lp_free[slot])
                        free[bank] = oe
                        got.append((oe, slot))
                    lss_free[zz] = t
                    return got, rc

                def values(n):
                    i, g = todo[n]
                    b = u * UB + i
                    got, rc = turn[n]
                    sm = ls[0:S, n % 3]
                    dd = []
                    for r in range(2):
                        oe, slot = got[r]
                        yield oe
                        kv = 2 * g + r
                        bank = pick(anyl)
                        for j in range(4):
                            o = mm(PS[0:S, bank, j * 128:(j + 1) * 128], LP[0:S, slot, j * S:(j + 1) * S],
                                   LV[0:S, z, i, kv * 128:(kv + 1) * 128], True, True, oe, vr[i], free[bank])
                        lp_free[slot] = o
                        d3 = dve(lambda e, r=r, bank=bank: e.tensor_tensor(
                            LO[0:S, r * 512:(r + 1) * 512].rearrange("p (h n) -> p h n", h=4),
                            PS[0:S, bank, :].rearrange("p (h n) -> p h n", h=4),
                            sm[:, 2, 4 * r:4 * r + 4].unsqueeze(2).to_broadcast([S, 4, 128]), ALU.mult),
                            o, rc, lo_free[0])
                        free[bank] = d3
                        dd.append(d3)
                    sm_free[n % 3] = d3
                    lastpv = o
                    oes = []
                    for half in range(2):
                        yield dd[half]
                        bank = pick(anyl)
                        for c in range(4):
                            cc = half * 4 + c
                            t = tr(PS[:, bank, c * S:(c + 1) * S], LO[0:S, cc * 128:(cc + 1) * 128], S, dd[half],
                                   free[bank])
                        oe = evac(half, LOT[:, half * 4:half * 4 + 4, :],
                                  PS[:, bank, 0:448].rearrange("p (c n) -> p c n", c=4), t, lot_free[0])
                        free[bank] = oe
                        oes.append(oe)
                    lo_free[0] = t
                    yield oes
                    bo_ = pick(anyl)
                    for c in range(8):
                        o = mm(PS[0:S, bo_, :], LOT[:, c, :], Wlo[2 * g + c // 4][:, c % 4, :], c == 0, c == 7, oes, l_lo,
                               free[bo_])
                    lot_free[0] = o
                    xa = dve(lambda e: e.tensor_tensor(x[0:S, b, :], x[0:S, b, :], PS[0:S, bo_, :], ALU.add),
                             o, x_ready[b])
                    free[bo_] = xa
                    x_ready[b] = xa
                    return lastpv

                turn = {}
                for n in range(6):
                    if n < 4:
                        yield [free[2 * (n % 2)], free[2 * (n % 2) + 1]]
                        yield from scores(n)
                    if 1 <= n <= 4:
                        yield state[n - 1]
                        turn[n - 1] = turned(n - 1)
                    if n >= 2:
                        lp = yield from values(n - 2)
                l_free[z] = lp

            for _ in chain(l_prep, projectl(0)):
                pass
            l_ent = {}

            def load_ent(l, j, *after):
                l_ent[l, j] = load(f"ent{l}{j}", [(W[:, j, :], a["entwT"][l][:, j, :]),
                                                  (W[:, 4 + j, :], a["entpw"][l][:, j, :])], *after)

            for u in range(NU):
                fill = chain(prep(u + 1, anyl), projectl(u + 1)) if u + 1 < NU else iter(())
                weave(attendl(u), fill, SHAREL)
                if u == NU - 2 and stop >= 5:
                    load_ent(0, 1, pe.ops[-1])
                    load_ent(0, 2, pe.ops[-1])

        if stop >= 5:
            fence = last()
            at[0] = 0
            C5 = carve(2 * 1500).rearrange("p (z k n) -> p z k n", z=2, k=4)
            M5 = carve(2 * 1536).rearrange("p (z t n) -> p z t n", z=2, t=3)
            MF = carve(3000).rearrange("p (b n) -> p b n", b=8)
            NB = carve(2 * SC).rearrange("p (z n) -> p z n", z=2)
            T5 = carve(2 * D).rearrange("p (k n) -> p k n", k=2)
            S5 = carve(2 * SC).rearrange("p (z n) -> p z n", z=2)
            P5 = carve(2 * 3 * S).rearrange("p (z t n) -> p z t n", z=2, t=3)
            mu = carve(8 * SC // 4).bitcast(U8)
            keep = max(at[0], 13312)
            at[0] = keep
            BC = carve(2 * D).rearrange("p (k n) -> p k n", k=2)
            RA = carve(6 * D).rearrange("p (k n) -> p k n", k=6)
            s5 = sb("s5", [128, 8, 4])
            scale5 = float(np.float32(1.0) / np.sqrt(np.float32(512)))
            any5 = [5, 6, 7]
            c5_free = [None] * 2
            l_c5 = [None] * 8

            def load5(b):
                l_c5[b] = load(f"c5{b}", [(C5[:, b % 2], a["ctxT"][b]), (M5[0:KC, b % 2], a["ctx"][b])],
                               fence, c5_free[b % 2])

            l_mu = load("mu", [(mu[0:S, :], a["cmask"])], fence)
            load5(0)
            load_ent(0, 0, fence)
            load5(1)
            load_ent(0, 3, fence)
            l_ra = load("rows2a", [(RA, a["rows2"][:, 0:6, :])], fence)
            m1 = dve(lambda e: e.tensor_copy(MF[0:S, :, :], mu[0:S, :].rearrange("p (b n) -> p b n", b=8)),
                     l_mu, fence)
            m3 = dve(lambda e: e.tensor_reduce(s5[0:S, :, 3], MF[0:S, :, :], AX.X, ALU.max), m1)
            s5_free = [None, None]
            p5_free = [None, None]

            def cos_sin(v, s_, c_, scale, ops, w=None):
                hi = v.shape[0]
                o1 = act(lambda e: e.activation(s_, v, ACT.Sin, scale=scale / 2), ops, w, fence)
                o2 = act(lambda e: e.activation(c_, v, ACT.Abs), ops, w, fence)
                o3 = act(lambda e: e.activation(c_, c_, ACT.Sin, bias=C("halfpi", 0, hi), scale=-scale / 2), o2)
                o4 = dve(lambda e: e.tensor_tensor(c_, c_, s_, ALU.subtract), o3, o1)
                o5 = dve(lambda e: e.tensor_tensor(c_, c_, s_, ALU.mult), o4)
                return dve(lambda e: e.tensor_scalar(v, c_, 2.0, 1.0, ALU.mult, ALU.add), o5)

            mod = []

            def readout():
                pend = {}

                def modes():
                    for n in range(4):
                        ph = RA[:, 2 + n, :]
                        u = T5[:, 0, :]
                        d = dve(lambda e, ph=ph: e.tensor_scalar(u, ph, float(1 / (2 * np.pi)), 12582912.0, ALU.mult,
                                                                 ALU.add), l_ra, mod[-1:])
                        d = dve(lambda e: e.tensor_scalar(u, u, -12582912.0, None, ALU.add), d)
                        d = dve(lambda e, ph=ph: e.scalar_tensor_tensor(ph, u, -6.28125, ph, ALU.mult, ALU.add), d)
                        d = dve(lambda e, ph=ph: e.scalar_tensor_tensor(
                            ph, u, -float(2 * np.pi - 6.28125), ph, ALU.mult, ALU.add), d)
                        mod.append(cos_sin(ph, u, T5[:, 1, :], 1.0, d))


                def scores5(b):
                    z = b % 2
                    o5, k, v = norm(b, [x_ready[b]])
                    m2 = dve(lambda e: e.tensor_scalar(NB[0:S, z, :], MF[0:S, b, :], -1.0, 1e30, ALU.add, ALU.mult),
                             m1)
                    yield o5
                    put_t(b, v, [o5], pick(any5), k)
                    yield [xT_ready[b], l_c5[b]]
                    bank = pick(any5)
                    for k in range(4):
                        o = mm(PS[0:S, bank, 0:SC], xT[:, k, b * S:(b + 1) * S], C5[:, z, k, :], k == 0, k == 3,
                               xT_ready[b], l_c5[b], free[bank])
                    xT_free[b] = o
                    sv = S5[0:S, z, :]
                    o = dve(lambda e: e.tensor_tensor(sv, PS[0:S, bank, 0:SC], MF[0:S, b, :], ALU.mult), o, m2,
                            s5_free[z])
                    free[bank] = o
                    o = dve(lambda e: e.tensor_tensor(sv, sv, NB[0:S, z, :], ALU.add), o)
                    o = dve(lambda e: e.tensor_reduce(s5[0:S, b, 0:1], sv, AX.X, ALU.max, negate=True), o)
                    o = dve(lambda e: e.tensor_scalar(s5[0:S, b, 1:2], s5[0:S, b, 0:1], scale5, None, ALU.mult), o)
                    o = act(lambda e: e.activation(sv, sv, ACT.Exp, bias=s5[0:S, b, 1:2], scale=scale5,
                                                   accum_out=s5[0:S, b, 2:3]), o)
                    pend[b] = o

                def values5(b):
                    z = b % 2
                    o = pend[b]
                    q = dve(lambda e: e.reciprocal(s5[0:S, b, 2:3], s5[0:S, b, 2:3]), o)
                    q = dve(lambda e: e.tensor_tensor(s5[0:S, b, 2:3], s5[0:S, b, 2:3], s5[0:S, b, 3:4], ALU.mult),
                            q, m3)
                    yield o
                    bank = pick(any5)
                    for t_ in range(3):
                        t = tr(PS[0:KC, bank, t_ * S:(t_ + 1) * S], S5[0:S, z, t_ * KC:(t_ + 1) * KC], S, o,
                               free[bank])
                    s5_free[z] = t
                    oe = act(lambda e: e.activation(P5[0:KC, z, :, :].rearrange("p t n -> p (t n)"),
                                                    PS[0:KC, bank, 0:3 * S], ACT.Copy), t, p5_free[z], fence)
                    free[bank] = oe
                    yield oe
                    bv = pick(any5)
                    for t_ in range(3):
                        o = mm(PS[0:S, bv, :], P5[0:KC, z, t_, :], M5[0:KC, z, t_, :], t_ == 0, t_ == 2, oe,
                               free[bv])
                    p5_free[z] = o
                    c5_free[z] = o
                    xa = dve(lambda e: e.scalar_tensor_tensor(x[0:S, b, :], PS[0:S, bv, :], s5[0:S, b, 2:3],
                                                              x[0:S, b, :], ALU.mult, ALU.add), o, q, x_ready[b])
                    free[bv] = xa
                    x_ready[b] = xa
                    if b + 2 < NBATCH:
                        load5(b + 2)

                for b in range(NBATCH + 1):
                    if b < NBATCH:
                        yield from scores5(b)
                    if b >= 1:
                        yield from values5(b - 1)
                    if b == 6:
                        modes()

            wc_done = [None, None]

            def products():
                for l in range(2):
                    for k in range(16):
                        j, kk = (1, 2, 0, 3)[k // 4], k % 4
                        wT = W[:, j, kk * D:(kk + 1) * D]
                        pw = W[:, 4 + j, kk * D:(kk + 1) * D]
                        if kk == 0:
                            yield l_ent[l, j]
                        for m in range(4):
                            o = mm(PS[:, m, :], wT[:, m * 128:(m + 1) * 128], pw, k == 0, k == 15, l_ent[l, j],
                                   free[m], fence)
                            if m % 2:
                                yield
                        eb = CL("entb")[:, 16 * l + 4 * j + kk:16 * l + 4 * j + kk + 1].to_broadcast([128, S])
                        o = mm(PS[0:S, 4, :], eb, pw, k == 0, k == 15, free[4])
                        if kk == 3 and l == 0:
                            load_ent(1, j, o)
                        elif kk == 3:
                            load_rest(j, o)
                        yield
                    got = []
                    for m in range(4):
                        oe = evac(m, W[:, 8 + l, m * 512:(m + 1) * 512], PS[:, m, :], o, fence)
                        free[m] = oe
                        got.append(oe)
                    oe = act(lambda e, l=l: e.activation(BC[0:S, l, :], PS[0:S, 4, :], ACT.Copy), o)
                    free[4] = oe
                    got.append(oe)
                    wc_done[l] = got
                    yield

            l_rest = {}

            def load_rest(j, *after):
                if j == 0:
                    l_rest[0] = load("ampph", [(W[:, 0, :], a["ampph"][:, 0, :]), (W[:, 4, :], a["ampph"][:, 1, :])], *after)
                elif j < 3:
                    l_rest[j] = load(f"path{j}", [(W[:, j, :], a["pathw"][j - 1][:, 0, :]),
                                                  (W[:, 4 + j, :], a["pathw"][j - 1][:, 1, :])], *after)

            if stop == 5:
                for _ in readout():
                    pass
            else:
                weave(readout(), products(), SHARE5)

        if stop >= 6:
            fence = last()
            at[0] = 0
            RB = carve(14 * D).rearrange("p (k n) -> p k n", k=14)
            H = carve(NBATCH * D).rearrange("p (b n) -> p b n", b=NBATCH)
            TS = carve(4 * D).rearrange("p (k n) -> p k n", k=4)
            assert at[0] <= keep
            f_act = act(lambda e: e.activation(TS[0:1, 0, 0:1], cst[0:1, 0:1], ACT.Copy), fence)
            f_dve = dve(lambda e: e.tensor_copy(pad[0:1, 0:1], pad[0:1, 2:3]), fence, c_pad)
            f_pool = pool(lambda e: e.memset(pad[0:1, 1:2], 0.0), fence)
            l_rb = load("rows2b", [(RB, a["rows2"][:, 6:20, :])], fence)
            l_ap, l_pw = l_rest[0], [l_rest[1], l_rest[2]]

            def rb(name, hi=S):
                n = ROW2.index(name)
                return RA[0:hi, n, :] if n < 6 else RB[0:hi, n - 6, :]

            def amp(b):
                return W[0:S, 3 + 4 * (b // 4), (b % 4) * D:(b % 4 + 1) * D]

            def entering(b):
                put_t(b, normed[b][2], [normed[b][0]], 4 + b % 2, normed[b][1])

            hr = [None] * NBATCH
            pre = [None] * NBATCH
            y_free = [None] * 4
            Wa = W[:, 0, :].rearrange("p (k n) -> p k n", k=4)
            Wp_ = W[:, 4, :].rearrange("p (k n) -> p k n", k=4)
            normed = {0: norm(0, [x_ready[0]]), 1: norm(1, [x_ready[1]])}

            def amp_phase(b):
                if b + 1 < NBATCH:
                    entering(b + 1)
                if b + 2 < NBATCH:
                    normed[b + 2] = norm(b + 2, [x_ready[b + 2]])
                got = []
                for bank, w in ((2 * (b % 2), Wa), (2 * (b % 2) + 1, Wp_)):
                    for k in range(4):
                        o = mm(PS[0:S, bank, :], xT[:, k, b * S:(b + 1) * S], w[:, k, :], k == 0, k == 3,
                               xT_ready[b], l_ap, free[bank])
                    got.append((o, bank))
                xT_free[b] = o
                (oa, ba), (op, bp) = got
                d1 = dve(lambda e: e.tensor_tensor(amp(b), PS[0:S, ba, :], rb("ampb"), ALU.add),
                         oa, l_ra, fence)
                free[ba] = d1
                d2 = dve(lambda e: e.tensor_tensor(H[0:S, b, :], PS[0:S, bp, :], rb("phb"), ALU.add), op)
                free[bp] = d2
                pre[b] = (d1, d2)

            def bounded(b):
                a1 = act(lambda e: e.activation(amp(b), amp(b), ACT.Sigmoid), pre[b][0])
                a2 = act(lambda e: e.activation(H[0:S, b, :], H[0:S, b, :], ACT.Tanh), pre[b][1])
                hr[b] = [a1, a2]

            cs_free = [None, None]

            def wave(b):
                z = b % 2
                if b == 4:
                    y_free[:] = [list(cs_free)] * 4
                    cs_free[:] = [xT_free[7], xT_free[7]]
                room = TS if b < 4 else W[:, 0, :].rearrange("p (k n) -> p k n", k=4)
                a3 = cos_sin(H[0:S, b, :], room[0:S, 2 * z, :], room[0:S, 2 * z + 1, :], float(np.pi), hr[b],
                             cs_free[z])
                cs_free[z] = a3
                hr[b] = pool(lambda e: e.tensor_tensor(H[0:S, b, :], H[0:S, b, :], amp(b), ALU.mult),
                             a3, hr[b])

            wp_done = []

            def paths(l):
                p0 = W[:, 1 + l, :].rearrange("p (k n) -> p k n", k=4)
                p1 = W[:, 5 + l, :].rearrange("p (k n) -> p k n", k=4)
                m0 = rb(f"ph{l}0", 128).unsqueeze(1).to_broadcast([128, 4, D])
                m1_ = rb(f"ph{l}1", 128).unsqueeze(1).to_broadcast([128, 4, D])
                d0 = dve(lambda e: e.tensor_tensor(p0, p0, m0, ALU.mult), mod, l_pw[l])
                q0 = dve(lambda e: e.tensor_tensor(p1, p1, m1_, ALU.mult), mod, l_pw[l])
                wp = dve(lambda e: e.tensor_tensor(p0, p0, p1, ALU.add), d0, q0)
                d0 = pool(lambda e: e.tensor_tensor(rb(f"pb{l}0"), rb(f"pb{l}0"), rb(f"ph{l}0"), ALU.mult), mod, l_rb)
                d1 = pool(lambda e: e.tensor_tensor(rb(f"pb{l}1"), rb(f"pb{l}1"), rb(f"ph{l}1"), ALU.mult), mod)
                d2 = pool(lambda e: e.tensor_tensor(rb(f"pb{l}0"), rb(f"pb{l}0"), rb(f"pb{l}1"), ALU.add), d0, d1)
                wp_done.append([wp, d2])

            entering(0)
            for b in range(4):
                amp_phase(b)
                bounded(b)
            for b in range(4, NBATCH):
                amp_phase(b)
                wave(b - 4)
            for b in range(4, NBATCH):
                bounded(b)
            for l in range(2):
                bcomb = pool(lambda e, l=l: e.tensor_tensor(rb(f"entpb{l}"), BC[0:S, l, :], rb(f"entpb{l}"), ALU.add),
                             wc_done[l], l_rb)
            paths(0)

            t = [0]

            def product(l, part, b):
                w = (W[:, 8 + l, :] if part == 0 else W[:, 1 + l, :]).rearrange("p (k n) -> p k n", k=4)
                wd = [wc_done[l], bcomb] if part == 0 else wp_done[l]
                bias = f"entpb{l}" if part == 0 else f"pb{l}0"
                hb = H[0:S, b, :]
                z = t[0] % 4
                t[0] += 1
                y = TS[0:S, z, :]
                r1 = pool(lambda e: e.tensor_tensor(y, hb, rb(bias), ALU.add), hr[b], y_free[z], wd)
                bank = b % 4
                for k in range(4):
                    o = mm(PS[0:S, bank, :], xT[:, k, b * S:(b + 1) * S], w[:, k, :], k == 0, k == 3,
                           xT_ready[b], wd, free[bank])
                xT_free[b] = o
                r2 = dve(lambda e: e.tensor_tensor(y, PS[0:S, bank, :], y, ALU.add), o, r1)
                free[bank] = r2
                o1 = dve(lambda e: e.bn_stats(st[0:S, b, :], y), r2)
                o2 = dve(lambda e: e.bn_aggr(mv[0:S, b, :], st[0:S, b, :]), o1)
                o3 = dve(lambda e: e.tensor_scalar(veps[0:S, b:b + 1], mv[0:S, b, 1:2], 1e-5, None, ALU.add), o2)
                o4 = pool(lambda e: e.tensor_tensor(rstd[0:S, b:b + 1], veps[0:S, b:b + 1], mhalf[0:S, 0:1],
                                                    ALU.pow), o3, c_mh)
                return l, part, b, z, o4

            def finish(l, part, b, z, o4):
                hb = H[0:S, b, :]
                y = TS[0:S, z, :]
                gn, bn = (f"g3{l}", f"b3{l}") if part == 0 else (f"g4{l}", f"b4{l}")
                o5 = dve(lambda e: e.tensor_scalar(y, y, mv[0:S, b, 0:1], rstd[0:S, b:b + 1], ALU.subtract,
                                                   ALU.mult), o4)
                r3 = dve(lambda e: e.tensor_tensor(y, y, rb(gn), ALU.mult), o5, l_rb)
                r4 = pool(lambda e: e.tensor_tensor(hb, y, rb(bn), ALU.add), r3, xT_ready[b])
                y_free[z] = r4
                hr[b] = r4
                if (l, part) == (1, 1):
                    x_ready[b] = dve(lambda e: e.tensor_tensor(x[0:S, b, :], x[0:S, b, :], hb, ALU.add),
                                     r4, x_ready[b])

            steps = [(l, part, b) for l in range(2) for part in range(2) for b in range(NBATCH)]

            def turn_h(n):
                b = steps[n][2]
                put_t(b, H[0:S, b, :], [hr[b]], 4 + b % 2)

            turn_h(0)
            pend = None
            for n, step_ in enumerate(steps):
                if n < 4:
                    wave(n + 4)
                if n == 12:
                    paths(1)
                if n + 1 < len(steps):
                    turn_h(n + 1)
                now_ = product(*step_)
                if pend:
                    finish(*pend)
                pend = now_
            finish(*pend)

        stores = [load(f"out{u}", [(out[:, u * UB:(u + 1) * UB, :], x[0:S, u * UB:(u + 1) * UB, :])],
                       x_ready[u * UB:(u + 1) * UB]) for u in range(NU)]

        count(queues)
        block = ctx.enter_context(nc.Block())

        @block.sync
        def _(e):
            play(e, sp)
            for s_ in stores:
                e.wait_ge(s_.sem, s_.value)

        @block.tensor
        def _(e):
            play(e, pe)

        @block.vector
        def _(e):
            play(e, dve)

        @block.scalar
        def _(e):
            play(e, act)

        @block.gpsimd
        def _(e):
            play(e, pool)


def kmaj(w):
    k, n = w.shape
    return w.reshape(k // 128, 128, n).transpose(1, 0, 2)


def slots(w):
    return np.ascontiguousarray(w.reshape(128, -1, 2048))


def layout(i):
    o = {"consts": CONSTS}
    o["x"] = i["x"].transpose(1, 0, 2)
    q = kmaj(i["L0_attn_Wq"].reshape(512, 2048)).reshape(128, 4, 2, 4, 4, 32, 2)
    q = q.transpose(0, 2, 4, 1, 6, 3, 5)
    o["w0q"] = slots(q)
    k = kmaj(i["L0_attn_Wk"].reshape(512, 512)).reshape(128, 4, 2, 4, 32, 2).transpose(0, 1, 2, 5, 3, 4)
    v = kmaj(i["L0_attn_Wv"].reshape(512, 512))
    o["w0kv"] = np.ascontiguousarray(np.stack([k.reshape(128, 2048), v.reshape(128, 2048)], 1))
    o["w0o"] = slots(kmaj(i["L0_attn_Wo"].reshape(2048, 512)))
    o["wx"] = np.stack([kmaj(i["L0_xattn_" + w]).reshape(128, 2048) for w in ("Wq", "Wk", "Wv", "Wo")], 1)
    o["mask"] = i["mask_Bx1xSxS_fk0"][:, 0].transpose(1, 0, 2)
    o["ctxT"] = i["ctx_2048"].transpose(0, 2, 1).reshape(8, 4, 128, SC).transpose(0, 2, 1, 3)
    g = i["L0_ffn_gating_einsum"].transpose(0, 3, 1, 2).reshape(8, 4, 128, 1024).transpose(0, 2, 1, 3)
    ln = i["L0_ffn_linear"].reshape(8, 4, 128, 512).transpose(0, 2, 1, 3)
    o["we"] = np.concatenate([g.reshape(8, 128, 4096), ln.reshape(8, 128, 2048)], 2).reshape(8, 128, 3, 2048)
    q = kmaj(i["L1_attn_Wq"].T).reshape(128, 4, 2, 2, 4, 2, 64).transpose(0, 2, 4, 1, 5, 3, 6)
    o["w1q"] = slots(q)
    o["w1o"] = slots(kmaj(i["L1_attn_Wo"].T))
    ku = i["L1_attn_Wk_up"].reshape(2, 2, 2, 64, 64).transpose(4, 0, 2, 1, 3).reshape(64, 512)
    small = np.zeros((128, 1664), np.float32)
    small[:, 0:256] = kmaj(i["L1_attn_Wk_down"].T).reshape(128, 256)
    small[:, 256:640] = kmaj(i["L1_attn_Wv_down"].T).reshape(128, 384)
    small[0:64, 640:1152] = ku
    small[0:96, 1152:1664] = i["L1_attn_Wv_up"].T
    o["w1s"] = small
    o["ctx"] = i["ctx_2048"].reshape(8, 3, KC, D).transpose(0, 2, 1, 3)
    o["cmask"] = np.broadcast_to(i["mask_BxS2_bk0"].reshape(1, 8 * SC), (S, 8 * SC))
    o["entwT"] = np.stack([kmaj(w.T).reshape(128, 4, 2048) for w in i["L1_ffn_ent_w"]])
    o["entpw"] = np.stack([kmaj(w).reshape(128, 4, 2048) for w in i["L1_ffn_ent_pw"]])
    o["ampph"] = np.stack([kmaj(i[n]).reshape(128, 2048) for n in ("L1_ffn_amp_w", "L1_ffn_ph_w")], 1)
    o["pathw"] = np.stack([np.stack([kmaj(w).reshape(128, 2048) for w in wl], 1) for wl in i["L1_ffn_path_w"]])
    r2 = [i["L1_ffn_amp_b"], i["L1_ffn_ph_b"], *i["L1_ffn_phase"].reshape(4, 512), *i["L1_ffn_ent_pb"],
          *i["L1_ffn_path_b"].reshape(4, 512)]
    for n in "34":
        for l in range(2):
            r2 += [i[f"L1_ffn_ln{n}_g"][l], i[f"L1_ffn_ln{n}_b"][l]]
    o["rows2"] = np.broadcast_to(np.stack(r2), (128, 20, D))
    cols = [
        i["L0_attn_bq"].reshape(2, 4, 4, 32, 2).transpose(1, 3, 0, 2, 4).reshape(128, 16),
        i["L0_attn_bk"].reshape(2, 4, 32, 2).transpose(1, 2, 0, 3).reshape(128, 4),
        i["L0_ffn_router_scale"].reshape(4, 128).T,
        i["L1_attn_k_anchor"].reshape(2, 2, 2, 64).transpose(1, 3, 0, 2).reshape(128, 4),
        kmaj(i["L0_ffn_router_logits"]).reshape(128, 32),
        i["L1_ffn_ent_b"].reshape(2, 16, 128).transpose(2, 0, 1).reshape(128, 32)]
    o["cols"] = np.concatenate(cols, 1)
    rows = [i["L0_attn_bv"].ravel(), i["L0_attn_bo"], i["L0_attn_sinks"], i["L0_xattn_gate"].ravel(),
            i["L0_ffn_per_expert_scale"], i["L1_attn_v_anchor"]]
    o["rows"] = np.broadcast_to(np.concatenate(rows), (128, NROW))
    return {k: np.ascontiguousarray(v) for k, v in o.items()}


def kernel(**inputs):
    import concourse.bacc as bacc
    from concourse.bass_utils import run_bass_kernel_spmd as run

    arrays = layout({k: np.asarray(v) for k, v in inputs.items()})
    nc = bacc.Bacc("TRN2", target_bir_lowering=False, num_devices=1)
    aps = {k: nc.dram_tensor("in_" + k, v.shape, mybir.dt.from_np(v.dtype), kind="ExternalInput").ap()
           for k, v in arrays.items()}
    out = nc.dram_tensor("out", (S, NBATCH, D), F32, kind="ExternalOutput").ap()
    program(nc, aps, out)
    r = run(nc, [{"in_" + k: v for k, v in arrays.items()}], core_ids=[0])
    return np.ascontiguousarray(r.results[0]["out"].transpose(1, 0, 2))
```
